# Optimizing a Trainium2 kernel written in Bass

```python
import numpy as np
import jax
import jax.numpy as jnp

def _softmax(x, axis=-1):
    return jax.nn.softmax(x, axis=axis)

def _gelu(x):
    return jax.nn.gelu(x, approximate=True)

def _silu(x):
    return jax.nn.silu(x)

def _sigmoid(x):
    return jax.nn.sigmoid(x)

def _layernorm(x, axis=-1, eps=1e-05):
    m = jnp.mean(x, axis=axis, keepdims=True)
    v = jnp.var(x, axis=axis, keepdims=True)
    return (x - m) / jnp.sqrt(v + eps)

def _scatter_add(tgt, idx, src, axis=0):
    return tgt.at[idx].add(src)

def _segment_sum(src, seg, n):
    return jax.ops.segment_sum(src, seg, n)
kernel_name = 'mk_lm_tower_d1_tok_ids1024_r4_b9852e'

def setup_inputs(seed: int=0):
    np.random.seed(seed)
    _w = jnp.asarray

    def _rec_inputs():
        import jax
        import jax.numpy as jnp
        _rk = jax.random.key(seed)
        x = jax.random.randint(jax.random.fold_in(_rk, 1), (64, 128), 0, 31993, jnp.int32)
        return x
    x = _rec_inputs()

    def _L0_tok_setup():
        import jax, jax.numpy as jnp
        import numpy as np
        V, D, CTX, NL = (8000, 256, 512, 2)
        B, T = (4, 512)
        EPS = 1e-05

        def _layer_norm(x, gamma, beta):
            mu = jnp.mean(x, axis=-1, keepdims=True)
            var = jnp.var(x, axis=-1, keepdims=True)
            return gamma * (x - mu) / jnp.sqrt(var + EPS) + beta
        key = jax.random.key(seed)
        ks = jax.random.split(key, 12)
        s = 0.02
        return {'x': jax.random.randint(ks[0], (B, T), 0, V), 'emb': jax.random.normal(ks[1], (V, D), jnp.float32) * s, 'pos': jax.random.normal(ks[2], (CTX, D), jnp.float32) * s, 'wq': jax.random.normal(ks[3], (NL, D, D), jnp.float32) * s, 'wk': jax.random.normal(ks[4], (NL, D, D), jnp.float32) * s, 'wv': jax.random.normal(ks[5], (NL, D, D), jnp.float32) * s, 'wo': jax.random.normal(ks[6], (NL, D, D), jnp.float32) * s, 'wup': jax.random.normal(ks[7], (NL, D, 4 * D), jnp.float32) * s, 'bup': jnp.zeros((NL, 4 * D), jnp.float32), 'wdown': jax.random.normal(ks[8], (NL, 4 * D, D), jnp.float32) * s, 'bdown': jnp.zeros((NL, D), jnp.float32), 'ga': jnp.ones((NL, D), jnp.float32), 'ba': jnp.zeros((NL, D), jnp.float32), 'gm': jnp.ones((NL, D), jnp.float32), 'bm': jnp.zeros((NL, D), jnp.float32)}
    _L0_tok_all = _L0_tok_setup()
    _L0_tok_in = {k: v for k, v in _L0_tok_all.items() if k in ('emb', 'pos', 'wq', 'wk', 'wv', 'wo', 'wup', 'bup', 'wdown', 'bdown', 'ga', 'ba', 'gm', 'bm')}
    del _L0_tok_all

    def _L0_attn_setup():
        import jax, jax.numpy as jnp
        import numpy as np
        H = 4
        DK = 64
        DV = 64
        M = 64
        GATE_NORM = 16.0
        EPS = 1e-05

        def _rmsnorm(x, w):
            var = jnp.mean(jnp.square(x), axis=-1, keepdims=True)
            return x * jax.lax.rsqrt(var + EPS) * w

        def _swish(x):
            return x * jax.nn.sigmoid(x)

        def _gsa_scan(q, k, v, s, g):
            B, Hh = (q.shape[1], q.shape[2])
            Hk0 = jnp.zeros((B, Hh, DK, M), q.dtype)
            Hv0 = jnp.zeros((B, Hh, M, DV), q.dtype)

            def step(carry, xs):
                Hk, Hv = carry
                qt, kt, vt, st, gt = xs
                lam = jnp.exp(gt)
                Hk = Hk * lam[:, :, None, :] + kt[..., :, None] * st[..., None, :]
                z = jnp.einsum('bhk,bhkm->bhm', qt, Hk)
                p = jax.nn.softmax(z, axis=-1)
                Hv = Hv * lam[..., :, None] + st[..., :, None] * vt[..., None, :]
                ot = jnp.einsum('bhm,bhmv->bhv', p, Hv)
                return ((Hk, Hv), ot)
            _, o = jax.lax.scan(step, (Hk0, Hv0), (q, k, v, s, g))
            return o
        key = jax.random.key(seed)
        ks = jax.random.split(key, 8)
        B, T, D = (4, 512, 256)
        scale = 2 ** (-2.5) * (2.0 / (D + D)) ** 0.5 * 3.0 ** 0.5 * 2
        return {'hidden_states': jax.random.normal(ks[0], (B, T, D), jnp.float32), 'norm_weight': jnp.ones((D,), jnp.float32), 'w_q': jax.random.normal(ks[1], (D, D), jnp.float32) * scale, 'w_k': jax.random.normal(ks[2], (D, D), jnp.float32) * scale, 'w_v': jax.random.normal(ks[3], (D, D), jnp.float32) * scale, 'w_f': jax.random.normal(ks[4], (H * M, D), jnp.float32) * scale, 'gnorm_weight': jnp.ones((D,), jnp.float32), 'w_o': jax.random.normal(ks[5], (D, D), jnp.float32) * scale}
    _L0_attn_all = _L0_attn_setup()
    _L0_attn_in = {k: v for k, v in _L0_attn_all.items() if k in ('norm_weight', 'w_q', 'w_k', 'w_v', 'w_f', 'gnorm_weight', 'w_o')}
    del _L0_attn_all

    def _L0_ffn_setup():
        import jax, jax.numpy as jnp
        import numpy as np
        TOP_K = 2
        key = jax.random.key(seed)
        ks = jax.random.split(key, 8)
        B, S, H, F, E = (1, 256, 256, 256, 8)
        Fs = 2 * F
        s = lambda k, shape, scale: jax.random.normal(k, shape, dtype=jnp.float32) * scale
        return {'x': s(ks[0], (B, S, H), 1.0), 'router_w': s(ks[1], (H, E), 0.02), 'gate_w': s(ks[2], (E, H, F), 0.02), 'up_w': s(ks[3], (E, H, F), 0.02), 'down_w': s(ks[4], (E, F, H), 0.02), 'shared_gate_w': s(ks[5], (H, Fs), 0.02), 'shared_up_w': s(ks[6], (H, Fs), 0.02), 'shared_down_w': s(ks[7], (Fs, H), 0.02)}
    _L0_ffn_all = _L0_ffn_setup()
    _L0_ffn_in = {k: v for k, v in _L0_ffn_all.items() if k in ('router_w', 'gate_w', 'up_w', 'down_w', 'shared_gate_w', 'shared_up_w', 'shared_down_w')}
    del _L0_ffn_all
    return {'x': x, 'L0_tok_emb': _L0_tok_in['emb'], 'L0_tok_pos': _L0_tok_in['pos'], 'L0_tok_wq': _L0_tok_in['wq'], 'L0_tok_wk': _L0_tok_in['wk'], 'L0_tok_wv': _L0_tok_in['wv'], 'L0_tok_wo': _L0_tok_in['wo'], 'L0_tok_wup': _L0_tok_in['wup'], 'L0_tok_bup': _L0_tok_in['bup'], 'L0_tok_wdown': _L0_tok_in['wdown'], 'L0_tok_bdown': _L0_tok_in['bdown'], 'L0_tok_ga': _L0_tok_in['ga'], 'L0_tok_ba': _L0_tok_in['ba'], 'L0_tok_gm': _L0_tok_in['gm'], 'L0_tok_bm': _L0_tok_in['bm'], 'L0_attn_norm_weight': _L0_attn_in['norm_weight'], 'L0_attn_w_q': _L0_attn_in['w_q'], 'L0_attn_w_k': _L0_attn_in['w_k'], 'L0_attn_w_v': _L0_attn_in['w_v'], 'L0_attn_w_f': _L0_attn_in['w_f'], 'L0_attn_gnorm_weight': _L0_attn_in['gnorm_weight'], 'L0_attn_w_o': _L0_attn_in['w_o'], 'L0_ffn_router_w': _L0_ffn_in['router_w'], 'L0_ffn_gate_w': _L0_ffn_in['gate_w'], 'L0_ffn_up_w': _L0_ffn_in['up_w'], 'L0_ffn_down_w': _L0_ffn_in['down_w'], 'L0_ffn_shared_gate_w': _L0_ffn_in['shared_gate_w'], 'L0_ffn_shared_up_w': _L0_ffn_in['shared_up_w'], 'L0_ffn_shared_down_w': _L0_ffn_in['shared_down_w']}

def reference(x, L0_tok_emb, L0_tok_pos, L0_tok_wq, L0_tok_wk, L0_tok_wv, L0_tok_wo, L0_tok_wup, L0_tok_bup, L0_tok_wdown, L0_tok_bdown, L0_tok_ga, L0_tok_ba, L0_tok_gm, L0_tok_bm, L0_attn_norm_weight, L0_attn_w_q, L0_attn_w_k, L0_attn_w_v, L0_attn_w_f, L0_attn_gnorm_weight, L0_attn_w_o, L0_ffn_router_w, L0_ffn_gate_w, L0_ffn_up_w, L0_ffn_down_w, L0_ffn_shared_gate_w, L0_ffn_shared_up_w, L0_ffn_shared_down_w):
    import jax
    import jax.numpy as jnp

    def _L0_tok_ref(x, emb, pos, wq, wk, wv, wo, wup, bup, wdown, bdown, ga, ba, gm, bm):
        import jax, jax.numpy as jnp
        import numpy as np
        V, D, CTX, NL = (8000, 256, 512, 2)
        B, T = (4, 512)
        EPS = 1e-05

        def _layer_norm(x, gamma, beta):
            mu = jnp.mean(x, axis=-1, keepdims=True)
            var = jnp.var(x, axis=-1, keepdims=True)
            return gamma * (x - mu) / jnp.sqrt(var + EPS) + beta
        Bx, Tx = x.shape
        d_model = emb.shape[-1]
        inv_sqrt_d = 1.0 / jnp.sqrt(jnp.asarray(d_model, jnp.float32))
        h = emb[x] + pos[:Tx][None, :, :]
        causal = jnp.tril(jnp.ones((Tx, Tx), bool))
        neg_inf = jnp.asarray(-jnp.inf, h.dtype)
        n_layers = wq.shape[0]
        for l in range(n_layers):
            residual = h
            q = h @ wq[l]
            k = h @ wk[l]
            v = h @ wv[l]
            wei = jnp.einsum('btd,bsd->bts', q, k) * inv_sqrt_d
            wei = jnp.where(causal[None], wei, neg_inf)
            attn = jax.nn.softmax(wei, axis=-1)
            out = jnp.einsum('bts,bsd->btd', attn, v)
            z = out @ wo[l]
            h = _layer_norm(residual + z, ga[l], ba[l])
            m = jax.nn.relu(h @ wup[l] + bup[l]) @ wdown[l] + bdown[l]
            h = _layer_norm(h + m, gm[l], bm[l])
        return h

    def _L0_attn_ref(hidden_states, norm_weight, w_q, w_k, w_v, w_f, gnorm_weight, w_o):
        import jax, jax.numpy as jnp
        import numpy as np
        H = 4
        DK = 64
        DV = 64
        M = 64
        GATE_NORM = 16.0
        EPS = 1e-05

        def _rmsnorm(x, w):
            var = jnp.mean(jnp.square(x), axis=-1, keepdims=True)
            return x * jax.lax.rsqrt(var + EPS) * w

        def _swish(x):
            return x * jax.nn.sigmoid(x)

        def _gsa_scan(q, k, v, s, g):
            B, Hh = (q.shape[1], q.shape[2])
            Hk0 = jnp.zeros((B, Hh, DK, M), q.dtype)
            Hv0 = jnp.zeros((B, Hh, M, DV), q.dtype)

            def step(carry, xs):
                Hk, Hv = carry
                qt, kt, vt, st, gt = xs
                lam = jnp.exp(gt)
                Hk = Hk * lam[:, :, None, :] + kt[..., :, None] * st[..., None, :]
                z = jnp.einsum('bhk,bhkm->bhm', qt, Hk)
                p = jax.nn.softmax(z, axis=-1)
                Hv = Hv * lam[..., :, None] + st[..., :, None] * vt[..., None, :]
                ot = jnp.einsum('bhm,bhmv->bhv', p, Hv)
                return ((Hk, Hv), ot)
            _, o = jax.lax.scan(step, (Hk0, Hv0), (q, k, v, s, g))
            return o
        B, T, D = hidden_states.shape
        h = _rmsnorm(hidden_states, norm_weight)
        q = _swish(h @ w_q.T).reshape(B, T, H, DK)
        k = _swish(h @ w_k.T).reshape(B, T, H, DK)
        v = _swish(h @ w_v.T).reshape(B, T, H, DV)
        f = jax.nn.log_sigmoid(h @ w_f.T).reshape(B, T, H, M) / GATE_NORM
        s = 1.0 - jnp.exp(f)
        tm = lambda x: jnp.transpose(x, (1, 0, 2, 3))
        o = _gsa_scan(tm(q), tm(k), tm(v), tm(s), tm(f))
        o = jnp.transpose(o, (1, 0, 2, 3)).reshape(B, T, H * DV)
        o = _swish(o)
        o = _rmsnorm(o, gnorm_weight)
        return o @ w_o.T

    def _L0_ffn_ref(x, router_w, gate_w, up_w, down_w, shared_gate_w, shared_up_w, shared_down_w):
        import jax, jax.numpy as jnp
        import numpy as np
        TOP_K = 2
        B, S, H = x.shape
        N = B * S
        xf = x.reshape(N, H)
        scores = jax.nn.softmax(xf @ router_w, axis=-1)
        topk_scores, topk_idx = jax.lax.top_k(scores, TOP_K)
        E = scores.shape[-1]
        combine = jnp.zeros((N, E), dtype=x.dtype).at[jnp.arange(N)[:, None], topk_idx].add(topk_scores)
        g = jnp.einsum('nh,ehf->enf', xf, gate_w)
        u = jnp.einsum('nh,ehf->enf', xf, up_w)
        y = jnp.einsum('enf,efh->enh', jax.nn.silu(g) * u, down_w)
        routed = jnp.einsum('enh,ne->nh', y, combine)
        shared = jax.nn.silu(xf @ shared_gate_w) * (xf @ shared_up_w) @ shared_down_w
        return (shared + routed).reshape(B, S, H)
    h = _L0_tok_ref(x, L0_tok_emb, L0_tok_pos, L0_tok_wq, L0_tok_wk, L0_tok_wv, L0_tok_wo, L0_tok_wup, L0_tok_bup, L0_tok_wdown, L0_tok_bdown, L0_tok_ga, L0_tok_ba, L0_tok_gm, L0_tok_bm)
    h = h + _L0_attn_ref(_layernorm(h, axis=-1), L0_attn_norm_weight, L0_attn_w_q, L0_attn_w_k, L0_attn_w_v, L0_attn_w_f, L0_attn_gnorm_weight, L0_attn_w_o)
    h = h + _L0_ffn_ref(_layernorm(h, axis=-1), L0_ffn_router_w, L0_ffn_gate_w, L0_ffn_up_w, L0_ffn_down_w, L0_ffn_shared_gate_w, L0_ffn_shared_up_w, L0_ffn_shared_down_w)
    return h

_drawn_inputs = setup_inputs


def setup_inputs(seed=0):
    import zlib

    import numpy as np

    out = dict(_drawn_inputs(seed))
    spreads = {'L0_tok_bup': (0.0, 0.1),
     'L0_tok_bdown': (0.0, 0.1),
     'L0_tok_ga': (1.0, 0.2),
     'L0_tok_ba': (0.0, 0.1),
     'L0_tok_gm': (1.0, 0.2),
     'L0_tok_bm': (0.0, 0.1),
     'L0_attn_norm_weight': (1.0, 0.2),
     'L0_attn_gnorm_weight': (1.0, 0.2)}
    factors = {'L0_tok_wq': 8.0,
     'L0_tok_wk': 8.0,
     'L0_attn_w_q': 8.0,
     'L0_attn_w_k': 8.0,
     'L0_attn_w_f': 5.419,
     'L0_ffn_router_w': 8.0,
     'L0_ffn_gate_w': 8.0,
     'L0_ffn_up_w': 8.0,
     'L0_ffn_down_w': 8.0,
     'L0_ffn_shared_gate_w': 2.909,
     'L0_ffn_shared_up_w': 2.734,
     'L0_ffn_shared_down_w': 2.894}
    for name, (base, spread) in spreads.items():
        noise = np.random.default_rng([zlib.crc32(name.encode()), seed]).standard_normal(out[name].shape)
        drawn = base * np.exp(spread * noise) if base else spread * noise
        out[name] = jnp.asarray(drawn.astype(out[name].dtype))
    for name, factor in factors.items():
        out[name] = (out[name] * factor).astype(out[name].dtype)
    return out
```

```python
from contextlib import ExitStack

import concourse.bass as bass
from concourse import mybir

F32 = mybir.dt.float32
F16 = mybir.dt.float16
I32 = mybir.dt.int32
ALU = mybir.AluOpType
ACT = mybir.ActivationFunctionType
AX = mybir.AxisListType.X

P = 128
G = 4
GT = G * P
EPS = 1e-5
WS = 64.0
IWS = 1.0 / WS
NEG = -1e30
GATE_NORM = 16.0
EXP_CLAMP = 80.0

A_LINKS = 106
M_LINKS = 5

A_USES = []
for _l in range(2):
    A_USES += [f"{n}.{_l}" for n in ("x0", "x1", "t0", "t1", "v0", "v1", "sc", "pt", "z0", "z1", "y0", "y1",
                                     *[f"up{m}" for m in range(8)], "dn0", "dn1")]
A_USES += ["gx0", "gx1", "q0", "q1", "q2", "q3", "fv0", "fv1", "fv2", "fv3", "D0", "D1",
           "A00", "A01", "A10", "A11", "st0", "st1", "gz0", "gz1", "gp0", "gp1", "B00", "B01", "B10", "B11",
           "o0", "o1", "ot0", "ot1", "w0", "w1", "mx0", "mx1"]


def moe_steps(E):
    out = [("router", 0)]
    for c in range(2 * E):
        out.append(("gu", c))
        if c % 2 and c >= 3:
            out.append(("down", (c - 3) // 2))
    return out + [("tail", 0), ("down", E - 1)]


def m_uses(E):
    out = []
    for name, n in moe_steps(E):
        if name == "router":
            out.append("rl")
        elif name == "gu":
            out += [f"g{n}", f"u{n}"]
        elif name == "down":
            out += [f"e{n}.0", f"e{n}.1"]
    return out


def build(nc, x, emb, pos, wq, wk, wv, wo, wup, bup, wdown, bdown, ga, ba, gm, bm,
          norm_w, a_q, a_k, a_v, a_f, gnorm_w, a_o, router_w, gate_w, up_w, down_w, sg_w, su_w, sd_w, out):
    SEQS, T = x.shape
    V, D = emb.shape
    NL = wq.shape[0]
    F = wup.shape[2]
    NE = gate_w.shape[0]
    HEADS, DK = 4, 64
    KB = D // P
    FB = F // P
    NG = SEQS // G
    NX = NE + sg_w.shape[1] // D
    NC = 2 * NX
    assert T == P and NL == 2 and KB == 2 and D == HEADS * DK and gate_w.shape[2] == D

    M_USES = m_uses(NX)
    BANK, ORD, PER = {}, {}, [0] * 8
    for base, uses in ((0, A_USES), (4, M_USES)):
        for n, name in enumerate(uses):
            b = base + n % 4
            BANK[name], ORD[name] = b, PER[b]
            PER[b] += 1

    with ExitStack() as ctx:
        def sb(name, shape, dt=F32):
            return ctx.enter_context(nc.sbuf_tensor(name, shape, dt))

        def sem(name):
            return ctx.enter_context(nc.semaphore(name))

        bank = [ctx.enter_context(nc.psum_tensor(f"bank{b}", [P, 512], F32)) for b in range(8)]

        Wm = sb("Wm", [P, 2, NL, KB, D], F16)
        Wvo = sb("Wvo", [P, 2, NL, KB, D], F16)
        Wup = sb("Wup", [P, 2, NL, KB, F], F16)
        Wdn = sb("Wdn", [P, 2, NL, FB, D], F16)
        Wqk = sb("Wqk", [P, 2, 2, KB, D], F16)
        Wfv = sb("Wfv", [P, 2, KB, 2 * D], F16)
        Wao = sb("Wao", [P, 2, KB, D], F16)
        Wg = sb("Wg", [P, 2, NX, KB, D], F16)
        Wu = sb("Wu", [P, 2, NX, KB, D], F16)
        Wd = sb("Wd", [P, 2, NX, KB, D], F16)
        rw = sb("rw", [P, KB, NE])

        ident = sb("ident", [P, P])
        causal = sb("causal", [P, P])
        upper = sb("upper", [P, P])
        tri = sb("tri", [P, P])
        posb = sb("posb", [P, D])
        gb = sb("gb", [P, NL, 4, D])
        gcol = sb("gcol", [P, NL, 4, KB])
        bupc = sb("bupc", [P, NL, FB])
        nwc = sb("nwc", [P, 2, KB])
        idx = sb("idx", [P, SEQS + G], I32)
        cur = sb("cur", [P, G], I32)
        nws = sb("nws", [P, 2, KB])

        smax = sb("smax", [P, G])
        nbias = sb("nbias", [P, G])
        rsum = sb("rsum", [P, G])
        rinv = sb("rinv", [P, G])
        stat = sb("stat", [P, G, 6])
        mv = sb("mv", [P, G, 2])
        vare = sb("vare", [P, G])
        rstd = sb("rstd", [P, G])
        newt = sb("newt", [P, G])
        zmax = sb("zmax", [P, G * HEADS])
        zsum = sb("zsum", [P, G * HEADS])
        ssq = sb("ssq", [P, G])
        lg = sb("lg", [P, G, NE])
        top = sb("top", [P, G, 8])
        ex = sb("ex", [P, G, NE])
        keep = sb("keep", [P, G, NE])
        esum = sb("esum", [P, G])
        comb = sb("comb", [P, G, NE])

        W1K = 1024
        arena = sb("arena", [P, 21 * W1K])

        def cut(at, n=1, lo=0, size=None):
            a = at * W1K + lo
            return arena[:, a:a + (size or n * W1K)]

        def tok(ap):
            return ap.rearrange("p (j d) -> p j d", j=G)

        def feat(ap):
            return ap.rearrange("p (k t) -> p k t", k=KB)

        H = tok(cut(0))
        HR = tok(cut(1)); PPT = feat(cut(1))
        HTF = feat(cut(2)); SPT = feat(cut(2))
        HTP = cut(3).bitcast(F16).rearrange("p (a k t) -> p a k t", a=2, k=KB)
        TT = feat(cut(4)); QT = feat(cut(4))
        VO = tok(cut(5)); KT = feat(cut(5))
        U = tok(cut(6))
        Xn = tok(cut(7))
        EMB = tok(cut(8)); VB = tok(cut(8))
        EB = cut(9)
        PB = cut(10)
        SM = cut(10, size=512).rearrange("p (j s) -> p j s", j=G)
        PT = cut(10, lo=512, size=512).rearrange("p (j s) -> p j s", j=G)
        AP = cut(11, 4).bitcast(F16).rearrange("p (a f t) -> p a f t", a=2, f=FB)
        AT = cut(11, 2).rearrange("p (a b c t) -> p a b c t", a=2, b=2, c=4)
        BT = cut(13, 2).rearrange("p (a b c t) -> p a b c t", a=2, b=2, c=4)
        XF = HTF
        XP = cut(15).bitcast(F16).rearrange("p (a k t) -> p a k t", a=2, k=KB)
        ACC = tok(cut(16))
        ME = cut(17).rearrange("p (b t) -> p b t", b=2)
        MA = cut(18).rearrange("p (b t) -> p b t", b=2)
        MP = cut(19, 2).bitcast(F16).rearrange("p (b a m t) -> p b a m t", b=2, a=2, m=2)

        s_load = [sem(f"load{n}") for n in range(16)]
        s_const = sem("const_made")
        s_step = sem("setup_dve_step")
        s_ids = sem("ids_as_floats")
        s_nws = sem("norm_weights_scaled")
        s_idx = sem("ids_transposed")
        s_sfull = sem("setup_bank_full")
        s_shi = sem("setup_hi_made")
        s_slo = sem("setup_lo_made")
        s_rawt = sem("raw_transposed")
        full = [sem(f"bank_full{b}") for b in range(8)]
        free = [sem(f"bank_free{b}") for b in range(8)]
        cur_ready = sem("cur_ready")
        emb_ready = sem("emb_ready")
        emb_used = sem("emb_used")
        h_ready = sem("h_embedded")
        ht_ready = sem("ht_ready")
        nb_ready = sem("nbias_ready")
        p_ready = sem("probs_ready")
        x_ready = sem("normed_ready")
        hr_ready = sem("residual_ready")
        h_affine = sem("h_affine_ready")
        relu_ready = sem("relu_ready")
        a_ready = sem("hidden_ready")
        qe_ready = sem("q_tanh_ready")
        ve_ready = sem("v_tanh_ready")
        mn_ready = sem("f_min_ready")
        fl_ready = sem("f_log_ready")
        g_ready = sem("gate_ready")
        es_ready = sem("gate_exp_ready")
        ei_ready = sem("decay_inv_exp_ready")
        e_ready = sem("decay_exp_ready")
        sp_ready = sem("slots_ready")
        zs_ready = sem("z_shifted")
        ze_ready = sem("z_exp_ready")
        pp_ready = sem("slot_probs_ready")
        oe_ready = sem("o_tanh_ready")
        os_ready = sem("o_swished")
        xm_ready = sem("moe_x_ready")
        acc_ready = sem("acc_started")
        rx_ready = sem("router_shifted")
        re_ready = sem("router_exp_ready")
        me_ready = sem("moe_tanh_ready")
        mhi_ready = sem("moe_hi_ready")
        mlo_ready = sem("moe_hidden_ready")
        acc_done = sem("acc_done")
        out_done = sem("out_written")
        dve_a = sem("dve_step_a")
        dve_m = sem("dve_step_m")
        pool_a = sem("pool_step_a")
        idle = sem("wait_holder")
        acc_free = sem("acc_free")
        sq_ready = sem("squares_summed")
        fa_step = sem("f_abs_exp_step")

        def passes(w, xp):
            return ((w[0], xp[0]), (w[0], xp[1]), (w[1], xp[0]))

        L_X, L_QKVO, L_ATT, L_UP, L_DN, L_WG, L_WU, L_WD, L_ROWS, L_COLS = 0, 1, 3, 4, 6, 8, 9, 10, 11, 12
        MAT = KB * D
        o_att = NL * 4 * MAT
        o_up = o_att + 5 * MAT
        o_dn = o_up + NL * KB * F
        o_wg = o_dn + NL * FB * D
        o_end = o_wg + NX * MAT
        bdn = arena[:, o_end:o_end + NL * D].rearrange("p (l d) -> p l d", l=NL)
        ids = arena[0:SEQS, o_end + NL * D:o_end + NL * D + 3 * P].rearrange("p (a t) -> p a t", a=3)
        xi, xf, xneg = ids[:, 0].bitcast(I32), ids[:, 1], ids[:, 2]
        QKVO = [arena[:, l * 4 * MAT:(l + 1) * 4 * MAT].rearrange("p (w k d) -> p w k d", w=4, k=KB) for l in range(NL)]
        ATT = arena[:, o_att:o_up].rearrange("p (w k d) -> p w k d", w=5, k=KB)
        RUP = [arena[:, o_up + l * KB * F:o_up + (l + 1) * KB * F] for l in range(NL)]
        RDN = [arena[:, o_dn + l * FB * D:o_dn + (l + 1) * FB * D] for l in range(NL)]
        RX = [arena[:, o:o + NX * MAT] for o in (o_wg, o_up, o_wg)]
        WX = (Wg, Wu, Wd)
        WT = Wg[:].rearrange("p a e k d -> p (a e k d)").bitcast(F32)[:, 0:NL * 3 * MAT].rearrange(
            "p (l w k d) -> p l w k d", l=NL, w=3, k=KB)

        def flat(ap):
            return ap.rearrange("p a b -> p (a b)")

        def att_dst(n, a, k):
            if n < 2:
                return Wqk[:, a, n, k]
            if n < 4:
                return Wfv[:, a, k, (n - 2) * D:(n - 1) * D]
            return Wao[:, a, k]

        cols = [(nwc[:, 0], norm_w), (nwc[:, 1], gnorm_w)]
        for l in range(NL):
            cols += [(gcol[:, l, n], w[l]) for n, w in enumerate((ga, ba, gm, bm))]
            cols.append((bupc[:, l], bup[l]))

        with nc.Block() as block:
            @block.sync
            def _(sp):
                sp.dma_start(xi, x).then_inc(s_load[L_X], 16)
                for l in range(NL):
                    for n, w in enumerate((wq, wk, wv, wo)):
                        sp.dma_start(QKVO[l][:, n], w[l].rearrange("(k p) d -> p k d", p=P)).then_inc(s_load[L_QKVO + l], 16)
                for n, w in enumerate((a_q, a_k, a_f, a_v, a_o)):
                    sp.dma_start(ATT[:, n], w.rearrange("(k p) d -> p k d", p=P)).then_inc(s_load[L_ATT], 16)
                for l in range(NL):
                    sp.dma_start(RUP[l].rearrange("p (k f) -> p k f", k=KB),
                                 wup[l].rearrange("(k p) f -> p k f", p=P)).then_inc(s_load[L_UP + l], 16)
                    sp.dma_start(RDN[l].rearrange("p (k d) -> p k d", k=FB),
                                 wdown[l].rearrange("(k p) d -> p k d", p=P)).then_inc(s_load[L_DN + l], 16)
                for n, (w, ws) in enumerate(((gate_w, sg_w), (up_w, su_w), (down_w, sd_w))):
                    if n == 1:
                        sp.wait_ge(s_slo, 2 * NL)
                    if n == 2:
                        sp.wait_ge(s_slo, 2 * NL + 10)
                    v = RX[n].rearrange("p (e k d) -> p e k d", e=NX, k=KB)
                    for e in range(NE):
                        sp.dma_start(v[:, e], w[e].rearrange("(k p) d -> p k d", p=P)).then_inc(s_load[L_WG + n], 16)
                    for e in range(NX - NE):
                        src = ws[:, e * D:(e + 1) * D] if n < 2 else ws[e * D:(e + 1) * D, :]
                        sp.dma_start(v[:, NE + e], src.rearrange("(k p) d -> p k d", p=P)).then_inc(s_load[L_WG + n], 16)

            @block.scalar
            def _(act):
                rows = [(posb[:], pos[0:P, :])]
                for l in range(NL):
                    rows += [(gb[:, l, n], w[l].partition_broadcast(P)) for n, w in enumerate((ga, ba, gm, bm))]
                    rows.append((bdn[:, l], bdown[l].partition_broadcast(P)))
                for dst, src in rows:
                    act.dma_start(dst, src).then_inc(s_load[L_ROWS], 16)
                for dst, src in cols:
                    act.dma_start(dst, src.rearrange("(k p) -> p k", p=P),
                                  allow_slow_non_contiguous=True).then_inc(s_load[L_COLS], 16)
                act.dma_start(rw[:], router_w.rearrange("(k p) e -> p k e", p=P)).then_inc(s_load[L_COLS], 16)
                for l in range(NL):
                    act.wait_ge(s_load[L_UP + l], 16)
                    act.activation(flat(Wup[:, 0, l]), RUP[l], ACT.Copy, scale=WS).then_inc(s_shi, 1)
                    act.wait_ge(s_load[L_DN + l], 16)
                    act.activation(flat(Wdn[:, 0, l]), RDN[l], ACT.Copy, scale=WS).then_inc(s_shi, 1)
                for n in range(3 * NL):
                    act.wait_ge(s_sfull, 2 + n)
                    act.activation(flat(WT[:, n // 3, n % 3]), bank[1 + n][:], ACT.Copy).then_inc(s_rawt, 1)
                act.wait_ge(s_nws, 1)
                for n in range(5):
                    act.wait_ge(s_sfull, 8 + n)
                    for k in range(KB):
                        i = act.activation(att_dst(n, 0, k), bank[(7 + n) % 8][:, k * D:(k + 1) * D], ACT.Identity,
                                           scale=nws[:, n // 4, k:k + 1])
                    i.then_inc(s_shi, 1)
                for n in range(2 * NL):
                    act.wait_ge(s_sfull, 13 + n)
                    act.activation(flat((Wm, Wvo)[n % 2][:, 0, n // 2]), bank[(12 + n) % 8][:], ACT.Copy,
                                   scale=WS).then_inc(s_shi, 1)
                for n in range(3):
                    act.wait_ge(s_load[L_WG + n], 16 * NX)
                    act.activation(WX[n][:, 0].rearrange("p e k d -> p (e k d)"), RX[n], ACT.Copy, scale=WS).then_inc(s_shi, 1)

            @block.gpsimd
            def _(pool):
                pool.memset(ident[:], 0.0).then_inc(s_const, 1)
                pool.memset(causal[:], 0.0).then_inc(s_const, 1)
                pool.memset(upper[:], 1.0).then_inc(s_const, 1)
                pool.wait_ge(s_const, 3)
                pool.affine_select(out=ident[:], in_=ident[:], compare_op=ALU.not_equal, fill=1.0, base=0,
                                   pattern=[[-1, P]], channel_multiplier=1).then_inc(s_const, 1)
                pool.affine_select(out=causal[:], in_=causal[:], compare_op=ALU.is_ge, fill=NEG, base=0,
                                   pattern=[[-1, P]], channel_multiplier=1).then_inc(s_const, 1)
                pool.affine_select(out=upper[:], in_=upper[:], compare_op=ALU.is_ge, fill=0.0, base=0,
                                   pattern=[[1, P]], channel_multiplier=-1).then_inc(s_const, 1)
                pool.wait_ge(s_load[L_ROWS], 16 * (1 + 5 * NL))
                for l in range(NL):
                    pool.tensor_tensor(gb[:, l, 1], gb[:, l, 1], bdn[:, l], ALU.add).then_inc(s_const, 1)

            @block.vector
            def _(dve):
                steps = [0]

                def link(ins):
                    steps[0] += 1
                    ins.then_inc(s_step, 1)
                    dve.wait_ge(s_step, steps[0])

                dve.wait_ge(s_load[L_X], 16)
                link(dve.tensor_copy(xf, xi))
                link(dve.tensor_scalar(xneg, xf, 0.0, float(V), ALU.is_lt, ALU.mult))
                link(dve.tensor_tensor(xf, xf, xneg, ALU.add))
                dve.tensor_scalar(xf, xf, 0.0, float(V - 1), ALU.max, ALU.min).then_inc(s_ids, 1)
                dve.memset(idx[:, SEQS:SEQS + G], 0)
                dve.wait_ge(s_const, 6)
                dve.tensor_scalar(tri[:], upper[:], upper[:, P // 2 - 1:P // 2], None, ALU.subtract)
                dve.wait_ge(s_load[L_COLS], 16 * (len(cols) + 1))
                dve.tensor_scalar(nws[:], nwc[:], WS, None, ALU.mult).then_inc(s_nws, 1)
                dve.wait_ge(s_sfull, 1)
                dve.tensor_copy(idx[:, 0:SEQS], bank[0][:, 0:SEQS]).then_inc(s_idx, 1)
                for n in range(2 * NL):
                    l = n // 2
                    w, raw = (Wdn, RDN[l]) if n % 2 else (Wup, RUP[l])
                    dve.wait_ge(s_shi, n + 1)
                    dve.scalar_tensor_tensor(flat(w[:, 1, l]), raw, WS, flat(w[:, 0, l]), ALU.mult, ALU.subtract).then_inc(s_slo, 1)
                dve.wait_ge(s_nws, 1)
                for n in range(5):
                    dve.wait_ge(s_shi, 2 * NL + n + 1)
                    for k in range(KB):
                        i = dve.scalar_tensor_tensor(att_dst(n, 1, k), bank[(7 + n) % 8][:, k * D:(k + 1) * D],
                                                     nws[:, n // 4, k:k + 1], att_dst(n, 0, k), ALU.mult, ALU.subtract)
                    i.then_inc(s_slo, 1)
                for n in range(2 * NL):
                    w = (Wm, Wvo)[n % 2]
                    dve.wait_ge(s_shi, 2 * NL + 5 + n + 1)
                    dve.scalar_tensor_tensor(flat(w[:, 1, n // 2]), bank[(12 + n) % 8][:], WS, flat(w[:, 0, n // 2]),
                                             ALU.mult, ALU.subtract).then_inc(s_slo, 1)
                for n in range(3):
                    dve.wait_ge(s_shi, 2 * NL + 5 + 2 * NL + n + 1)
                    dve.scalar_tensor_tensor(WX[n][:, 1].rearrange("p e k d -> p (e k d)"), RX[n], WS,
                                             WX[n][:, 0].rearrange("p e k d -> p (e k d)"), ALU.mult,
                                             ALU.subtract).then_inc(s_slo, 1)

            @block.tensor
            def _(pe):
                pe.wait_ge(s_const, 6)
                pe.wait_ge(s_ids, 1)
                pe.transpose(bank[0][:, 0:SEQS], xf, ident[0:SEQS, 0:SEQS]).then_inc(s_sfull, 1)

                def turn(src, b):
                    for kk in range(KB):
                        for k in range(KB):
                            i = pe.transpose(bank[b][:, kk * D + k * P:kk * D + (k + 1) * P],
                                             src[:, k, kk * P:(kk + 1) * P], ident[:])
                    i.then_inc(s_sfull, 1)

                for n in range(3 * NL):
                    if n % 3 == 0:
                        pe.wait_ge(s_load[L_QKVO + n // 3], 64)
                    turn(QKVO[n // 3][:, n % 3], 1 + n)
                pe.wait_ge(s_load[L_ATT], 80)
                for n in range(5):
                    if n == 1:
                        pe.wait_ge(s_idx, 1)
                        pe.wait_ge(s_rawt, 3 * NL)
                    turn(ATT[:, n], (7 + n) % 8)
                for n in range(2 * NL):
                    l, w = divmod(n, 2)
                    if n == 3:
                        pe.wait_ge(s_slo, 2 * NL + 1)
                    b = bank[(12 + n) % 8]
                    for k in range(KB):
                        for c in range(KB):
                            lhs = WT[:, l, 2 * w, c, k * P:(k + 1) * P]
                            rhs = QKVO[l][:, 3, c] if w else WT[:, l, 1, c]
                            i = pe.matmul(b[:, k * D:(k + 1) * D], lhs, rhs, start=(c == 0), stop=(c == KB - 1))
                    i.then_inc(s_sfull, 1)

        A_STEPS = [("embed",)]
        for l in range(NL):
            A_STEPS += [("x", l), ("tv", l), ("sc", l), ("pt", l), ("z", l), ("y", l), ("up", l), ("dn", l)]
        A_STEPS += [(n,) for n in ("gx", "qk", "fv", "decay", "scores", "st", "gz", "gp", "vscores", "o", "ot", "w", "mx")]
        M_STEPS = moe_steps(NX)
        MERGED = []
        done = 0
        for n, s in enumerate(A_STEPS):
            want = min(len(M_STEPS), (n + 1) * len(M_STEPS) // (len(A_STEPS) - 2)) if s[0] != "mx" else len(M_STEPS)
            MERGED += [("m", m) for m in M_STEPS[done:want]]
            done = want
            MERGED.append(("a", s))

        def run(eng, do_a, do_m):
            for s in A_STEPS:
                do_a(0, *s)
            with eng.Fori(1, NG) as g:
                for kind, s in MERGED:
                    if kind == "a":
                        do_a(g, *s)
                    else:
                        do_m(g - 1, *s)
            for s in M_STEPS:
                do_m(NG - 1, *s)

        def filled(g, name):
            return full[BANK[name]], PER[BANK[name]] * g + ORD[name] + 1

        def vacant(g, name):
            return free[BANK[name]], PER[BANK[name]] * g + ORD[name] + 1

        def taken(g, name):
            return free[BANK[name]], PER[BANK[name]] * g + ORD[name] + 2

        def ps(name):
            return bank[BANK[name]]

        HT = {"x0": 0, "y0": 1, "x1": 2, "y1": 3, "gx": 4, "ot": 5}
        XR = {"z0": 0, "dn0": 1, "z1": 2, "dn1": 3, "gx": 4, "w": 5}

        def ht(g, key):
            return ht_ready, 2 * len(HT) * g + 2 * HT[key] + 2

        with nc.Block() as block:
            @block.sync
            def _(sp):
                def do_m(g, name, c):
                    if name == "down" and c == NX - 1:
                        sp.wait_ge(acc_done, g + 1)
                        sp.dma_start(out[bass.ds(g * G, G)].rearrange("s t d -> t s d"), ACC).then_inc(out_done, 16)
                        sp.wait_ge(out_done, 16 * g + 16)
                        sp.sem_inc(acc_free, 1)

                sp.sem_inc(acc_free, 1)
                run(sp, lambda g, *s: None, do_m)

            @block.tensor
            def _(pe):
                def products(dst, pairs):
                    for n, (lhs, rhs) in enumerate(pairs):
                        i = pe.matmul(dst, lhs, rhs, start=(n == 0), stop=(n == len(pairs) - 1))
                    return i

                def by_feature(dst, w, xp, m):
                    return products(dst, [(wa[:, k, m * P:(m + 1) * P], xa[:, k])
                                          for k in range(w[0].shape[1]) for wa, xa in passes(w, xp)])

                def by_token(dst, w, xp, j):
                    return products(dst, [(xa[:, k, j * P:(j + 1) * P], wa[:, k])
                                          for k in range(w[0].shape[1]) for wa, xa in passes(w, xp)])

                def turn(g, src, stem):
                    for k in range(KB):
                        name = stem(k)
                        pe.wait_ge(*vacant(g, name))
                        for j in range(G):
                            i = pe.transpose(ps(name)[:, j * P:(j + 1) * P], src[:, j, k * P:(k + 1) * P], ident[:])
                        i.then_inc(full[BANK[name]], 1)

                H2 = (HTP[:, 0], HTP[:, 1])
                X2 = (XP[:, 0], XP[:, 1])

                def do_a(g, name, l=None):
                    if name == "x":
                        if l == 0:
                            pe.wait_ge(h_ready, g + 1)
                            turn(g, H, lambda k: f"x{k}.0")
                        else:
                            pe.wait_ge(x_ready, 6 * g + XR["dn0"] + 1)
                            turn(g, Xn, lambda k: f"x{k}.1")
                    elif name == "tv":
                        pe.wait_ge(*ht(g, f"x{l}"))
                        w = (Wm[:, 0, l], Wm[:, 1, l])
                        for m in range(KB):
                            pe.wait_ge(*vacant(g, f"t{m}.{l}"))
                            by_feature(ps(f"t{m}.{l}")[:], w, H2, m).then_inc(full[BANK[f"t{m}.{l}"]], 1)
                        w = (Wvo[:, 0, l], Wvo[:, 1, l])
                        for jj in range(G // 2):
                            n = f"v{jj}.{l}"
                            pe.wait_ge(*vacant(g, n))
                            for j2 in range(2):
                                i = by_token(ps(n)[:, j2 * D:(j2 + 1) * D], w, H2, 2 * jj + j2)
                            i.then_inc(full[BANK[n]], 1)
                    elif name == "sc":
                        n = f"sc.{l}"
                        pe.wait_ge(*taken(g, f"t0.{l}"))
                        pe.wait_ge(*taken(g, f"t1.{l}"))
                        pe.wait_ge(*vacant(g, n))
                        for j in range(G):
                            js = slice(j * P, (j + 1) * P)
                            i = products(ps(n)[:, js], [(TT[:, k, js], HTF[:, k, js]) for k in range(KB)])
                        i.then_inc(full[BANK[n]], 1)
                    elif name == "pt":
                        n = f"pt.{l}"
                        pe.wait_ge(p_ready, NL * g + l + 1)
                        pe.wait_ge(*vacant(g, n))
                        for j in range(G):
                            i = pe.transpose(ps(n)[:, j * P:(j + 1) * P], SM[:, j], ident[:])
                        i.then_inc(full[BANK[n]], 1)
                    elif name == "z":
                        pe.wait_ge(*taken(g, f"pt.{l}"))
                        pe.wait_ge(*taken(g, f"v0.{l}"))
                        pe.wait_ge(*taken(g, f"v1.{l}"))
                        for jj in range(G // 2):
                            n = f"z{jj}.{l}"
                            pe.wait_ge(*vacant(g, n))
                            for j2 in range(2):
                                i = pe.matmul(ps(n)[:, j2 * D:(j2 + 1) * D], PT[:, 2 * jj + j2], VO[:, 2 * jj + j2],
                                              start=True, stop=True)
                            i.then_inc(full[BANK[n]], 1)
                    elif name == "y":
                        pe.wait_ge(x_ready, 6 * g + XR[f"z{l}"] + 1)
                        turn(g, Xn, lambda k: f"y{k}.{l}")
                    elif name == "up":
                        pe.wait_ge(*ht(g, f"y{l}"))
                        w = (Wup[:, 0, l], Wup[:, 1, l])
                        for m in range(FB):
                            n = f"up{m}.{l}"
                            pe.wait_ge(*vacant(g, n))
                            by_feature(ps(n)[:], w, H2, m).then_inc(full[BANK[n]], 1)
                    elif name == "dn":
                        pe.wait_ge(a_ready, NL * FB * g + (l + 1) * FB)
                        w = (Wdn[:, 0, l], Wdn[:, 1, l])
                        for jj in range(G // 2):
                            n = f"dn{jj}.{l}"
                            pe.wait_ge(*vacant(g, n))
                            for j2 in range(2):
                                i = by_token(ps(n)[:, j2 * D:(j2 + 1) * D], w, (AP[:, 0], AP[:, 1]), 2 * jj + j2)
                            i.then_inc(full[BANK[n]], 1)
                    elif name == "gx":
                        pe.wait_ge(x_ready, 6 * g + XR["gx"] + 1)
                        turn(g, Xn, lambda k: f"gx{k}")
                    elif name == "qk":
                        pe.wait_ge(*ht(g, "gx"))
                        for n in range(4):
                            pe.wait_ge(*vacant(g, f"q{n}"))
                            w = (Wqk[:, 0, n // 2], Wqk[:, 1, n // 2])
                            by_feature(ps(f"q{n}")[:], w, H2, n % 2).then_inc(full[BANK[f"q{n}"]], 1)
                    elif name == "fv":
                        for j in range(G):
                            pe.wait_ge(*vacant(g, f"fv{j}"))
                            by_token(ps(f"fv{j}")[:], (Wfv[:, 0], Wfv[:, 1]), H2, j).then_inc(full[BANK[f"fv{j}"]], 1)
                    elif name == "decay":
                        pe.wait_ge(g_ready, g + 1)
                        for jj in range(G // 2):
                            n = f"D{jj}"
                            pe.wait_ge(*vacant(g, n))
                            for j2 in range(2):
                                i = pe.matmul(ps(n)[:, j2 * D:(j2 + 1) * D], tri[:], U[:, 2 * jj + j2], start=True, stop=True)
                            i.then_inc(full[BANK[n]], 1)
                    elif name in ("scores", "vscores"):
                        if name == "scores":
                            stem, left, right = "A", KT, QT
                            pe.wait_ge(*taken(g, "q3"))
                        else:
                            stem, left, right = "B", SPT, PPT
                            for n in ("st0", "st1", "gp0", "gp1"):
                                pe.wait_ge(*taken(g, n))
                        for jj in range(G // 2):
                            for par in range(2):
                                pe.wait_ge(*vacant(g, f"{stem}{jj}{par}"))
                            for j2 in range(2):
                                js = slice((2 * jj + j2) * P, (2 * jj + j2 + 1) * P)
                                for hc in range(2):
                                    for par in range(2):
                                        n = f"{stem}{jj}{par}"
                                        c = j2 * 2 + hc
                                        rows = slice(par * DK, (par + 1) * DK)
                                        i = pe.matmul(ps(n)[:, c * P:(c + 1) * P], left[rows, hc, js], right[rows, hc, js],
                                                      start=True, stop=True)
                                        if c == 3:
                                            i.then_inc(full[BANK[n]], 1)
                    elif name == "st":
                        pe.wait_ge(sp_ready, g + 1)
                        turn(g, Xn, lambda k: f"st{k}")
                    elif name == "gz":
                        pe.wait_ge(*taken(g, "A01"))
                        pe.wait_ge(*taken(g, "A10"))
                        pe.wait_ge(*taken(g, "A11"))
                        for jj in range(G // 2):
                            n = f"gz{jj}"
                            pe.wait_ge(*vacant(g, n))
                            for j2 in range(2):
                                for h in range(HEADS):
                                    c = j2 * HEADS + h
                                    i = pe.matmul(ps(n)[:, c * DK:(c + 1) * DK], AT[:, jj, h % 2, j2 * 2 + h // 2],
                                                  Xn[:, 2 * jj + j2, h * DK:(h + 1) * DK], start=True, stop=True)
                            i.then_inc(full[BANK[n]], 1)
                    elif name == "gp":
                        pe.wait_ge(pp_ready, g + 1)
                        turn(g, tok(PB), lambda k: f"gp{k}")
                    elif name == "o":
                        pe.wait_ge(*taken(g, "B01"))
                        pe.wait_ge(*taken(g, "B10"))
                        pe.wait_ge(*taken(g, "B11"))
                        pe.wait_ge(*taken(g, "fv3"))
                        for jj in range(G // 2):
                            n = f"o{jj}"
                            pe.wait_ge(*vacant(g, n))
                            for j2 in range(2):
                                for h in range(HEADS):
                                    c = j2 * HEADS + h
                                    i = pe.matmul(ps(n)[:, c * DK:(c + 1) * DK], BT[:, jj, h % 2, j2 * 2 + h // 2],
                                                  VB[:, 2 * jj + j2, h * DK:(h + 1) * DK], start=True, stop=True)
                            i.then_inc(full[BANK[n]], 1)
                    elif name == "ot":
                        pe.wait_ge(os_ready, g + 1)
                        turn(g, U, lambda k: f"ot{k}")
                    elif name == "w":
                        pe.wait_ge(*ht(g, "ot"))
                        for jj in range(G // 2):
                            n = f"w{jj}"
                            pe.wait_ge(*vacant(g, n))
                            for j2 in range(2):
                                i = by_token(ps(n)[:, j2 * D:(j2 + 1) * D], (Wao[:, 0], Wao[:, 1]), H2, 2 * jj + j2)
                            i.then_inc(full[BANK[n]], 1)
                    elif name == "mx":
                        pe.wait_ge(x_ready, 6 * g + XR["w"] + 1)
                        turn(g, Xn, lambda k: f"mx{k}")

                def do_m(g, name, c):
                    if name == "router":
                        pe.wait_ge(*taken(g, "mx0"))
                        pe.wait_ge(xm_ready, 2 * g + 2)
                        pe.wait_ge(*vacant(g, "rl"))
                        for j in range(G):
                            i = products(ps("rl")[:, j * NE:(j + 1) * NE],
                                         [(XF[:, k, j * P:(j + 1) * P], rw[:, k]) for k in range(KB)])
                        i.then_inc(full[BANK["rl"]], 1)
                    elif name == "gu":
                        e, m = divmod(c, 2)
                        for n, w in ((f"g{c}", Wg), (f"u{c}", Wu)):
                            pe.wait_ge(*vacant(g, n))
                            by_feature(ps(n)[:], (w[:, 0, e], w[:, 1, e]), X2, m).then_inc(full[BANK[n]], 1)
                    elif name == "down":
                        e = c
                        pe.wait_ge(mlo_ready, NC * g + 2 * e + 2)
                        for jj in range(G // 2):
                            n = f"e{e}.{jj}"
                            pe.wait_ge(*vacant(g, n))
                            for j2 in range(2):
                                i = by_token(ps(n)[:, j2 * D:(j2 + 1) * D], (Wd[:, 0, e], Wd[:, 1, e]),
                                             (MP[:, e % 2, 0], MP[:, e % 2, 1]), 2 * jj + j2)
                            i.then_inc(full[BANK[n]], 1)

                for b in range(8):
                    pe.sem_inc(free[b], 1)
                run(pe, do_a, do_m)

            @block.scalar
            def _(act):
                def take(g, name, dst, **kw):
                    act.wait_ge(*filled(g, name))
                    act.activation(dst, ps(name)[:], kw.pop("func", ACT.Copy), **kw).then_inc(free[BANK[name]], 1)

                def take_pair(g, name, dst, hi, scale=1.0, bias=0.0):
                    act.wait_ge(*filled(g, name))
                    act.activation(dst, ps(name)[:], ACT.Identity, scale=scale, bias=bias)
                    act.activation(hi, ps(name)[:], ACT.Identity, scale=scale, bias=bias).then_inc(free[BANK[name]], 1)

                def do_a(g, name, l=None):
                    if name == "x":
                        for k in range(KB):
                            sc, bi = (gcol[:, 0, 2, k:k + 1], gcol[:, 0, 3, k:k + 1]) if l else (1.0, 0.0)
                            take_pair(g, f"x{k}.{l}", HTF[:, k], HTP[:, 0, k], sc, bi)
                    elif name == "tv":
                        take(g, f"t0.{l}", TT[:, 0], scale=IWS)
                        take(g, f"v0.{l}", flat(VO[:, 0:2]), scale=IWS)
                    elif name == "sc":
                        act.wait_ge(nb_ready, NL * g + l + 1)
                        for j in range(G):
                            i = act.activation(SM[:, j], SM[:, j], ACT.Exp, bias=nbias[:, j:j + 1], scale=1.0 / D ** 0.5,
                                               accum_out=rsum[:, j:j + 1])
                        i.then_inc(p_ready, 1)
                    elif name == "y":
                        for k in range(KB):
                            take_pair(g, f"y{k}.{l}", HTF[:, k], HTP[:, 0, k], gcol[:, l, 0, k:k + 1], gcol[:, l, 1, k:k + 1])
                    elif name == "up":
                        for m in range(FB):
                            n = f"up{m}.{l}"
                            bias = bupc[:, l, m:m + 1]
                            act.wait_ge(*filled(g, n))
                            if m >= 2:
                                act.wait_ge(a_ready, NL * FB * g + l * FB + m - 1)
                            act.activation(EB[:, (m % 2) * GT:(m % 2 + 1) * GT], ps(n)[:], ACT.Relu, bias=bias, scale=IWS)
                            act.activation(AP[:, 0, m], ps(n)[:], ACT.Relu, bias=bias, scale=IWS).then_inc(free[BANK[n]], 1)
                    elif name == "gx":
                        for k in range(KB):
                            take_pair(g, f"gx{k}", HTF[:, k], HTP[:, 0, k])
                    elif name == "qk":
                        for n in range(4):
                            act.wait_ge(*filled(g, f"q{n}"))
                            if n >= 2:
                                act.wait_ge(*taken(g, f"q{n - 2}"))
                            act.activation(EB[:, (n % 2) * GT:(n % 2 + 1) * GT], ps(f"q{n}")[:], ACT.Tanh,
                                           scale=0.5 * IWS).then_inc(qe_ready, 1)
                    elif name == "fv":
                        for j in range(G):
                            js = slice(j * D, (j + 1) * D)
                            act.wait_ge(*filled(g, f"fv{j}"))
                            if j == 0:
                                act.wait_ge(*taken(g, "q3"))
                            act.activation(PB[:, js], ps(f"fv{j}")[:, 0:D], ACT.Abs, scale=IWS).then_inc(fa_step, 1)
                            act.activation(EB[:, js], ps(f"fv{j}")[:, D:2 * D], ACT.Tanh, scale=0.5 * IWS).then_inc(ve_ready, 1)
                        act.wait_ge(fa_step, (G + 1) * g + G)
                        act.activation(PB, PB, ACT.Exp, scale=-1.0).then_inc(fa_step, 1)
                        act.wait_ge(fa_step, (G + 1) * g + G + 1)
                        act.activation(PB, PB, ACT.Ln, bias=1.0).then_inc(fl_ready, 1)
                        act.wait_ge(g_ready, g + 1)
                        act.activation(cut(7), cut(6), ACT.Exp, scale=1.0 / GATE_NORM).then_inc(es_ready, 1)
                    elif name == "decay":
                        act.wait_ge(*taken(g, "D0"))
                        act.wait_ge(*taken(g, "D1"))
                        act.activation(PB, EB, ACT.Exp, scale=-1.0 / GATE_NORM).then_inc(ei_ready, 1)
                        act.activation(EB, EB, ACT.Exp, scale=1.0 / GATE_NORM).then_inc(e_ready, 1)
                    elif name == "st":
                        for k in range(KB):
                            take(g, f"st{k}", SPT[:, k])
                    elif name == "gz":
                        act.wait_ge(zs_ready, g + 1)
                        act.activation(PB, PB, ACT.Exp).then_inc(ze_ready, 1)
                    elif name == "gp":
                        take(g, "gp0", PPT[:, 0])
                    elif name == "o":
                        act.wait_ge(*taken(g, "o0"))
                        act.wait_ge(*taken(g, "o1"))
                        act.activation(EB, cut(6), ACT.Tanh, scale=0.5).then_inc(oe_ready, 1)
                        act.wait_ge(os_ready, g + 1)
                        for j in range(G):
                            i = act.activation(PB[:, j * D:(j + 1) * D], U[:, j], ACT.Square, scale=0.5, accum_out=ssq[:, j:j + 1])
                        i.then_inc(sq_ready, 1)
                    elif name == "ot":
                        for k in range(KB):
                            take_pair(g, f"ot{k}", HTF[:, k], HTP[:, 0, k])
                    elif name == "mx":
                        for k in range(KB):
                            take_pair(g, f"mx{k}", XF[:, k], XP[:, 0, k])

                def high(g, c):
                    e, m = divmod(c, 2)
                    act.wait_ge(*taken(g, f"u{c}"))
                    if e >= 2:
                        act.wait_ge(*filled(g, f"e{e - 2}.1"))
                    act.activation(MP[:, e % 2, 0, m], MA[:, c % 2], ACT.Copy).then_inc(mhi_ready, 1)

                def do_m(g, name, c):
                    if name == "router":
                        act.wait_ge(rx_ready, g + 1)
                        act.activation(ex[:], ex[:], ACT.Exp).then_inc(re_ready, 1)
                    elif name == "gu":
                        act.wait_ge(*filled(g, f"g{c}"))
                        act.activation(ME[:, c % 2], ps(f"g{c}")[:], ACT.Tanh, scale=0.5 * IWS).then_inc(me_ready, 1)
                        if c:
                            high(g, c - 1)
                    elif name == "tail":
                        high(g, NC - 1)

                run(act, do_a, do_m)

            @block.gpsimd
            def _(pool):
                def rows(l, n):
                    return gb[:, l, n:n + 1].to_broadcast([P, G, D])

                def gather():
                    for j in range(G):
                        pool.indirect_dma_start(EMB[:, j], None, emb, bass.IndirectOffsetOnAxis(cur[:, j:j + 1], 0)).then_inc(emb_ready, 16)

                def affine(g, k, l, dst, n, done):
                    pool.wait_ge(x_ready, 6 * g + k + 1)
                    pool.tensor_tensor(dst, Xn, rows(l, n), ALU.mult).then_inc(pool_a, 1)
                    pool.wait_ge(pool_a, 2 * NL * g + k + 1)
                    pool.tensor_tensor(dst, dst, rows(l, n + 1), ALU.add).then_inc(done, 1)

                def do_a(g, name, l=None):
                    if name == "z":
                        affine(g, XR[f"z{l}"], l, HR, 0, hr_ready)
                    elif name == "dn":
                        affine(g, XR[f"dn{l}"], l, H, 2, h_affine)
                    elif name == "o":
                        pool.wait_ge(*filled(g, "o1"))
                        pool.sem_inc(idle, 1)
                        pool.wait_ge(cur_ready, g + 2)
                        pool.sem_inc(idle, 1)
                        gather()

                def low(g, c):
                    e, m = divmod(c, 2)
                    pool.wait_ge(mhi_ready, NC * g + c + 1)
                    pool.tensor_tensor(MP[:, e % 2, 1, m], MA[:, c % 2], MP[:, e % 2, 0, m], ALU.subtract).then_inc(mlo_ready, 1)

                def do_m(g, name, c):
                    if name == "router":
                        pool.wait_ge(x_ready, 6 * g + 6)
                        pool.sem_inc(idle, 1)
                        pool.wait_ge(acc_free, g + 1)
                        pool.sem_inc(idle, 1)
                        pool.tensor_copy(ACC, H).then_inc(acc_ready, 1)
                    elif name == "gu" and c:
                        low(g, c - 1)
                    elif name == "tail":
                        low(g, NC - 1)

                pool.wait_ge(cur_ready, 1)
                gather()
                run(pool, do_a, do_m)

            @block.vector
            def _(dve):
                count = {"a": 0, "m": 0}
                PER_A, PER_M = A_LINKS, M_LINKS

                def link_a(g, ins):
                    count["a"] += 1
                    ins.then_inc(dve_a, 1)
                    dve.wait_ge(dve_a, PER_A * g + count["a"])

                def link_m(g, ins):
                    count["m"] += 1
                    ins.then_inc(dve_m, 1)
                    dve.wait_ge(dve_m, PER_M * g + count["m"])

                def inverse_root(g, last=1.0):
                    link_a(g, dve.tensor_scalar(newt[:].bitcast(I32), vare[:].bitcast(I32), 1, None,
                                                ALU.logical_shift_right))
                    link_a(g, dve.tensor_scalar(rstd[:].bitcast(I32), newt[:].bitcast(I32), -1.0, float(0x5f3759df),
                                                ALU.mult, ALU.add))
                    for _ in range(3):
                        link_a(g, dve.scalar_tensor_tensor(newt[:], rstd[:], -0.5, rstd[:], ALU.mult, ALU.mult))
                        link_a(g, dve.tensor_tensor(newt[:], newt[:], vare[:], ALU.mult))
                        link_a(g, dve.scalar_tensor_tensor(rstd[:], newt[:], 1.5, rstd[:], ALU.add, ALU.mult))
                    if last != 1.0:
                        link_a(g, dve.tensor_scalar(rstd[:], rstd[:], last, None, ALU.mult))

                def norm(g, src, mul=1.0, add=EPS):
                    for j in range(G):
                        i = dve.bn_stats(stat[:, j], src[:, j])
                    link_a(g, i)
                    dve.sem_inc(idle, 1)
                    for j in range(G):
                        i = dve.bn_aggr(mv[:, j], stat[:, j])
                    link_a(g, i)
                    link_a(g, dve.tensor_scalar(vare[:], mv[:, :, 1], mul, add, ALU.mult, ALU.add))
                    inverse_root(g)
                    for j in range(G):
                        i = dve.tensor_scalar(Xn[:, j], src[:, j], mv[:, j, 0:1], rstd[:, j:j + 1], ALU.subtract, ALU.mult)
                    i.then_inc(x_ready, 1)

                def lows(g, stem, F, Pr, done):
                    for k in range(KB):
                        dve.wait_ge(*taken(g, stem(k)))
                        dve.tensor_tensor(Pr[:, 1, k], F[:, k], Pr[:, 0, k], ALU.subtract).then_inc(done, 1)

                def half(ap, jj):
                    return ap[:, jj * GT:(jj + 1) * GT]


                def do_a(g, name, l=None):
                    if name == "embed":
                        if not isinstance(g, int):
                            dve.wait_ge(acc_ready, g)
                        dve.wait_ge(emb_ready, 16 * G * g + 16 * G)
                        dve.tensor_tensor(H, EMB, posb[:, None, :].to_broadcast([P, G, D]), ALU.add).then_inc(h_ready, 1)
                        dve.tensor_copy(cur[:], idx[:, bass.ds(G * g + G, G)]).then_inc(cur_ready, 1)
                    elif name == "x":
                        lows(g, lambda k: f"x{k}.{l}", HTF, HTP, ht_ready)
                    elif name == "tv":
                        dve.wait_ge(*filled(g, f"t1.{l}"))
                        dve.tensor_scalar(TT[:, 1], ps(f"t1.{l}")[:], IWS, None, ALU.mult).then_inc(free[BANK[f"t1.{l}"]], 1)
                        dve.wait_ge(*filled(g, f"v1.{l}"))
                        dve.tensor_scalar(flat(VO[:, 2:4]), ps(f"v1.{l}")[:], IWS, None, ALU.mult).then_inc(free[BANK[f"v1.{l}"]], 1)
                    elif name == "sc":
                        n = f"sc.{l}"
                        dve.wait_ge(*filled(g, n))
                        dve.tensor_tensor(SM, ps(n)[:].rearrange("p (j s) -> p j s", j=G),
                                          causal[:, None, :].to_broadcast([P, G, P]), ALU.add).then_inc(free[BANK[n]], 1)
                        dve.wait_ge(*taken(g, n))
                        link_a(g, dve.tensor_reduce(smax[:], SM, AX, ALU.max))
                        dve.tensor_scalar(nbias[:], smax[:], -1.0 / D ** 0.5, None, ALU.mult).then_inc(nb_ready, 1)
                        dve.wait_ge(p_ready, NL * g + l + 1)
                        link_a(g, dve.reciprocal(rinv[:], rsum[:]))
                    elif name == "pt":
                        n = f"pt.{l}"
                        dve.wait_ge(*filled(g, n))
                        dve.tensor_copy(flat(PT), ps(n)[:]).then_inc(free[BANK[n]], 1)
                    elif name == "z":
                        if l == 0:
                            dve.wait_ge(h_ready, g + 1)
                        else:
                            dve.wait_ge(h_affine, NL * g + 1)
                        for jj in range(G // 2):
                            n = f"z{jj}.{l}"
                            dve.wait_ge(*filled(g, n))
                            for j2 in range(2):
                                j = 2 * jj + j2
                                i = dve.scalar_tensor_tensor(U[:, j], ps(n)[:, j2 * D:(j2 + 1) * D], rinv[:, j:j + 1],
                                                             H[:, j], ALU.mult, ALU.add)
                            i.then_inc(free[BANK[n]], 1)
                        dve.wait_ge(*taken(g, f"z0.{l}"))
                        dve.wait_ge(*taken(g, f"z1.{l}"))
                        norm(g, U)
                    elif name == "y":
                        lows(g, lambda k: f"y{k}.{l}", HTF, HTP, ht_ready)
                    elif name == "up":
                        for m in range(FB):
                            dve.wait_ge(*taken(g, f"up{m}.{l}"))
                            dve.tensor_tensor(AP[:, 1, m], half(EB, m % 2), AP[:, 0, m], ALU.subtract).then_inc(a_ready, 1)
                    elif name == "dn":
                        dve.wait_ge(hr_ready, NL * g + l + 1)
                        for jj in range(G // 2):
                            n = f"dn{jj}.{l}"
                            dve.wait_ge(*filled(g, n))
                            dve.scalar_tensor_tensor(flat(U[:, 2 * jj:2 * jj + 2]), ps(n)[:], IWS,
                                                     flat(HR[:, 2 * jj:2 * jj + 2]), ALU.mult, ALU.add).then_inc(free[BANK[n]], 1)
                        dve.wait_ge(*taken(g, f"dn0.{l}"))
                        dve.wait_ge(*taken(g, f"dn1.{l}"))
                        norm(g, U)
                    elif name == "gx":
                        dve.wait_ge(h_affine, NL * g + NL)
                        norm(g, H, 1.0 + EPS, EPS * EPS)
                        lows(g, lambda k: f"gx{k}", HTF, HTP, ht_ready)
                    elif name == "qk":
                        for n in range(4):
                            dve.wait_ge(qe_ready, 4 * g + n + 1)
                            dst = (QT, KT)[n // 2][:, n % 2]
                            dve.scalar_tensor_tensor(dst, half(EB, n % 2), 1.0, ps(f"q{n}")[:], ALU.add,
                                                     ALU.mult).then_inc(free[BANK[f"q{n}"]], 1)
                    elif name == "fv":
                        for j in range(G):
                            n = f"fv{j}"
                            dve.wait_ge(ve_ready, G * g + j + 1)
                            i = dve.tensor_scalar(U[:, j], ps(n)[:, 0:D], 0.0, IWS, ALU.min, ALU.mult)
                            if j == G - 1:
                                i.then_inc(mn_ready, 1)
                            dve.scalar_tensor_tensor(VB[:, j], EB[:, j * D:(j + 1) * D], 1.0, ps(n)[:, D:2 * D], ALU.add,
                                                     ALU.mult).then_inc(free[BANK[n]], 1)
                        dve.wait_ge(mn_ready, g + 1)
                        dve.wait_ge(fl_ready, g + 1)
                        dve.tensor_tensor(cut(6), cut(6), PB, ALU.subtract).then_inc(g_ready, 1)
                    elif name == "decay":
                        for jj in range(G // 2):
                            n = f"D{jj}"
                            dve.wait_ge(*filled(g, n))
                            dve.tensor_scalar(half(EB, jj), ps(n)[:], EXP_CLAMP * GATE_NORM, -EXP_CLAMP * GATE_NORM,
                                              ALU.min, ALU.max).then_inc(free[BANK[n]], 1)
                        dve.wait_ge(es_ready, g + 1)
                        link_a(g, dve.tensor_scalar(cut(7), cut(7), -1.0, 1.0, ALU.mult, ALU.add))
                        dve.wait_ge(ei_ready, g + 1)
                        dve.tensor_tensor(cut(7), cut(7), PB, ALU.mult).then_inc(sp_ready, 1)
                    elif name in ("scores", "vscores"):
                        stem, dst, f = ("A", AT, (0.5 * IWS) ** 2) if name == "scores" else ("B", BT, 1.0)
                        for jj in range(G // 2):
                            for par in range(2):
                                n = f"{stem}{jj}{par}"
                                dve.wait_ge(*filled(g, n))
                                dve.scalar_tensor_tensor(dst[:, jj, par], ps(n)[:].rearrange("p (c t) -> p c t", c=4), f,
                                                         upper[:, None, :].to_broadcast([P, 4, P]), ALU.mult,
                                                         ALU.mult).then_inc(free[BANK[n]], 1)
                    elif name == "gz":
                        dve.wait_ge(e_ready, g + 1)
                        for jj in range(G // 2):
                            n = f"gz{jj}"
                            dve.wait_ge(*filled(g, n))
                            dve.tensor_tensor(half(PB, jj), ps(n)[:], half(EB, jj), ALU.mult).then_inc(free[BANK[n]], 1)
                        z3 = PB.rearrange("p (c m) -> p c m", c=G * HEADS)
                        dve.wait_ge(*taken(g, "gz0"))
                        dve.wait_ge(*taken(g, "gz1"))
                        link_a(g, dve.tensor_reduce(zmax[:], z3, AX, ALU.max))
                        dve.tensor_tensor(z3, z3, zmax[:, :, None].to_broadcast([P, G * HEADS, DK]),
                                          ALU.subtract).then_inc(zs_ready, 1)
                        dve.wait_ge(ze_ready, g + 1)
                        link_a(g, dve.tensor_reduce(zsum[:], z3, AX, ALU.add))
                        dve.tensor_tensor(PB, PB, EB, ALU.mult).then_inc(pp_ready, 1)
                        link_a(g, dve.reciprocal(zsum[:], zsum[:]))
                        link_a(g, dve.tensor_scalar(zsum[:], zsum[:], 0.5 * IWS, None, ALU.mult))
                    elif name == "gp":
                        dve.wait_ge(*filled(g, "gp1"))
                        dve.tensor_copy(PPT[:, 1], ps("gp1")[:]).then_inc(free[BANK["gp1"]], 1)
                    elif name == "o":
                        for jj in range(G // 2):
                            n = f"o{jj}"
                            dve.wait_ge(*filled(g, n))
                            zi = zsum[:, jj * 2 * HEADS:(jj + 1) * 2 * HEADS, None].to_broadcast([P, 2 * HEADS, DK])
                            dve.tensor_tensor(flat(U[:, 2 * jj:2 * jj + 2]).rearrange("p (c v) -> p c v", c=2 * HEADS),
                                              ps(n)[:].rearrange("p (c v) -> p c v", c=2 * HEADS), zi,
                                              ALU.mult).then_inc(free[BANK[n]], 1)
                        dve.wait_ge(oe_ready, g + 1)
                        dve.scalar_tensor_tensor(cut(6), EB, 1.0, cut(6), ALU.add, ALU.mult).then_inc(os_ready, 1)
                        dve.wait_ge(sq_ready, g + 1)
                        link_a(g, dve.tensor_scalar(vare[:], ssq[:], 1.0 / D, EPS, ALU.mult, ALU.add))
                        inverse_root(g, 0.5 * IWS)
                    elif name == "ot":
                        lows(g, lambda k: f"ot{k}", HTF, HTP, ht_ready)
                    elif name == "w":
                        for jj in range(G // 2):
                            n = f"w{jj}"
                            dve.wait_ge(*filled(g, n))
                            for j2 in range(2):
                                j = 2 * jj + j2
                                i = dve.scalar_tensor_tensor(H[:, j], ps(n)[:, j2 * D:(j2 + 1) * D], rstd[:, j:j + 1],
                                                             H[:, j], ALU.mult, ALU.add)
                            i.then_inc(free[BANK[n]], 1)
                        dve.wait_ge(*taken(g, "w0"))
                        dve.wait_ge(*taken(g, "w1"))
                        norm(g, H)
                    elif name == "mx":
                        lows(g, lambda k: f"mx{k}", XF, XP, xm_ready)
                        assert count["a"] == A_LINKS, count
                        count["a"] = 0

                def do_m(g, name, c):
                    if name == "router":
                        dve.wait_ge(*filled(g, "rl"))
                        dve.tensor_copy(lg[:], ps("rl")[:, 0:G * NE].rearrange("p (j e) -> p j e", j=G)).then_inc(free[BANK["rl"]], 1)
                        dve.wait_ge(*taken(g, "rl"))
                        dve.sem_inc(idle, 1)
                        for j in range(G):
                            i = dve.max(top[:, j], lg[:, j])
                        link_m(g, i)
                        dve.tensor_tensor(ex[:], lg[:], top[:, :, 0:1].to_broadcast([P, G, NE]), ALU.subtract).then_inc(rx_ready, 1)
                        dve.tensor_tensor(keep[:], lg[:], top[:, :, 1:2].to_broadcast([P, G, NE]), ALU.is_ge)
                        dve.wait_ge(re_ready, g + 1)
                        link_m(g, dve.tensor_reduce(esum[:], ex[:], AX, ALU.add))
                        link_m(g, dve.reciprocal(esum[:], esum[:]))
                        link_m(g, dve.tensor_tensor(comb[:], ex[:], keep[:], ALU.mult))
                        link_m(g, dve.scalar_tensor_tensor(comb[:], comb[:], IWS, esum[:, :, None].to_broadcast([P, G, NE]),
                                                           ALU.mult, ALU.mult))
                    elif name == "gu":
                        dve.wait_ge(me_ready, NC * g + c + 1)
                        if c >= 2:
                            dve.wait_ge(mlo_ready, NC * g + c - 1)
                        dve.scalar_tensor_tensor(MA[:, c % 2], ME[:, c % 2], 1.0, ps(f"g{c}")[:], ALU.add,
                                                 ALU.mult).then_inc(free[BANK[f"g{c}"]], 1)
                        dve.wait_ge(*filled(g, f"u{c}"))
                        dve.wait_ge(*taken(g, f"g{c}"))
                        dve.scalar_tensor_tensor(MA[:, c % 2], ps(f"u{c}")[:], 0.5 * IWS * IWS, MA[:, c % 2], ALU.mult,
                                                 ALU.mult).then_inc(free[BANK[f"u{c}"]], 1)
                    elif name == "down":
                        e = c
                        if e == 0:
                            dve.wait_ge(acc_ready, g + 1)
                        else:
                            dve.wait_ge(*taken(g, f"e{e - 1}.0"))
                            dve.wait_ge(*taken(g, f"e{e - 1}.1"))
                        for jj in range(G // 2):
                            n = f"e{e}.{jj}"
                            dve.wait_ge(*filled(g, n))
                            if e < NE:
                                for j2 in range(2):
                                    j = 2 * jj + j2
                                    i = dve.scalar_tensor_tensor(ACC[:, j], ps(n)[:, j2 * D:(j2 + 1) * D],
                                                                 comb[:, j, e:e + 1], ACC[:, j], ALU.mult, ALU.add)
                            else:
                                half_acc = flat(ACC[:, 2 * jj:2 * jj + 2])
                                i = dve.scalar_tensor_tensor(half_acc, ps(n)[:], IWS, half_acc, ALU.mult, ALU.add)
                            i.then_inc(free[BANK[n]], 1)
                        if e == NX - 1:
                            dve.wait_ge(*taken(g, f"e{e}.0"))
                            dve.wait_ge(*taken(g, f"e{e}.1"))
                            dve.sem_inc(acc_done, 1)
                            assert count["m"] == M_LINKS, count
                            count["m"] = 0

                dve.tensor_copy(cur[:], idx[:, 0:G]).then_inc(cur_ready, 1)
                run(dve, do_a, do_m)


_INS = ['x', 'L0_tok_emb', 'L0_tok_pos', 'L0_tok_wq', 'L0_tok_wk', 'L0_tok_wv', 'L0_tok_wo', 'L0_tok_wup', 'L0_tok_bup',
        'L0_tok_wdown', 'L0_tok_bdown', 'L0_tok_ga', 'L0_tok_ba', 'L0_tok_gm', 'L0_tok_bm', 'L0_attn_norm_weight',
        'L0_attn_w_q', 'L0_attn_w_k', 'L0_attn_w_v', 'L0_attn_w_f', 'L0_attn_gnorm_weight', 'L0_attn_w_o',
        'L0_ffn_router_w', 'L0_ffn_gate_w', 'L0_ffn_up_w', 'L0_ffn_down_w', 'L0_ffn_shared_gate_w',
        'L0_ffn_shared_up_w', 'L0_ffn_shared_down_w']


def kernel(**inputs):
    import numpy as _np
    import concourse.bacc as _bacc
    from concourse import mybir as _mybir
    from concourse.bass_utils import run_bass_kernel_spmd as _run

    nc = _bacc.Bacc("TRN2", target_bir_lowering=False, num_devices=1)
    arrays, args = {}, []
    for name in _INS:
        a = _np.ascontiguousarray(inputs[name])
        arrays[f"in_{name}"] = a
        args.append(nc.dram_tensor(f"in_{name}", a.shape, _mybir.dt.from_np(a.dtype), kind="ExternalInput").ap())
    seqs, steps = inputs["x"].shape
    width = inputs["L0_tok_emb"].shape[1]
    args.append(nc.dram_tensor("out_0", (seqs, steps, width), _mybir.dt.float32, kind="ExternalOutput").ap())
    build(nc, *args)
    r = _run(nc, [arrays], core_ids=[0])
    return r.results[0]["out_0"]
```

```python
from contextlib import ExitStack

import concourse.bass as bass
from concourse import mybir

F32 = mybir.dt.float32
F16 = mybir.dt.float16
I32 = mybir.dt.int32
ALU = mybir.AluOpType
ACT = mybir.ActivationFunctionType
AX = mybir.AxisListType.X

P = 128
G = 2
GT = G * P
EPS = 1e-5
WS = 64.0
IWS = 1.0 / WS
NEG = -1e30
GATE_NORM = 16.0
EXP_CLAMP = 80.0

LINKS = {"a": 29, "b": 29, "s": 46, "m": 5}



def layer_rows(l):
    rows = [("embed", (l,), [("D", 0.7)], []), ("gather", (l,), [("G", 2.1)], None)] if l == 0 else []
    rows += [("x", (l,), [("P", 0.4), ("A", 1.0), ("D", 0.6)], ["embed"] if l == 0 else []),
             ("t", (l,), [("P", 1.3), ("A", 0.5)], None),
             ("v", (l,), [("P", 1.3), ("D", 0.6)], ["x"]),
             ("sc", (l,), [("P", 0.9), ("D", 1.3)], ["t"]),
             ("sexp", (l,), [("A", 0.6)], None),
             ("pt", (l,), [("P", 0.2), ("D", 0.5)], None),
             ("z", (l,), [("P", 0.9), ("D", 0.8)], ["pt", "v"]),
             ("mnorm", (l,), [("D", 3.9)], None),
             ("mid", (l,), [("G", 2.5)], None),
             ("hr", (l,), [("G", 1.3)], None),
             ("y", (l,), [("P", 0.4), ("A", 1.0), ("D", 0.6)], ["mid"])]
    rows += [("up", (l, q), [("P", 1.3), ("A", 1.5), ("D", 0.6)],
              [f"up{q - 2}"] if q >= 2 else ["y", "b:dn"] if l == 0 else ["y"]) for q in range(4)]
    return rows + [("dn", (l,), [("P", 5.2), ("D", 0.6)], None),
                   ("onorm", (l,), [("D", 3.9)], None),
                   ("out", (l,), [("G", 2.5)], ["onorm", "b:y", "b:hr"] if l == 0 else ["onorm", "s:res"])]


S_ROWS = [("norm", (), [("D", 4.5)], ["m:mx"]),
          ("gx", (), [("P", 0.4), ("A", 1.0), ("D", 0.6)], None),
          ("qk", (), [("P", 2.6), ("A", 1.0), ("D", 1.2)], None),
          ("fv", (), [("P", 2.6), ("A", 1.6), ("D", 1.6)], ["qk", "m:acc"]),
          ("lnf", (), [("A", 3.6)], None),
          ("scores", (), [("P", 1.7), ("D", 1.2)], ["fv"]),
          ("g", (), [("D", 0.6)], ["lnf", "fv"]),
          ("gexp", (), [("A", 0.5)], None),
          ("decay", (), [("P", 0.9), ("D", 0.6)], ["g", "scores"]),
          ("dexp", (), [("A", 1.0)], None),
          ("slots", (), [("D", 1.3)], None),
          ("st", (), [("P", 0.4), ("A", 0.5)], None),
          ("gz", (), [("P", 1.7), ("D", 2.0)], None),
          ("zexp", (), [("A", 0.5)], None),
          ("pp", (), [("D", 0.6)], None),
          ("gp", (), [("P", 0.4), ("A", 0.5)], None),
          ("vscores", (), [("P", 1.7), ("D", 1.2)], None),
          ("zsum", (), [("D", 1.2)], ["zexp"]),
          ("o", (), [("P", 1.7), ("D", 0.6)], ["vscores", "zsum"]),
          ("otanh", (), [("A", 0.5)], None),
          ("osw", (), [("D", 0.6)], None),
          ("ssq", (), [("A", 0.8)], None),
          ("ot", (), [("P", 0.4), ("A", 1.0), ("D", 0.6)], ["osw"]),
          ("root", (), [("D", 2.2)], ["ssq"]),
          ("w", (), [("P", 1.3)], ["ot"]),
          ("res", (), [("D", 0.8)], ["w", "root"]),
          ("fnorm", (), [("D", 4.3)], None)]


def moe_rows(start, end, NX):
    rows = []
    if start == 0:
        rows = [("mx", (), [("P", 0.4), ("A", 1.0), ("D", 0.6)], [f"n:down{NX - 1}"]),
                ("acc", (), [("G", 1.9)], [f"n:down{NX - 1}"]),
                ("router", (), [("P", 0.3), ("D", 0.6)], ["mx"]),
                ("rexp", (), [("A", 0.2)], None),
                ("gates", (), [("D", 0.7)], None)]
    e_down = start - 1 if start else 0
    for e in range(start, end):
        rows.append(("gu", (e,), [("P", 2.6), ("A", 0.5), ("D", 1.2)],
                     ["router"] if e == 0 else ([f"gu{e - 1}"] if e > start else []) +
                     ([f"down{e - 2}"] if e - 2 >= max(start - 1, 0) else [])))
        rows.append(("split", (e,), [("A", 0.5), ("G", 1.2)], None))
        if e:
            rows.append(("down", (e_down,), [("P", 1.3), ("D", 0.8)],
                         ([f"split{e_down}"] if e_down >= start else []) + [f"gu{e}"] + (["gates", "acc"] if start == 0 else [])))
            e_down += 1
    if end == NX:
        rows.append(("down", (NX - 1,), [("P", 1.3), ("D", 0.8)], [f"split{NX - 1}"]))
    return rows


HOP = 0.15


def key_of(name, args, part):
    return name + (str(args[-1]) if name in ("up", "gu", "split", "down") else "")


def plan(**parts):
    visits = {}
    rest, queue = {}, {}
    info = {}
    for part, rows in parts.items():
        above = None
        for name, args, steps, after in rows:
            key = key_of(name, args, part)
            for n, (eng, cost) in enumerate(steps):
                if n:
                    needs = [(part, key, n - 1)]
                else:
                    needs = []
                    for a in ([above] if after is None else after):
                        p, k = a.split(":") if ":" in a else (part, a)
                        if p in parts:
                            needs.append((p, k, None))
                visits[part, key, n] = [eng, cost, needs]
                info[part, key, n] = (part, name, args, eng)
                queue.setdefault((part, eng), []).append((part, key, n))
            above = key
    last = {}
    for part, key, n in visits:
        last[part, key] = max(n, last.get((part, key), 0))
    for v in visits.values():
        v[2] = [(p, k, last[p, k] if n is None else n) for p, k, n in v[2]]
    follow = {me: [] for me in visits}
    for me, (_, _, needs) in visits.items():
        for need in needs:
            follow[need].append(me)

    def way(me):
        if me not in rest:
            rest[me] = visits[me][1] + max((way(f) + HOP for f in follow[me]), default=0.0)
        return rest[me]

    for me in visits:
        way(me)
    free, end, order = {e: 0.0 for e in "PADG"}, {}, []
    while len(order) < len(visits):
        can = []
        for (part, eng), q in queue.items():
            if q and all(n in end for n in visits[q[0]][2]):
                start = max([free[eng]] + [end[n] + HOP for n in visits[q[0]][2]])
                can.append((start, -rest[q[0]], part, eng))
        soon = min(c[0] for c in can)
        _, start, part, eng = min((c[1], c[0], c[2], c[3]) for c in can if c[0] <= soon + 0.2)
        me = queue[part, eng].pop(0)
        end[me] = free[eng] = start + visits[me][1]
        order.append(info[me])
    return order


LAYER_USES = ["x", "t", "v", "sc", "pt", "z", "y", "up0", "up1", "up2", "up3", "dn"]
S_USES = ["gx", "q", "k", "fv0", "fv1", "A0", "A1", "D", "st", "gz", "gp", "B0", "B1", "o", "ot", "w"]


def m_uses(E):
    out = ["mx", "rl"]
    for name, args, _, _ in moe_rows(0, E, E):
        if name == "gu":
            out += [f"g{args[0]}", f"u{args[0]}"]
        elif name == "down":
            out.append(f"e{args[0]}")
    return out


def build(nc, x, emb, pos, wq, wk, wv, wo, wup, bup, wdown, bdown, ga, ba, gm, bm,
          norm_w, a_q, a_k, a_v, a_f, gnorm_w, a_o, router_w, gate_w, up_w, down_w, sg_w, su_w, sd_w, out):
    SEQS, T = x.shape
    V, D = emb.shape
    NL = wq.shape[0]
    F = wup.shape[2]
    NE = gate_w.shape[0]
    HEADS, DK = 4, 64
    KB = D // P
    FB = F // P
    NG = SEQS // G
    NX = NE + sg_w.shape[1] // D
    assert T == P and NL == 2 and KB == 2 and D == HEADS * DK and gate_w.shape[2] == D

    BANK, ORD, PER = {}, {}, [0] * 8
    for base, uses in ((0, [f"{n}.0" for n in LAYER_USES]), (2, [f"{n}.1" for n in LAYER_USES]), (4, S_USES),
                       (6, m_uses(NX))):
        for n, name in enumerate(uses):
            b = base + n % 2
            BANK[name], ORD[name] = b, PER[b]
            PER[b] += 1

    with ExitStack() as ctx:
        def sb(name, shape, dt=F32):
            return ctx.enter_context(nc.sbuf_tensor(name, shape, dt))

        def sem(name):
            return ctx.enter_context(nc.semaphore(name))

        bank = [ctx.enter_context(nc.psum_tensor(f"bank{b}", [P, 512], F32)) for b in range(8)]

        Wm = sb("Wm", [P, 2, NL, KB, D], F16)
        Wvo = sb("Wvo", [P, 2, NL, KB, D], F16)
        Wup = sb("Wup", [P, 2, NL, KB, F], F16)
        Wdn = sb("Wdn", [P, 2, NL, FB, D], F16)
        Wqk = sb("Wqk", [P, 2, 2, KB, D], F16)
        Wfv = sb("Wfv", [P, 2, KB, 2 * D], F16)
        Wao = sb("Wao", [P, 2, KB, D], F16)
        Wg = sb("Wg", [P, 2, NX, KB, D], F16)
        Wu = sb("Wu", [P, 2, NX, KB, D], F16)
        Wd = sb("Wd", [P, 2, NX, KB, D], F16)
        rw = sb("rw", [P, KB, NE])

        ident = sb("ident", [P, P])
        causal = sb("causal", [P, P])
        upper = sb("upper", [P, P])
        tri = sb("tri", [P, P])
        posb = sb("posb", [P, D])
        gb = sb("gb", [P, NL, 4, D])
        bdn = sb("bdn", [P, NL, D])
        bupc = sb("bupc", [P, NL, FB])
        nwc = sb("nwc", [P, 2, KB])
        idx = sb("idx", [P, SEQS + G], I32)
        cur = sb("cur", [P, G], I32)
        nws = sb("nws", [P, 2, KB])

        smax, nbias, rsum, rinv = ([sb(f"{n}{l}", [P, G]) for l in range(NL)] for n in ("smax", "nbias", "rsum", "rinv"))
        NORM = {p: [sb(f"{n}_{p}", [P, G, *d]) for n, d in (("stat", (6,)), ("mv", (2,)), ("vare", ()), ("rstd", ()), ("newt", ()))]
                for p in "abs"}
        zmax = sb("zmax", [P, G * HEADS])
        zsum = sb("zsum", [P, G * HEADS])
        ssq = sb("ssq", [P, G])
        lg = sb("lg", [P, G, NE])
        top = sb("top", [P, G, 8])
        ex = sb("ex", [P, G, NE])
        keep = sb("keep", [P, G, NE])
        esum = sb("esum", [P, G])
        comb = sb("comb", [P, G, NE])

        SLOT = 512
        arena = sb("arena", [P, 41 * SLOT])
        taken_slots = [0]

        def cut(n=1):
            a = taken_slots[0]
            taken_slots[0] += n
            return arena[:, a * SLOT:(a + n) * SLOT]

        def tok(ap):
            return ap.rearrange("p (j d) -> p j d", j=G)

        def feat(ap):
            return ap.rearrange("p (k t) -> p k t", k=KB)

        def pair(ap, n):
            return ap.bitcast(F16).rearrange("p (a k t) -> p a k t", a=2, k=n)

        EMB = tok(cut())
        H, U, VO = ([tok(cut()) for l in range(NL)] for _ in range(3))
        HTF, TT = ([feat(cut()) for l in range(NL)] for _ in range(2))
        HR = [tok(t.rearrange("p k t -> p (k t)")) for t in TT]
        HTP = [pair(cut(), KB) for l in range(NL)]
        sp_ = [cut() for l in range(NL)]
        SM = [a[:, 0:G * P].rearrange("p (j s) -> p j s", j=G) for a in sp_]
        PT = [a[:, G * P:2 * G * P].rearrange("p (j s) -> p j s", j=G) for a in sp_]
        RT = cut(2).rearrange("p (b m t) -> p b m t", b=2, m=2)
        AP = pair(cut(4), FB)
        HS, US, XS, VB, EB, PB = (tok(cut()) for _ in range(6))
        HO = US
        ZF, QT, KT = (feat(cut()) for _ in range(3))
        SPT = ZF
        PPT = QT
        ZP = pair(cut(), KB)
        AT = cut(2).rearrange("p (a c t) -> p a c t", a=2, c=4)
        BT = AT
        XP = pair(cut(), KB)
        ACC = tok(cut())
        ME = cut(2).rearrange("p (b t) -> p b t", b=2)
        MA = cut(2).rearrange("p (b t) -> p b t", b=2)
        XF = feat(MA[:, 0])
        MP = cut(2).rearrange("p (b t) -> p b t", b=2)
        MP = [pair(MP[:, b], 2) for b in range(2)]

        s_load = [sem(f"load{n}") for n in range(16)]
        s_const = sem("const_made")
        s_step = sem("setup_dve_step")
        s_ids = sem("ids_as_floats")
        s_nws = sem("norm_weights_scaled")
        s_idx = sem("ids_transposed")
        s_sfull = sem("setup_bank_full")
        s_shi = sem("setup_hi_made")
        s_slo = sem("setup_lo_made")
        s_rawt = sem("raw_transposed")
        full = [sem(f"bank_full{b}") for b in range(8)]
        free = [sem(f"bank_free{b}") for b in range(8)]
        cur_ready = sem("row_numbers_ready")
        emb_ready = sem("rows_gathered")
        h_ready = sem("h_embedded")
        ht_ready, nb_ready, p_ready, x_ready, mid_ready, hr_ready, a_ready, out_ready, pool_step = (
            [sem(f"{n}{l}") for l in range(NL)]
            for n in ("layer_operand_ready", "nbias_ready", "probs_ready", "layer_normed", "mid_affine_ready",
                      "residual_ready", "hidden_ready", "layer_out_ready", "pool_step"))
        xs_ready = sem("slot_normed")
        zt_ready = sem("slot_operand_ready")
        qe_ready = sem("q_tanh_ready")
        fa_step = sem("f_abs_exp_step")
        ve_ready = sem("v_tanh_ready")
        mn_ready = sem("f_min_ready")
        fl_ready = sem("f_log_ready")
        g_ready = sem("gate_ready")
        es_ready = sem("gate_exp_ready")
        ei_ready = sem("decay_inv_exp_ready")
        e_ready = sem("decay_exp_ready")
        sp_ready = sem("slots_ready")
        zs_ready = sem("z_shifted")
        ze_ready = sem("z_exp_ready")
        pp_ready = sem("slot_probs_ready")
        oe_ready = sem("o_tanh_ready")
        os_ready = sem("o_swished")
        sq_ready = sem("squares_summed")
        xm_ready = sem("moe_x_ready")
        acc_ready = sem("acc_started")
        rx_ready = sem("router_shifted")
        re_ready = sem("router_exp_ready")
        me_ready = sem("moe_tanh_ready")
        mhi_ready = sem("moe_hi_ready")
        mlo_ready = sem("moe_hidden_ready")
        acc_done = sem("acc_done")
        acc_free = sem("acc_free")
        out_done = sem("out_written")
        dve_step = {p: sem(f"dve_step_{p}") for p in "absm"}
        idle = sem("wait_holder")

        def passes(w, xp):
            return ((w[0], xp[0]), (w[0], xp[1]), (w[1], xp[0]))

        L_X, L_QKVO, L_ATT, L_UP, L_DN, L_WG, L_WU, L_WD, L_ROWS, L_COLS = 0, 1, 3, 4, 6, 8, 9, 10, 11, 12
        MAT = KB * D
        o_att = NL * 4 * MAT
        o_up = o_att + 5 * MAT
        o_dn = o_up + NL * KB * F
        o_wg = o_dn + NL * FB * D
        o_end = o_wg + NX * MAT
        ids = arena[0:SEQS, o_end:o_end + 3 * P].rearrange("p (a t) -> p a t", a=3)
        xi, xf, xneg = ids[:, 0].bitcast(I32), ids[:, 1], ids[:, 2]
        QKVO = [arena[:, l * 4 * MAT:(l + 1) * 4 * MAT].rearrange("p (w k d) -> p w k d", w=4, k=KB) for l in range(NL)]
        ATT = arena[:, o_att:o_up].rearrange("p (w k d) -> p w k d", w=5, k=KB)
        RUP = [arena[:, o_up + l * KB * F:o_up + (l + 1) * KB * F] for l in range(NL)]
        RDN = [arena[:, o_dn + l * FB * D:o_dn + (l + 1) * FB * D] for l in range(NL)]
        RX = [arena[:, o:o + NX * MAT] for o in (o_wg, o_up, o_wg)]
        WX = (Wg, Wu, Wd)
        WT = Wg[:].rearrange("p a e k d -> p (a e k d)").bitcast(F32)[:, 0:NL * 3 * MAT].rearrange(
            "p (l w k d) -> p l w k d", l=NL, w=3, k=KB)

        def flat(ap):
            return ap.rearrange("p a b -> p (a b)")

        def att_dst(n, a, k):
            if n < 2:
                return Wqk[:, a, n, k]
            if n < 4:
                return Wfv[:, a, k, (n - 2) * D:(n - 1) * D]
            return Wao[:, a, k]

        cols = [(nwc[:, 0], norm_w), (nwc[:, 1], gnorm_w)]
        for l in range(NL):
            cols.append((bupc[:, l], bup[l]))

        with nc.Block() as block:
            @block.sync
            def _(sp):
                sp.dma_start(xi, x).then_inc(s_load[L_X], 16)
                for l in range(NL):
                    for n, w in enumerate((wq, wk, wv, wo)):
                        sp.dma_start(QKVO[l][:, n], w[l].rearrange("(k p) d -> p k d", p=P)).then_inc(s_load[L_QKVO + l], 16)
                for n, w in enumerate((a_q, a_k, a_f, a_v, a_o)):
                    sp.dma_start(ATT[:, n], w.rearrange("(k p) d -> p k d", p=P)).then_inc(s_load[L_ATT], 16)
                for l in range(NL):
                    sp.dma_start(RUP[l].rearrange("p (k f) -> p k f", k=KB),
                                 wup[l].rearrange("(k p) f -> p k f", p=P)).then_inc(s_load[L_UP + l], 16)
                    sp.dma_start(RDN[l].rearrange("p (k d) -> p k d", k=FB),
                                 wdown[l].rearrange("(k p) d -> p k d", p=P)).then_inc(s_load[L_DN + l], 16)
                for n, (w, ws) in enumerate(((gate_w, sg_w), (up_w, su_w), (down_w, sd_w))):
                    if n == 1:
                        sp.wait_ge(s_slo, 2 * NL)
                    if n == 2:
                        sp.wait_ge(s_slo, 2 * NL + 10)
                    v = RX[n].rearrange("p (e k d) -> p e k d", e=NX, k=KB)
                    for e in range(NE):
                        sp.dma_start(v[:, e], w[e].rearrange("(k p) d -> p k d", p=P)).then_inc(s_load[L_WG + n], 16)
                    for e in range(NX - NE):
                        src = ws[:, e * D:(e + 1) * D] if n < 2 else ws[e * D:(e + 1) * D, :]
                        sp.dma_start(v[:, NE + e], src.rearrange("(k p) d -> p k d", p=P)).then_inc(s_load[L_WG + n], 16)

            @block.scalar
            def _(act):
                rows = [(posb[:], pos[0:P, :])]
                for l in range(NL):
                    rows += [(gb[:, l, n], w[l].partition_broadcast(P)) for n, w in enumerate((ga, ba, gm, bm))]
                    rows.append((bdn[:, l], bdown[l].partition_broadcast(P)))
                for dst, src in rows:
                    act.dma_start(dst, src).then_inc(s_load[L_ROWS], 16)
                for dst, src in cols:
                    act.dma_start(dst, src.rearrange("(k p) -> p k", p=P),
                                  allow_slow_non_contiguous=True).then_inc(s_load[L_COLS], 16)
                act.dma_start(rw[:], router_w.rearrange("(k p) e -> p k e", p=P)).then_inc(s_load[L_COLS], 16)
                for l in range(NL):
                    act.wait_ge(s_load[L_UP + l], 16)
                    act.activation(flat(Wup[:, 0, l]), RUP[l], ACT.Copy, scale=WS).then_inc(s_shi, 1)
                    act.wait_ge(s_load[L_DN + l], 16)
                    act.activation(flat(Wdn[:, 0, l]), RDN[l], ACT.Copy, scale=WS).then_inc(s_shi, 1)
                for n in range(3 * NL):
                    act.wait_ge(s_sfull, 2 + n)
                    act.activation(flat(WT[:, n // 3, n % 3]), bank[1 + n][:], ACT.Copy).then_inc(s_rawt, 1)
                act.wait_ge(s_nws, 1)
                for n in range(5):
                    act.wait_ge(s_sfull, 8 + n)
                    for k in range(KB):
                        i = act.activation(att_dst(n, 0, k), bank[(7 + n) % 8][:, k * D:(k + 1) * D], ACT.Identity,
                                           scale=nws[:, n // 4, k:k + 1])
                    i.then_inc(s_shi, 1)
                for n in range(2 * NL):
                    act.wait_ge(s_sfull, 13 + n)
                    act.activation(flat((Wm, Wvo)[n % 2][:, 0, n // 2]), bank[(12 + n) % 8][:], ACT.Copy,
                                   scale=WS).then_inc(s_shi, 1)
                for n in range(3):
                    act.wait_ge(s_load[L_WG + n], 16 * NX)
                    act.activation(WX[n][:, 0].rearrange("p e k d -> p (e k d)"), RX[n], ACT.Copy, scale=WS).then_inc(s_shi, 1)

            @block.gpsimd
            def _(pool):
                pool.memset(ident[:], 0.0).then_inc(s_const, 1)
                pool.memset(causal[:], 0.0).then_inc(s_const, 1)
                pool.memset(upper[:], 1.0).then_inc(s_const, 1)
                pool.wait_ge(s_const, 3)
                pool.affine_select(out=ident[:], in_=ident[:], compare_op=ALU.not_equal, fill=1.0, base=0,
                                   pattern=[[-1, P]], channel_multiplier=1).then_inc(s_const, 1)
                pool.affine_select(out=causal[:], in_=causal[:], compare_op=ALU.is_ge, fill=NEG, base=0,
                                   pattern=[[-1, P]], channel_multiplier=1).then_inc(s_const, 1)
                pool.affine_select(out=upper[:], in_=upper[:], compare_op=ALU.is_ge, fill=0.0, base=0,
                                   pattern=[[1, P]], channel_multiplier=-1).then_inc(s_const, 1)
                pool.wait_ge(s_load[L_ROWS], 16 * (1 + 5 * NL))

            @block.vector
            def _(dve):
                steps = [0]

                def link(ins):
                    steps[0] += 1
                    ins.then_inc(s_step, 1)
                    dve.wait_ge(s_step, steps[0])

                dve.wait_ge(s_load[L_X], 16)
                link(dve.tensor_copy(xf, xi))
                link(dve.tensor_scalar(xneg, xf, 0.0, float(V), ALU.is_lt, ALU.mult))
                link(dve.tensor_tensor(xf, xf, xneg, ALU.add))
                dve.tensor_scalar(xf, xf, 0.0, float(V - 1), ALU.max, ALU.min).then_inc(s_ids, 1)
                dve.memset(idx[:, SEQS:SEQS + G], 0)
                dve.wait_ge(s_const, 6)
                dve.tensor_scalar(tri[:], upper[:], upper[:, P // 2 - 1:P // 2], None, ALU.subtract)
                dve.wait_ge(s_load[L_COLS], 16 * (len(cols) + 1))
                dve.tensor_scalar(nws[:], nwc[:], WS, None, ALU.mult).then_inc(s_nws, 1)
                dve.wait_ge(s_sfull, 1)
                dve.tensor_copy(idx[:, 0:SEQS], bank[0][:, 0:SEQS]).then_inc(s_idx, 1)
                for n in range(2 * NL):
                    l = n // 2
                    w, raw = (Wdn, RDN[l]) if n % 2 else (Wup, RUP[l])
                    dve.wait_ge(s_shi, n + 1)
                    dve.scalar_tensor_tensor(flat(w[:, 1, l]), raw, WS, flat(w[:, 0, l]), ALU.mult, ALU.subtract).then_inc(s_slo, 1)
                dve.wait_ge(s_nws, 1)
                for n in range(5):
                    dve.wait_ge(s_shi, 2 * NL + n + 1)
                    for k in range(KB):
                        i = dve.scalar_tensor_tensor(att_dst(n, 1, k), bank[(7 + n) % 8][:, k * D:(k + 1) * D],
                                                     nws[:, n // 4, k:k + 1], att_dst(n, 0, k), ALU.mult, ALU.subtract)
                    i.then_inc(s_slo, 1)
                for n in range(2 * NL):
                    w = (Wm, Wvo)[n % 2]
                    dve.wait_ge(s_shi, 2 * NL + 5 + n + 1)
                    dve.scalar_tensor_tensor(flat(w[:, 1, n // 2]), bank[(12 + n) % 8][:], WS, flat(w[:, 0, n // 2]),
                                             ALU.mult, ALU.subtract).then_inc(s_slo, 1)
                for n in range(3):
                    dve.wait_ge(s_shi, 2 * NL + 5 + 2 * NL + n + 1)
                    dve.scalar_tensor_tensor(WX[n][:, 1].rearrange("p e k d -> p (e k d)"), RX[n], WS,
                                             WX[n][:, 0].rearrange("p e k d -> p (e k d)"), ALU.mult,
                                             ALU.subtract).then_inc(s_slo, 1)

            @block.tensor
            def _(pe):
                pe.wait_ge(s_const, 6)
                pe.wait_ge(s_ids, 1)
                pe.transpose(bank[0][:, 0:SEQS], xf, ident[0:SEQS, 0:SEQS]).then_inc(s_sfull, 1)

                def turn(src, b):
                    for kk in range(KB):
                        for k in range(KB):
                            i = pe.transpose(bank[b][:, kk * D + k * P:kk * D + (k + 1) * P],
                                             src[:, k, kk * P:(kk + 1) * P], ident[:])
                    i.then_inc(s_sfull, 1)

                for n in range(3 * NL):
                    if n % 3 == 0:
                        pe.wait_ge(s_load[L_QKVO + n // 3], 64)
                    turn(QKVO[n // 3][:, n % 3], 1 + n)
                pe.wait_ge(s_load[L_ATT], 80)
                for n in range(5):
                    if n == 1:
                        pe.wait_ge(s_idx, 1)
                        pe.wait_ge(s_rawt, 3 * NL)
                    turn(ATT[:, n], (7 + n) % 8)
                for n in range(2 * NL):
                    l, w = divmod(n, 2)
                    if n == 3:
                        pe.wait_ge(s_slo, 2 * NL + 1)
                    b = bank[(12 + n) % 8]
                    for k in range(KB):
                        for c in range(KB):
                            lhs = WT[:, l, 2 * w, c, k * P:(k + 1) * P]
                            rhs = QKVO[l][:, 3, c] if w else WT[:, l, 1, c]
                            i = pe.matmul(b[:, k * D:(k + 1) * D], lhs, rhs, start=(c == 0), stop=(c == KB - 1))
                    i.then_inc(s_sfull, 1)

        ROWS = {"a": layer_rows(0), "b": layer_rows(1), "s": S_ROWS, "m": moe_rows(0, NE, NX), "n": moe_rows(NE, NX, NX)}
        LAG = {p: n for n, p in enumerate("absmn")}
        ORDER = {}

        def run(eng, letter, do_t, do_s, do_m):
            do = {"a": do_t, "b": do_t, "s": do_s, "m": do_m, "n": do_m}

            def steps(parts, g):
                if parts not in ORDER:
                    ORDER[parts] = plan(**{p: ROWS[p] for p in parts})
                for part, name, args, at in ORDER[parts]:
                    if at == letter:
                        do[part](g - LAG[part], name, *args)

            for n in range(4):
                steps("absmn"[:n + 1], n)
            with eng.Fori(4, NG) as g:
                steps("absmn", g)
            for n in range(4):
                steps("absmn"[n + 1:], NG + n)

        def filled(g, name):
            return full[BANK[name]], PER[BANK[name]] * g + ORD[name] + 1

        def vacant(g, name):
            return free[BANK[name]], PER[BANK[name]] * g + ORD[name] + 1

        def taken(g, name):
            return free[BANK[name]], PER[BANK[name]] * g + ORD[name] + 2

        def ps(name):
            return bank[BANK[name]]

        def first(g):
            return isinstance(g, int) and g == 0

        with nc.Block() as block:
            @block.sync
            def _(sp):
                def store(g):
                    sp.wait_ge(acc_done, g + 1)
                    sp.dma_start(out[bass.ds(g * G, G)].rearrange("s t d -> t s d"), ACC).then_inc(out_done, 16)
                    sp.wait_ge(out_done, 16 * g + 16)
                    sp.sem_inc(acc_free, 1)

                sp.sem_inc(acc_free, 1)
                with sp.Fori(0, NG) as g:
                    store(g)

            @block.tensor
            def _(pe):
                def products(dst, pairs):
                    for n, (lhs, rhs) in enumerate(pairs):
                        i = pe.matmul(dst, lhs, rhs, start=(n == 0), stop=(n == len(pairs) - 1))
                    return i

                def by_feature(dst, w, xp, m):
                    return products(dst, [(wa[:, k, m * P:(m + 1) * P], xa[:, k])
                                          for k in range(w[0].shape[1]) for wa, xa in passes(w, xp)])

                def by_token(dst, w, xp, j):
                    return products(dst, [(xa[:, k, j * P:(j + 1) * P], wa[:, k])
                                          for k in range(w[0].shape[1]) for wa, xa in passes(w, xp)])

                def both(ap):
                    return ap[:, 0], ap[:, 1]

                def turn(g, src, name):
                    pe.wait_ge(*vacant(g, name))
                    for k in range(KB):
                        for j in range(G):
                            i = pe.transpose(ps(name)[:, k * GT + j * P:k * GT + (j + 1) * P], src[:, j, k * P:(k + 1) * P],
                                             ident[:])
                    i.then_inc(full[BANK[name]], 1)

                HT2, Z2, X2 = [both(h) for h in HTP], both(ZP), both(XP)

                def do_t(g, name, l, q=None):
                    n = f"{name}.{l}"
                    if name == "x":
                        pe.wait_ge((h_ready, out_ready[0])[l], g + 1)
                        turn(g, H[l], n)
                    elif name == "t":
                        pe.wait_ge(ht_ready[l], 2 * g + 1)
                        pe.wait_ge(*vacant(g, n))
                        for m in range(KB):
                            i = by_feature(ps(n)[:, m * GT:(m + 1) * GT], both(Wm[:, :, l]), HT2[l], m)
                        i.then_inc(full[BANK[n]], 1)
                    elif name == "v":
                        pe.wait_ge(*vacant(g, n))
                        for j in range(G):
                            i = by_token(ps(n)[:, j * D:(j + 1) * D], both(Wvo[:, :, l]), HT2[l], j)
                        i.then_inc(full[BANK[n]], 1)
                    elif name == "sc":
                        pe.wait_ge(*taken(g, f"t.{l}"))
                        pe.wait_ge(*vacant(g, n))
                        for j in range(G):
                            js = slice(j * P, (j + 1) * P)
                            i = products(ps(n)[:, js], [(TT[l][:, k, js], HTF[l][:, k, js]) for k in range(KB)])
                        i.then_inc(full[BANK[n]], 1)
                    elif name == "pt":
                        pe.wait_ge(p_ready[l], g + 1)
                        pe.wait_ge(*vacant(g, n))
                        for j in range(G):
                            i = pe.transpose(ps(n)[:, j * P:(j + 1) * P], SM[l][:, j], ident[:])
                        i.then_inc(full[BANK[n]], 1)
                    elif name == "z":
                        pe.wait_ge(*taken(g, f"pt.{l}"))
                        pe.wait_ge(*taken(g, f"v.{l}"))
                        pe.wait_ge(*vacant(g, n))
                        for j in range(G):
                            i = pe.matmul(ps(n)[:, j * D:(j + 1) * D], PT[l][:, j], VO[l][:, j], start=True, stop=True)
                        i.then_inc(full[BANK[n]], 1)
                    elif name == "y":
                        pe.wait_ge(mid_ready[l], g + 1)
                        turn(g, H[l], n)
                    elif name == "up":
                        n = f"up{q}.{l}"
                        if q == 0:
                            pe.wait_ge(ht_ready[l], 2 * g + 2)
                        pe.wait_ge(*vacant(g, n))
                        for m in range(2):
                            i = by_feature(ps(n)[:, m * GT:(m + 1) * GT], both(Wup[:, :, l]), HT2[l], 2 * q + m)
                        i.then_inc(full[BANK[n]], 1)
                    elif name == "dn":
                        pe.wait_ge(a_ready[l], 4 * g + 4)
                        pe.wait_ge(*vacant(g, n))
                        for j in range(G):
                            i = by_token(ps(n)[:, j * D:(j + 1) * D], both(Wdn[:, :, l]), both(AP), j)
                        i.then_inc(full[BANK[n]], 1)

                def do_s(g, name):
                    if name == "gx":
                        pe.wait_ge(xs_ready, 2 * g + 1)
                        turn(g, XS, "gx")
                    elif name == "qk":
                        pe.wait_ge(zt_ready, 2 * g + 1)
                        for c, n in enumerate("qk"):
                            pe.wait_ge(*vacant(g, n))
                            for m in range(KB):
                                i = by_feature(ps(n)[:, m * GT:(m + 1) * GT], both(Wqk[:, :, c]), Z2, m)
                            i.then_inc(full[BANK[n]], 1)
                    elif name == "fv":
                        for j in range(G):
                            pe.wait_ge(*vacant(g, f"fv{j}"))
                            by_token(ps(f"fv{j}")[:], both(Wfv), Z2, j).then_inc(full[BANK[f"fv{j}"]], 1)
                    elif name == "decay":
                        pe.wait_ge(g_ready, g + 1)
                        pe.wait_ge(*vacant(g, "D"))
                        for j in range(G):
                            i = pe.matmul(ps("D")[:, j * D:(j + 1) * D], tri[:], US[:, j], start=True, stop=True)
                        i.then_inc(full[BANK["D"]], 1)
                    elif name in ("scores", "vscores"):
                        if name == "scores":
                            stem, left, right = "A", KT, QT
                            pe.wait_ge(*taken(g, "q"))
                            pe.wait_ge(*taken(g, "k"))
                        else:
                            stem, left, right = "B", SPT, PPT
                            pe.wait_ge(*taken(g, "st"))
                            pe.wait_ge(*taken(g, "gp"))
                        for par in range(2):
                            pe.wait_ge(*vacant(g, f"{stem}{par}"))
                        for j in range(G):
                            js = slice(j * P, (j + 1) * P)
                            for hc in range(2):
                                for par in range(2):
                                    n = f"{stem}{par}"
                                    c = j * 2 + hc
                                    rows = slice(par * DK, (par + 1) * DK)
                                    i = pe.matmul(ps(n)[:, c * P:(c + 1) * P], left[rows, hc, js], right[rows, hc, js],
                                                  start=True, stop=True)
                                    if c == 3:
                                        i.then_inc(full[BANK[n]], 1)
                    elif name == "st":
                        pe.wait_ge(sp_ready, g + 1)
                        turn(g, XS, "st")
                    elif name in ("gz", "o"):
                        if name == "gz":
                            left, right = AT, XS
                            pe.wait_ge(*taken(g, "A0"))
                            pe.wait_ge(*taken(g, "A1"))
                        else:
                            left, right = BT, VB
                            pe.wait_ge(*taken(g, "B0"))
                            pe.wait_ge(*taken(g, "B1"))
                            pe.wait_ge(*taken(g, "fv1"))
                        pe.wait_ge(*vacant(g, name))
                        for j in range(G):
                            for h in range(HEADS):
                                c = j * HEADS + h
                                i = pe.matmul(ps(name)[:, c * DK:(c + 1) * DK], left[:, h % 2, j * 2 + h // 2],
                                              right[:, j, h * DK:(h + 1) * DK], start=True, stop=True)
                        i.then_inc(full[BANK[name]], 1)
                    elif name == "gp":
                        pe.wait_ge(pp_ready, g + 1)
                        turn(g, EB, "gp")
                    elif name == "ot":
                        pe.wait_ge(os_ready, g + 1)
                        turn(g, US, "ot")
                    elif name == "w":
                        pe.wait_ge(zt_ready, 2 * g + 2)
                        pe.wait_ge(*vacant(g, "w"))
                        for j in range(G):
                            i = by_token(ps("w")[:, j * D:(j + 1) * D], both(Wao), Z2, j)
                        i.then_inc(full[BANK["w"]], 1)

                def do_m(g, name, e=None):
                    if name == "mx":
                        pe.wait_ge(xs_ready, 2 * g + 2)
                        turn(g, XS, "mx")
                    elif name == "router":
                        pe.wait_ge(*taken(g, "mx"))
                        pe.wait_ge(xm_ready, g + 1)
                        pe.wait_ge(*vacant(g, "rl"))
                        for j in range(G):
                            i = products(ps("rl")[:, j * NE:(j + 1) * NE],
                                         [(XF[:, k, j * P:(j + 1) * P], rw[:, k]) for k in range(KB)])
                        i.then_inc(full[BANK["rl"]], 1)
                    elif name == "gu":
                        for n, w in ((f"g{e}", Wg), (f"u{e}", Wu)):
                            pe.wait_ge(*vacant(g, n))
                            for m in range(2):
                                i = by_feature(ps(n)[:, m * GT:(m + 1) * GT], both(w[:, :, e]), X2, m)
                            i.then_inc(full[BANK[n]], 1)
                    elif name == "down":
                        n = f"e{e}"
                        pe.wait_ge(mlo_ready, NX * g + e + 1)
                        pe.wait_ge(*vacant(g, n))
                        for j in range(G):
                            i = by_token(ps(n)[:, j * D:(j + 1) * D], both(Wd[:, :, e]), both(MP[e % 2]), j)
                        i.then_inc(full[BANK[n]], 1)

                for b in range(8):
                    pe.sem_inc(free[b], 1)
                run(pe, "P", do_t, do_s, do_m)

            @block.scalar
            def _(act):
                def take(g, name, dst, **kw):
                    act.wait_ge(*filled(g, name))
                    act.activation(dst, ps(name)[:], ACT.Copy, **kw).then_inc(free[BANK[name]], 1)

                def take_pair(g, name, dst, hi):
                    act.wait_ge(*filled(g, name))
                    act.activation(flat(dst), ps(name)[:], ACT.Copy)
                    act.activation(flat(hi), ps(name)[:], ACT.Copy).then_inc(free[BANK[name]], 1)

                def do_t(g, name, l, q=None):
                    n = f"{name}.{l}"
                    if name in ("x", "y"):
                        take_pair(g, n, HTF[l], HTP[l][:, 0])
                    elif name == "t":
                        take(g, n, flat(TT[l]), scale=IWS)
                    elif name == "sexp":
                        act.wait_ge(nb_ready[l], g + 1)
                        for j in range(G):
                            i = act.activation(SM[l][:, j], SM[l][:, j], ACT.Exp, bias=nbias[l][:, j:j + 1],
                                               scale=1.0 / D ** 0.5, accum_out=rsum[l][:, j:j + 1])
                        i.then_inc(p_ready[l], 1)
                    elif name == "up":
                        n = f"up{q}.{l}"
                        if q == 0 and l == 0 and not first(g):
                            act.wait_ge(*filled(g - 1, "dn.1"))
                        act.wait_ge(*filled(g, n))
                        if q >= 2:
                            act.wait_ge(a_ready[l], 4 * g + q - 1)
                        for dst in (RT[:, q % 2], AP[:, 0, 2 * q:2 * q + 2]):
                            for m in range(2):
                                i = act.activation(dst[:, m], ps(n)[:, m * GT:(m + 1) * GT], ACT.Relu, scale=IWS,
                                                   bias=bupc[:, l, 2 * q + m:2 * q + m + 1])
                        i.then_inc(free[BANK[n]], 1)

                def do_s(g, name):
                    if name in ("gx", "ot"):
                        take_pair(g, name, ZF, ZP[:, 0])
                    elif name == "qk":
                        for n, dst in (("q", EB), ("k", PB)):
                            act.wait_ge(*filled(g, n))
                            act.activation(flat(dst), ps(n)[:], ACT.Tanh, scale=0.5 * IWS).then_inc(qe_ready, 1)
                    elif name == "fv":
                        act.wait_ge(*taken(g, "q"))
                        act.wait_ge(*taken(g, "k"))
                        for j in range(G):
                            act.wait_ge(*filled(g, f"fv{j}"))
                            act.activation(PB[:, j], ps(f"fv{j}")[:, 0:D], ACT.Abs, scale=IWS).then_inc(fa_step, 1)
                            act.activation(EB[:, j], ps(f"fv{j}")[:, D:2 * D], ACT.Tanh, scale=0.5 * IWS).then_inc(ve_ready, 1)
                    elif name == "lnf":
                        act.wait_ge(fa_step, (G + 1) * g + G)
                        act.activation(flat(PB), flat(PB), ACT.Exp, scale=-1.0).then_inc(fa_step, 1)
                        act.wait_ge(fa_step, (G + 1) * g + G + 1)
                        act.activation(flat(PB), flat(PB), ACT.Ln, bias=1.0).then_inc(fl_ready, 1)
                    elif name == "gexp":
                        act.wait_ge(g_ready, g + 1)
                        act.activation(flat(XS), flat(US), ACT.Exp, scale=1.0 / GATE_NORM).then_inc(es_ready, 1)
                    elif name == "dexp":
                        act.wait_ge(*taken(g, "D"))
                        act.activation(flat(PB), flat(EB), ACT.Exp, scale=-1.0 / GATE_NORM).then_inc(ei_ready, 1)
                        act.activation(flat(EB), flat(EB), ACT.Exp, scale=1.0 / GATE_NORM).then_inc(e_ready, 1)
                    elif name == "st":
                        take(g, "st", flat(SPT))
                    elif name == "zexp":
                        act.wait_ge(zs_ready, g + 1)
                        act.activation(flat(PB), flat(PB), ACT.Exp).then_inc(ze_ready, 1)
                    elif name == "gp":
                        take(g, "gp", flat(PPT))
                    elif name == "otanh":
                        act.wait_ge(*taken(g, "o"))
                        act.activation(flat(EB), flat(US), ACT.Tanh, scale=0.5).then_inc(oe_ready, 1)
                    elif name == "ssq":
                        act.wait_ge(os_ready, g + 1)
                        for j in range(G):
                            i = act.activation(PB[:, j], US[:, j], ACT.Square, scale=0.5, accum_out=ssq[:, j:j + 1])
                        i.then_inc(sq_ready, 1)

                def high(g, e):
                    act.wait_ge(*taken(g, f"u{e}"))
                    if e >= 2:
                        act.wait_ge(*filled(g, f"e{e - 2}"))
                    act.activation(flat(MP[e % 2][:, 0]), MA[:, e % 2], ACT.Copy).then_inc(mhi_ready, 1)

                def do_m(g, name, e=None):
                    if name == "mx":
                        take_pair(g, "mx", XF, XP[:, 0])
                    elif name == "rexp":
                        act.wait_ge(rx_ready, g + 1)
                        act.activation(ex[:], ex[:], ACT.Exp).then_inc(re_ready, 1)
                    elif name == "gu":
                        act.wait_ge(*filled(g, f"g{e}"))
                        act.activation(ME[:, e % 2], ps(f"g{e}")[:], ACT.Tanh, scale=0.5 * IWS).then_inc(me_ready, 1)
                    elif name == "split":
                        high(g, e)

                run(act, "A", do_t, do_s, do_m)

            @block.gpsimd
            def _(pool):
                def rows(ap):
                    return ap.to_broadcast([P, G, D])

                def gather():
                    for j in range(G):
                        pool.indirect_dma_start(EMB[:, j], None, emb, bass.IndirectOffsetOnAxis(cur[:, j:j + 1], 0)).then_inc(emb_ready, 16)

                def affine(g, dst, l, n, done):
                    pool.wait_ge(x_ready[l], 2 * g + n + 1)
                    pool.tensor_tensor(dst, U[l], rows(gb[:, l, 2 * n:2 * n + 1]), ALU.mult).then_inc(pool_step[l], 1)
                    pool.wait_ge(pool_step[l], 2 * g + n + 1)
                    pool.tensor_tensor(dst, dst, rows(gb[:, l, 2 * n + 1:2 * n + 2]), ALU.add).then_inc(done[l], 1)

                def do_t(g, name, l, q=None):
                    if name == "gather":
                        pool.wait_ge(cur_ready, g + 2)
                        pool.sem_inc(idle, 1)
                        gather()
                    elif name == "mid":
                        affine(g, H[l], l, 0, mid_ready)
                    elif name == "hr":
                        pool.wait_ge(mid_ready[l], g + 1)
                        pool.tensor_tensor(HR[l], H[l], rows(bdn[:, l:l + 1]), ALU.add).then_inc(hr_ready[l], 1)
                    elif name == "out":
                        if not first(g):
                            if l == 0:
                                pool.wait_ge(*filled(g - 1, "y.1"))
                            else:
                                pool.wait_ge(*taken(g - 1, "w"))
                        affine(g, (H[1], HS)[l], l, 1, out_ready)

                def do_s(g, name):
                    pass

                def low(g, e):
                    pool.wait_ge(mhi_ready, NX * g + e + 1)
                    pool.tensor_tensor(flat(MP[e % 2][:, 1]), MA[:, e % 2], flat(MP[e % 2][:, 0]), ALU.subtract).then_inc(mlo_ready, 1)

                def do_m(g, name, e=None):
                    if name == "acc":
                        pool.wait_ge(*taken(g, "w"))
                        pool.sem_inc(idle, 1)
                        pool.wait_ge(acc_free, g + 1)
                        pool.sem_inc(idle, 1)
                        pool.tensor_copy(ACC, HO).then_inc(acc_ready, 1)
                    elif name == "split":
                        low(g, e)

                pool.wait_ge(cur_ready, 1)
                gather()
                run(pool, "G", do_t, do_s, do_m)
                pool.wait_ge(emb_ready, 16 * G * (NG + 1))

            @block.vector
            def _(dve):
                count = dict.fromkeys(LINKS, 0)

                def link(part, g, ins):
                    count[part] += 1
                    ins.then_inc(dve_step[part], 1)
                    dve.wait_ge(dve_step[part], LINKS[part] * g + count[part])

                def close(part):
                    assert count[part] == LINKS[part], (part, count[part])
                    count[part] = 0

                def inverse_root(part, g, last=1.0):
                    _, _, vare, rstd, newt = NORM[part]
                    link(part, g, dve.tensor_scalar(newt[:].bitcast(I32), vare[:].bitcast(I32), 1, None,
                                                    ALU.logical_shift_right))
                    link(part, g, dve.tensor_scalar(rstd[:].bitcast(I32), newt[:].bitcast(I32), -1.0, float(0x5f3759df),
                                                    ALU.mult, ALU.add))
                    for _ in range(3):
                        link(part, g, dve.scalar_tensor_tensor(newt[:], rstd[:], -0.5, rstd[:], ALU.mult, ALU.mult))
                        link(part, g, dve.tensor_tensor(newt[:], newt[:], vare[:], ALU.mult))
                        link(part, g, dve.scalar_tensor_tensor(rstd[:], newt[:], 1.5, rstd[:], ALU.add, ALU.mult))
                    if last != 1.0:
                        link(part, g, dve.tensor_scalar(rstd[:], rstd[:], last, None, ALU.mult))

                def norm(part, g, src, dst, done, mul=1.0, add=EPS):
                    stat, mv, vare, rstd, _ = NORM[part]
                    for j in range(G):
                        i = dve.bn_stats(stat[:, j], src[:, j])
                    link(part, g, i)
                    dve.sem_inc(idle, 1)
                    for j in range(G):
                        i = dve.bn_aggr(mv[:, j], stat[:, j])
                    link(part, g, i)
                    link(part, g, dve.tensor_scalar(vare[:], mv[:, :, 1], mul, add, ALU.mult, ALU.add))
                    inverse_root(part, g)
                    for j in range(G):
                        i = dve.tensor_scalar(dst[:, j], src[:, j], mv[:, j, 0:1], rstd[:, j:j + 1], ALU.subtract, ALU.mult)
                    i.then_inc(done, 1)

                def low(g, name, F, Pr, done):
                    dve.wait_ge(*taken(g, name))
                    dve.tensor_tensor(flat(Pr[:, 1]), flat(F), flat(Pr[:, 0]), ALU.subtract).then_inc(done, 1)

                def do_t(g, name, l, q=None):
                    n = f"{name}.{l}"
                    part = "ab"[l]
                    if name == "embed":
                        dve.wait_ge(emb_ready, 16 * G * g + 16 * G)
                        dve.tensor_tensor(H[0], EMB, posb[:, None, :].to_broadcast([P, G, D]), ALU.add).then_inc(h_ready, 1)
                        dve.tensor_copy(cur[:], idx[:, bass.ds(G * g + G, G)]).then_inc(cur_ready, 1)
                    elif name in ("x", "y"):
                        low(g, n, HTF[l], HTP[l], ht_ready[l])
                    elif name == "v":
                        dve.wait_ge(*filled(g, n))
                        dve.tensor_scalar(flat(VO[l]), ps(n)[:], IWS, None, ALU.mult).then_inc(free[BANK[n]], 1)
                    elif name == "sc":
                        dve.wait_ge(*filled(g, n))
                        dve.tensor_tensor(SM[l], ps(n)[:, 0:G * P].rearrange("p (j s) -> p j s", j=G),
                                          causal[:, None, :].to_broadcast([P, G, P]), ALU.add).then_inc(free[BANK[n]], 1)
                        dve.wait_ge(*taken(g, n))
                        link(part, g, dve.tensor_reduce(smax[l][:], SM[l], AX, ALU.max))
                        dve.tensor_scalar(nbias[l][:], smax[l][:], -1.0 / D ** 0.5, None, ALU.mult).then_inc(nb_ready[l], 1)
                    elif name == "pt":
                        dve.wait_ge(p_ready[l], g + 1)
                        dve.reciprocal(rinv[l][:], rsum[l][:])
                        dve.wait_ge(*filled(g, n))
                        dve.tensor_copy(flat(PT[l]), ps(n)[:, 0:G * P]).then_inc(free[BANK[n]], 1)
                    elif name == "z":
                        if not first(g):
                            dve.wait_ge(out_ready[l], g)
                        dve.wait_ge((h_ready, out_ready[0])[l], g + 1)
                        dve.wait_ge(*taken(g, f"pt.{l}"))
                        dve.wait_ge(*filled(g, n))
                        for j in range(G):
                            i = dve.scalar_tensor_tensor(U[l][:, j], ps(n)[:, j * D:(j + 1) * D], rinv[l][:, j:j + 1],
                                                         H[l][:, j], ALU.mult, ALU.add)
                        i.then_inc(free[BANK[n]], 1)
                    elif name == "mnorm":
                        dve.wait_ge(*taken(g, f"z.{l}"))
                        norm(part, g, U[l], U[l], x_ready[l])
                    elif name == "up":
                        dve.wait_ge(*taken(g, f"up{q}.{l}"))
                        dve.tensor_tensor(flat(AP[:, 1, 2 * q:2 * q + 2]), flat(RT[:, q % 2]), flat(AP[:, 0, 2 * q:2 * q + 2]),
                                          ALU.subtract).then_inc(a_ready[l], 1)
                    elif name == "dn":
                        dve.wait_ge(hr_ready[l], g + 1)
                        dve.wait_ge(*filled(g, n))
                        dve.scalar_tensor_tensor(flat(U[l]), ps(n)[:], IWS, flat(HR[l]), ALU.mult,
                                                 ALU.add).then_inc(free[BANK[n]], 1)
                    elif name == "onorm":
                        dve.wait_ge(*taken(g, f"dn.{l}"))
                        norm(part, g, U[l], U[l], x_ready[l])
                        close(part)


                def do_s(g, name):
                    if name == "norm":
                        dve.wait_ge(out_ready[1], g + 1)
                        if not first(g):
                            dve.wait_ge(*filled(g - 1, "mx"))
                        norm("s", g, HS, XS, xs_ready, 1.0 + EPS, EPS * EPS)
                    elif name in ("gx", "ot"):
                        low(g, name, ZF, ZP, zt_ready)
                    elif name == "qk":
                        for c, (n, tanh, dst) in enumerate((("q", EB, QT), ("k", PB, KT))):
                            dve.wait_ge(qe_ready, 2 * g + c + 1)
                            dve.scalar_tensor_tensor(flat(dst), flat(tanh), 1.0, ps(n)[:], ALU.add,
                                                     ALU.mult).then_inc(free[BANK[n]], 1)
                    elif name == "fv":
                        if not first(g):
                            dve.wait_ge(acc_ready, g)
                        for j in range(G):
                            n = f"fv{j}"
                            dve.wait_ge(ve_ready, G * g + j + 1)
                            i = dve.tensor_scalar(US[:, j], ps(n)[:, 0:D], 0.0, IWS, ALU.min, ALU.mult)
                            if j == G - 1:
                                i.then_inc(mn_ready, 1)
                            dve.scalar_tensor_tensor(VB[:, j], EB[:, j], 1.0, ps(n)[:, D:2 * D], ALU.add,
                                                     ALU.mult).then_inc(free[BANK[n]], 1)
                    elif name == "g":
                        dve.wait_ge(mn_ready, g + 1)
                        dve.wait_ge(fl_ready, g + 1)
                        dve.tensor_tensor(flat(US), flat(US), flat(PB), ALU.subtract).then_inc(g_ready, 1)
                    elif name == "decay":
                        dve.wait_ge(*filled(g, "D"))
                        dve.tensor_scalar(flat(EB), ps("D")[:], EXP_CLAMP * GATE_NORM, -EXP_CLAMP * GATE_NORM,
                                          ALU.min, ALU.max).then_inc(free[BANK["D"]], 1)
                    elif name == "slots":
                        dve.wait_ge(es_ready, g + 1)
                        link("s", g, dve.tensor_scalar(flat(XS), flat(XS), -1.0, 1.0, ALU.mult, ALU.add))
                        dve.wait_ge(ei_ready, g + 1)
                        dve.tensor_tensor(flat(XS), flat(XS), flat(PB), ALU.mult).then_inc(sp_ready, 1)
                    elif name in ("scores", "vscores"):
                        stem, dst, f = ("A", AT, (0.5 * IWS) ** 2) if name == "scores" else ("B", BT, 1.0)
                        for par in range(2):
                            n = f"{stem}{par}"
                            dve.wait_ge(*filled(g, n))
                            dve.scalar_tensor_tensor(dst[:, par], ps(n)[:].rearrange("p (c t) -> p c t", c=4), f,
                                                     upper[:, None, :].to_broadcast([P, 4, P]), ALU.mult,
                                                     ALU.mult).then_inc(free[BANK[n]], 1)
                    elif name == "gz":
                        dve.wait_ge(e_ready, g + 1)
                        dve.wait_ge(*filled(g, "gz"))
                        dve.tensor_tensor(flat(PB), ps("gz")[:], flat(EB), ALU.mult).then_inc(free[BANK["gz"]], 1)
                        z3 = flat(PB).rearrange("p (c m) -> p c m", c=G * HEADS)
                        dve.wait_ge(*taken(g, "gz"))
                        link("s", g, dve.tensor_reduce(zmax[:], z3, AX, ALU.max))
                        dve.tensor_tensor(z3, z3, zmax[:, :, None].to_broadcast([P, G * HEADS, DK]),
                                          ALU.subtract).then_inc(zs_ready, 1)
                    elif name == "pp":
                        dve.wait_ge(ze_ready, g + 1)
                        dve.tensor_tensor(flat(EB), flat(PB), flat(EB), ALU.mult).then_inc(pp_ready, 1)
                    elif name == "zsum":
                        z3 = flat(PB).rearrange("p (c m) -> p c m", c=G * HEADS)
                        link("s", g, dve.tensor_reduce(zsum[:], z3, AX, ALU.add))
                        link("s", g, dve.reciprocal(zsum[:], zsum[:]))
                        link("s", g, dve.tensor_scalar(zsum[:], zsum[:], 0.5 * IWS, None, ALU.mult))
                    elif name == "o":
                        dve.wait_ge(*filled(g, "o"))
                        dve.tensor_tensor(flat(US).rearrange("p (c v) -> p c v", c=G * HEADS),
                                          ps("o")[:].rearrange("p (c v) -> p c v", c=G * HEADS),
                                          zsum[:, :, None].to_broadcast([P, G * HEADS, DK]), ALU.mult).then_inc(free[BANK["o"]], 1)
                    elif name == "osw":
                        dve.wait_ge(oe_ready, g + 1)
                        dve.scalar_tensor_tensor(flat(US), flat(EB), 1.0, flat(US), ALU.add, ALU.mult).then_inc(os_ready, 1)
                    elif name == "root":
                        dve.wait_ge(sq_ready, g + 1)
                        link("s", g, dve.tensor_scalar(NORM["s"][2][:], ssq[:], 1.0 / D, EPS, ALU.mult, ALU.add))
                        inverse_root("s", g, 0.5 * IWS)
                    elif name == "res":
                        dve.wait_ge(*filled(g, "w"))
                        for j in range(G):
                            i = dve.scalar_tensor_tensor(HO[:, j], ps("w")[:, j * D:(j + 1) * D], NORM["s"][3][:, j:j + 1],
                                                         HS[:, j], ALU.mult, ALU.add)
                        i.then_inc(free[BANK["w"]], 1)
                    elif name == "fnorm":
                        dve.wait_ge(*taken(g, "w"))
                        norm("s", g, HO, XS, xs_ready)
                        close("s")

                def do_m(g, name, e=None):
                    if name == "mx":
                        low(g, "mx", XF, XP, xm_ready)
                    elif name == "router":
                        dve.wait_ge(*filled(g, "rl"))
                        dve.tensor_copy(lg[:], ps("rl")[:, 0:G * NE].rearrange("p (j e) -> p j e", j=G)).then_inc(free[BANK["rl"]], 1)
                        dve.wait_ge(*taken(g, "rl"))
                        dve.sem_inc(idle, 1)
                        for j in range(G):
                            i = dve.max(top[:, j], lg[:, j])
                        link("m", g, i)
                        dve.tensor_tensor(ex[:], lg[:], top[:, :, 0:1].to_broadcast([P, G, NE]), ALU.subtract).then_inc(rx_ready, 1)
                        dve.tensor_tensor(keep[:], lg[:], top[:, :, 1:2].to_broadcast([P, G, NE]), ALU.is_ge)
                    elif name == "gates":
                        dve.wait_ge(re_ready, g + 1)
                        link("m", g, dve.tensor_reduce(esum[:], ex[:], AX, ALU.add))
                        link("m", g, dve.reciprocal(esum[:], esum[:]))
                        link("m", g, dve.tensor_tensor(comb[:], ex[:], keep[:], ALU.mult))
                        link("m", g, dve.scalar_tensor_tensor(comb[:], comb[:], IWS, esum[:, :, None].to_broadcast([P, G, NE]),
                                                              ALU.mult, ALU.mult))
                        close("m")
                    elif name == "gu":
                        dve.wait_ge(me_ready, NX * g + e + 1)
                        if e >= 2:
                            dve.wait_ge(mlo_ready, NX * g + e - 1)
                        dve.scalar_tensor_tensor(MA[:, e % 2], ME[:, e % 2], 1.0, ps(f"g{e}")[:], ALU.add,
                                                 ALU.mult).then_inc(free[BANK[f"g{e}"]], 1)
                        dve.wait_ge(*filled(g, f"u{e}"))
                        dve.wait_ge(*taken(g, f"g{e}"))
                        dve.scalar_tensor_tensor(MA[:, e % 2], ps(f"u{e}")[:], 0.5 * IWS * IWS, MA[:, e % 2], ALU.mult,
                                                 ALU.mult).then_inc(free[BANK[f"u{e}"]], 1)
                    elif name == "down":
                        if e == 0:
                            dve.wait_ge(acc_ready, g + 1)
                        else:
                            dve.wait_ge(*taken(g, f"e{e - 1}"))
                        n = f"e{e}"
                        dve.wait_ge(*filled(g, n))
                        if e < NE:
                            for j in range(G):
                                i = dve.scalar_tensor_tensor(ACC[:, j], ps(n)[:, j * D:(j + 1) * D], comb[:, j, e:e + 1],
                                                             ACC[:, j], ALU.mult, ALU.add)
                        else:
                            i = dve.scalar_tensor_tensor(flat(ACC), ps(n)[:], IWS, flat(ACC), ALU.mult, ALU.add)
                        i.then_inc(free[BANK[n]], 1)
                        if e == NX - 1:
                            dve.wait_ge(*taken(g, n))
                            dve.sem_inc(acc_done, 1)

                dve.tensor_copy(cur[:], idx[:, 0:G]).then_inc(cur_ready, 1)
                run(dve, "D", do_t, do_s, do_m)


_INS = ['x', 'L0_tok_emb', 'L0_tok_pos', 'L0_tok_wq', 'L0_tok_wk', 'L0_tok_wv', 'L0_tok_wo', 'L0_tok_wup', 'L0_tok_bup',
        'L0_tok_wdown', 'L0_tok_bdown', 'L0_tok_ga', 'L0_tok_ba', 'L0_tok_gm', 'L0_tok_bm', 'L0_attn_norm_weight',
        'L0_attn_w_q', 'L0_attn_w_k', 'L0_attn_w_v', 'L0_attn_w_f', 'L0_attn_gnorm_weight', 'L0_attn_w_o',
        'L0_ffn_router_w', 'L0_ffn_gate_w', 'L0_ffn_up_w', 'L0_ffn_down_w', 'L0_ffn_shared_gate_w',
        'L0_ffn_shared_up_w', 'L0_ffn_shared_down_w']


def kernel(**inputs):
    import numpy as _np
    import concourse.bacc as _bacc
    from concourse import mybir as _mybir
    from concourse.bass_utils import run_bass_kernel_spmd as _run

    nc = _bacc.Bacc("TRN2", target_bir_lowering=False, num_devices=1)
    arrays, args = {}, []
    for name in _INS:
        a = _np.ascontiguousarray(inputs[name])
        arrays[f"in_{name}"] = a
        args.append(nc.dram_tensor(f"in_{name}", a.shape, _mybir.dt.from_np(a.dtype), kind="ExternalInput").ap())
    seqs, steps = inputs["x"].shape
    width = inputs["L0_tok_emb"].shape[1]
    args.append(nc.dram_tensor("out_0", (seqs, steps, width), _mybir.dt.float32, kind="ExternalOutput").ap())
    build(nc, *args)
    r = _run(nc, [arrays], core_ids=[0])
    return r.results[0]["out_0"]
```

```python
from contextlib import ExitStack
from math import log2

import concourse.bass as bass
from concourse import mybir

F32 = mybir.dt.float32
F16 = mybir.dt.float16
I32 = mybir.dt.int32
ALU = mybir.AluOpType
ACT = mybir.ActivationFunctionType
AX = mybir.AxisListType.X

P = 128
G = 2
GT = G * P
EPS = 1e-5
WS = 64.0
IWS = 1.0 / WS
NEG = -1e30
GATE_NORM = 16.0
EXP_CLAMP = 80.0

LINKS = {"a": 21, "b": 21, "s": 33, "m": 5}



def layer_rows(l):
    rows = [("embed", (l,), [("D", 0.7)], []), ("gather", (l,), [("G", 2.1)], None)] if l == 0 else []
    rows += [("x", (l,), [("P", 0.4), ("A", 1.0), ("D", 0.6)], ["embed"] if l == 0 else []),
             ("t", (l,), [("P", 1.3), ("A", 0.5)], None),
             ("v", (l,), [("P", 1.3), ("D", 0.6)], ["x"]),
             ("sc", (l,), [("P", 0.9), ("D", 1.0)], ["t"]),
             ("sexp", (l,), [("A", 0.4)], None),
             ("pt", (l,), [("P", 0.2), ("D", 0.5)], None),
             ("z", (l,), [("P", 0.9), ("D", 0.8)], ["pt", "v"]),
             ("mstat", (l,), [("D", 1.5)], None), ("mroot", (l,), [("D", 1.4)], None), ("mnorm", (l,), [("D", 0.7)], None),
             ("mmul", (l,), [("G", 1.3)], None), ("mid", (l,), [("G", 1.3)], None),
             ("hr", (l,), [("G", 1.3)], None),
             ("y", (l,), [("P", 0.4), ("A", 1.0), ("D", 0.6)], ["mid"])]
    rows += [("up", (l, q), [("P", 1.3), ("A", 1.5), ("D", 0.6)],
              [f"up{q - 2}"] if q >= 2 else ["y", "b:dn"] if l == 0 else ["y"]) for q in range(4)]
    return rows + [("dn", (l,), [("P", 5.2), ("D", 0.6)], None),
                   ("ostat", (l,), [("D", 1.5)], None), ("oroot", (l,), [("D", 1.4)], None), ("onorm", (l,), [("D", 0.7)], None),
                   ("omul", (l,), [("G", 1.3)], ["onorm", "b:y", "b:hr"] if l == 0 else ["onorm", "s:res"]),
                   ("out", (l,), [("G", 1.3)], None)]


S_ROWS = [("nstat", (), [("D", 1.5)], []), ("nroot", (), [("D", 1.4)], None), ("norm", (), [("D", 0.7)], ["nroot", "m:mx"]),
          ("gx", (), [("P", 0.4), ("A", 1.0), ("D", 0.6)], None),
          ("qk", (), [("P", 2.6), ("A", 1.0), ("D", 1.2)], None),
          ("fv", (), [("P", 2.6), ("A", 1.1), ("D", 1.4)], ["qk", "m:acc"]),
          ("lnf", (), [("A", 3.6)], None),
          ("scores", (), [("P", 1.7), ("D", 1.2)], ["fv"]),
          ("g", (), [("D", 0.6)], ["lnf", "fv"]),
          ("gexp", (), [("A", 0.5)], None),
          ("decay", (), [("P", 0.9), ("D", 0.6)], ["g", "scores"]),
          ("dexp", (), [("A", 1.0)], None),
          ("slots", (), [("D", 1.3)], None),
          ("st", (), [("P", 0.4), ("A", 0.5)], None),
          ("gz", (), [("P", 1.7), ("D", 0.6)], None),
          ("zmax", (), [("D", 1.4)], None),
          ("zexp", (), [("A", 0.5)], None),
          ("pp", (), [("D", 0.6)], None),
          ("gp", (), [("P", 0.4), ("A", 0.5)], None),
          ("vscores", (), [("P", 1.7), ("D", 1.2)], None),
          ("zsum", (), [("D", 1.2)], ["zexp"]),
          ("o", (), [("P", 1.7), ("D", 0.6)], ["vscores", "zsum"]),
          ("otanh", (), [("A", 0.5)], None),
          ("osw", (), [("D", 0.6)], None),
          ("ssq", (), [("A", 0.8)], None),
          ("ot", (), [("P", 0.4), ("A", 1.0), ("D", 0.6)], ["osw"]),
          ("root", (), [("D", 1.6)], ["ssq"]),
          ("w", (), [("P", 1.3)], ["ot"]),
          ("res", (), [("D", 0.8)], ["w", "root"]),
          ("fstat", (), [("D", 1.5)], None), ("froot", (), [("D", 1.4)], None), ("fnorm", (), [("D", 0.7)], None)]


def moe_rows(start, end, NX):
    rows = []
    if start == 0:
        rows = [("mx", (), [("P", 0.4), ("A", 1.0), ("D", 0.6)], [f"n:down{NX - 1}"]),
                ("acc", (), [("G", 1.9)], [f"n:down{NX - 1}"]),
                ("router", (), [("P", 0.3), ("D", 0.9)], ["mx"]),
                ("rexp", (), [("A", 0.2)], None)]
    lo = start - 1 if start else 0
    for e in range(start, end):
        rows.append(("g", (e,), [("P", 1.3), ("A", 0.5)],
                     ["mx"] if e == 0 else ["glu0"] if e == 1 else [f"u{e - 1}"] if e > start else []))
        rows.append(("glu", (e,), [("D", 0.6)], [f"g{e}"] + ([f"split{e - 2}"] if e - 2 >= start else [])))
        rows.append(("u", (e,), [("P", 1.3), ("D", 0.6)], ["router"] if e == 0 else ["u0"] if e == 1 else [f"down{e - 2}"] if e - 2 >= lo else []))
        rows.append(("split", (e,), [("A", 0.5), ("G", 1.2)], None))
        if e == 0:
            rows.append(("gates", (), [("D", 0.7)], ["rexp"]))
        if e:
            rows.append(("down", (e - 1,), [("P", 1.3), ("D", 0.8)],
                         ([f"split{e - 1}"] if e - 1 >= start else []) + [f"glu{e}"] + (["gates", "acc"] if start == 0 else [])))
    if end == NX:
        rows.append(("down", (NX - 1,), [("P", 1.3), ("D", 0.8)], [f"split{NX - 1}"]))
    return rows


HOP = 0.2


def key_of(name, args, part):
    return name + (str(args[-1]) if name in ("up", "g", "glu", "u", "split", "down", "stage") and args else "")


PRIORITIES = [{"a": (0.61, -44.9), "b": (0.56, -30.1), "s": (0.35, 73.9), "m": (1.56, -56.6), "n": (0.2, 135.1), "w": (1, -100)},
              {"a": (1, -29), "b": (1, 28), "s": (1, 21), "m": (1, -20), "n": (1, 100), "w": (1, -100)},
              {"a": (1, -33), "b": (1, -26), "s": (1, 33), "m": (1, -23), "n": (1, 21), "w": (1, -100)},
              {"a": (1, 11), "b": (1, 20), "s": (1, 15), "m": (1, 28), "n": (1, 13), "w": (1, -100)}]


def plan(parts, priority):
    visits = {}
    rest, queue = {}, {}
    info = {}
    for part, rows in parts.items():
        above = None
        for name, args, steps, after in rows:
            key = key_of(name, args, part)
            for n, (eng, cost) in enumerate(steps):
                if n:
                    needs = [(part, key, n - 1)]
                else:
                    needs = []
                    for a in ([above] if after is None else after):
                        p, k = a.split(":") if ":" in a else (part, a)
                        if p in parts:
                            needs.append((p, k, None))
                visits[part, key, n] = [eng, cost, needs]
                info[part, key, n] = (part, name, args, eng)
                queue.setdefault((part, eng), []).append((part, key, n))
            above = key
    last = {}
    for part, key, n in visits:
        last[part, key] = max(n, last.get((part, key), 0))
    for v in visits.values():
        v[2] = [(p, k, last[p, k] if n is None else n) for p, k, n in v[2]]
    follow = {me: [] for me in visits}
    for me, (_, _, needs) in visits.items():
        for need in needs:
            follow[need].append(me)

    def way(me):
        if me not in rest:
            rest[me] = visits[me][1] + max((way(f) + HOP for f in follow[me]), default=0.0)
        return rest[me]

    for me in visits:
        way(me)
    free, end, order = {e: 0.0 for e in "PADG"}, {}, []
    while len(order) < len(visits):
        can = []
        for (part, eng), q in queue.items():
            if q and all(n in end for n in visits[q[0]][2]):
                start = max([free[eng]] + [end[n] + HOP for n in visits[q[0]][2]])
                can.append((start, -(priority[part][0] * rest[q[0]] + priority[part][1]), part, eng))
        soon = min(c[0] for c in can)
        _, start, part, eng = min((c[1], c[0], c[2], c[3]) for c in can if c[0] <= soon)
        me = queue[part, eng].pop(0)
        end[me] = free[eng] = start + visits[me][1]
        order.append(info[me])
    return max(end.values()), order


NEWTON, GUESS = {}, {}
for _last in (1.0, 0.5 * IWS):
    _c, _steps = _last, []
    for _ in range(3):
        _c = (0.5 * _c) ** (1.0 / 3.0)
        _steps.insert(0, _c)
    NEWTON[_last] = _steps
    GUESS[_last] = float(0x5f3759df - 2 ** 30) + log2(_c) * 2.0 ** 23


LAYER_USES = ["x", "t", "v", "sc", "pt", "z", "y", "up0", "up1", "up2", "up3", "dn"]
S_USES = ["gx", "q", "k", "fv0", "fv1", "A0", "A1", "D", "st", "gz", "gp", "B0", "B1", "o", "ot", "w"]


def m_uses(E):
    out = ["mx", "rl"]
    for name, args, _, _ in moe_rows(0, E, E):
        if name in ("g", "u"):
            out.append(f"{name}{args[0]}")
        elif name == "down":
            out.append(f"e{args[0]}")
    return out


def build(nc, x, emb, pos, wq, wk, wv, wo, wup, bup, wdown, bdown, ga, ba, gm, bm,
          norm_w, a_q, a_k, a_v, a_f, gnorm_w, a_o, router_w, gate_w, up_w, down_w, sg_w, su_w, sd_w, out):
    SEQS, T = x.shape
    V, D = emb.shape
    NL = wq.shape[0]
    F = wup.shape[2]
    NE = gate_w.shape[0]
    HEADS, DK = 4, 64
    KB = D // P
    FB = F // P
    NG = SEQS // G
    NX = NE + sg_w.shape[1] // D
    assert T == P and NL == 2 and KB == 2 and D == HEADS * DK and gate_w.shape[2] == D

    BANK, ORD, PER = {}, {}, [0] * 8
    for base, uses in ((0, [f"{n}.0" for n in LAYER_USES]), (2, [f"{n}.1" for n in LAYER_USES]), (4, S_USES),
                       (6, m_uses(NX))):
        for n, name in enumerate(uses):
            b = base + n % 2
            BANK[name], ORD[name] = b, PER[b]
            PER[b] += 1

    with ExitStack() as ctx:
        def sb(name, shape, dt=F32):
            return ctx.enter_context(nc.sbuf_tensor(name, shape, dt))

        def sem(name):
            return ctx.enter_context(nc.semaphore(name))

        bank = [ctx.enter_context(nc.psum_tensor(f"bank{b}", [P, 512], F32)) for b in range(8)]

        Wm = sb("Wm", [P, 2, NL, KB, D], F16)
        Wvo = sb("Wvo", [P, 2, NL, KB, D], F16)
        Wup = sb("Wup", [P, 2, NL, KB, F], F16)
        Wdn = sb("Wdn", [P, 2, NL, FB, D], F16)
        Wqk = sb("Wqk", [P, 2, 2, KB, D], F16)
        Wfv = sb("Wfv", [P, 2, KB, 2 * D], F16)
        Wao = sb("Wao", [P, 2, KB, D], F16)
        Wg = sb("Wg", [P, 2, NX, KB, D], F16)
        Wu = sb("Wu", [P, 2, NX, KB, D], F16)
        Wd = sb("Wd", [P, 2, NX, KB, D], F16)
        rw = sb("rw", [P, KB, NE])

        ident = sb("ident", [P, P])
        causal = sb("causal", [P, P])
        upper = sb("upper", [P, P])
        tri = sb("tri", [P, P])
        posb = sb("posb", [P, D])
        gb = sb("gb", [P, NL, 4, D])
        bdn = sb("bdn", [P, NL, D])
        bupc = sb("bupc", [P, NL, FB])
        nwc = sb("nwc", [P, 2, KB])
        idx = sb("idx", [P, SEQS + G], I32)
        cur = sb("cur", [P, G], I32)
        nws = sb("nws", [P, 2, KB])

        smax, nbias, rsum, rinv = ([sb(f"{n}{l}", [P, G]) for l in range(NL)] for n in ("smax", "nbias", "rsum", "rinv"))
        NORM = {p: [sb(f"{n}_{p}", [P, G, *d]) for n, d in (("stat", (6,)), ("mv", (2,)), ("vare", ()), ("rstd", ()), ("newt", ()))]
                for p in "abs"}
        zmax = sb("zmax", [P, G * HEADS])
        zsum = sb("zsum", [P, G * HEADS])
        ssq = sb("ssq", [P, G])
        lg = sb("lg", [P, G, NE])
        top = sb("top", [P, G, 8])
        ex = sb("ex", [P, G, NE])
        keep = sb("keep", [P, G, NE])
        esum = sb("esum", [P, G])
        comb = sb("comb", [P, G, NE])

        SLOT = 512
        arena = sb("arena", [P, 41 * SLOT])
        taken_slots = [0]

        def cut(n=1):
            a = taken_slots[0]
            taken_slots[0] += n
            return arena[:, a * SLOT:(a + n) * SLOT]

        def tok(ap):
            return ap.rearrange("p (j d) -> p j d", j=G)

        def feat(ap):
            return ap.rearrange("p (k t) -> p k t", k=KB)

        def pair(ap, n):
            return ap.bitcast(F16).rearrange("p (a k t) -> p a k t", a=2, k=n)

        EMB = tok(cut())
        H, U, VO = ([tok(cut()) for l in range(NL)] for _ in range(3))
        HTF, TT = ([feat(cut()) for l in range(NL)] for _ in range(2))
        HR = [tok(t.rearrange("p k t -> p (k t)")) for t in TT]
        HTP = [pair(cut(), KB) for l in range(NL)]
        sp_ = [cut() for l in range(NL)]
        SM = [a[:, 0:G * P].rearrange("p (j s) -> p j s", j=G) for a in sp_]
        PT = [a[:, G * P:2 * G * P].rearrange("p (j s) -> p j s", j=G) for a in sp_]
        RT = cut(2).rearrange("p (b m t) -> p b m t", b=2, m=2)
        AP = pair(cut(4), FB)
        HS, US, XS, VB, EB, PB = (tok(cut()) for _ in range(6))
        HO = US
        ZF, QT, KT = (feat(cut()) for _ in range(3))
        SPT = ZF
        PPT = QT
        ZP = pair(cut(), KB)
        AT = cut(2).rearrange("p (a c t) -> p a c t", a=2, c=4)
        BT = AT
        XP = pair(cut(), KB)
        ACC = tok(cut())
        ME = cut(2).rearrange("p (b t) -> p b t", b=2)
        MA = cut(2).rearrange("p (b t) -> p b t", b=2)
        XF = feat(MA[:, 0])
        MP = cut(2).rearrange("p (b t) -> p b t", b=2)
        MP = [pair(MP[:, b], 2) for b in range(2)]

        s_load = [sem(f"load{n}") for n in range(10)]
        s_const = sem("const_made")
        s_step = sem("setup_dve_step")
        s_ids = sem("ids_as_floats")
        s_nws = sem("norm_weights_scaled")
        s_idx = sem("ids_transposed")
        s_sfull = sem("setup_bank_full")
        s_shi = sem("setup_hi_made")
        s_slo = sem("setup_lo_made")
        s_rawt = sem("raw_transposed")
        stage_full = [sem(f"expert_stage_full{n}") for n in range(8)]
        stage_high = sem("expert_high_made")
        stage_low = sem("expert_low_made")
        full = [sem(f"bank_full{b}") for b in range(8)]
        free = [sem(f"bank_free{b}") for b in range(8)]
        cur_ready = sem("row_numbers_ready")
        emb_ready = sem("rows_gathered")
        h_ready = sem("h_embedded")
        ht_ready, nb_ready, p_ready, x_ready, mid_ready, hr_ready, a_ready, out_ready, pool_step = (
            [sem(f"{n}{l}") for l in range(NL)]
            for n in ("layer_operand_ready", "nbias_ready", "probs_ready", "layer_normed", "mid_affine_ready",
                      "residual_ready", "hidden_ready", "layer_out_ready", "pool_step"))
        xs_ready = sem("slot_normed")
        zt_ready = sem("slot_operand_ready")
        qe_ready = sem("q_tanh_ready")
        fa_step = sem("f_abs_exp_step")
        ve_ready = sem("v_tanh_ready")
        mn_ready = sem("f_min_ready")
        fl_ready = sem("f_log_ready")
        g_ready = sem("gate_ready")
        es_ready = sem("gate_exp_ready")
        ei_ready = sem("decay_inv_exp_ready")
        e_ready = sem("decay_exp_ready")
        sp_ready = sem("slots_ready")
        zs_ready = sem("z_shifted")
        ze_ready = sem("z_exp_ready")
        pp_ready = sem("slot_probs_ready")
        oe_ready = sem("o_tanh_ready")
        os_ready = sem("o_swished")
        sq_ready = sem("squares_summed")
        xm_ready = sem("moe_x_ready")
        acc_ready = sem("acc_started")
        rx_ready = sem("router_shifted")
        re_ready = sem("router_exp_ready")
        me_ready = sem("moe_tanh_ready")
        mhi_ready = sem("moe_hi_ready")
        mlo_ready = sem("moe_hidden_ready")
        acc_done = sem("acc_done")
        acc_free = sem("acc_free")
        out_done = sem("out_written")
        dve_step = {p: sem(f"dve_step_{p}") for p in "absm"}
        idle = sem("wait_holder")

        def passes(w, xp):
            return ((w[0], xp[0]), (w[0], xp[1]), (w[1], xp[0]))

        L_X, L_QKVO, L_ATT, L_UP, L_DN, L_ROWS, L_COLS = 0, 1, 3, 4, 6, 8, 9
        MAT = KB * D
        o_att = NL * 4 * MAT
        o_up = o_att + 5 * MAT
        o_dn = o_up + NL * KB * F
        o_end = o_dn + NL * FB * D
        ids = arena[0:SEQS, o_end:o_end + 3 * P].rearrange("p (a t) -> p a t", a=3)
        xi, xf, xneg = ids[:, 0].bitcast(I32), ids[:, 1], ids[:, 2]
        QKVO = [arena[:, l * 4 * MAT:(l + 1) * 4 * MAT].rearrange("p (w k d) -> p w k d", w=4, k=KB) for l in range(NL)]
        ATT = arena[:, o_att:o_up].rearrange("p (w k d) -> p w k d", w=5, k=KB)
        RUP = [arena[:, o_up + l * KB * F:o_up + (l + 1) * KB * F] for l in range(NL)]
        RDN = [arena[:, o_dn + l * FB * D:o_dn + (l + 1) * FB * D] for l in range(NL)]
        WX = (Wg, Wu, Wd)
        NSTAGE = 8
        STAGE = [arena[:, (taken_slots[0] - NSTAGE + n) * SLOT:(taken_slots[0] - NSTAGE + n) * SLOT + MAT] for n in range(NSTAGE)]
        assert MAT <= SLOT and o_end + 3 * P <= (taken_slots[0] - NSTAGE) * SLOT
        WT = Wg[:].rearrange("p a e k d -> p (a e k d)").bitcast(F32)[:, 0:NL * 3 * MAT].rearrange(
            "p (l w k d) -> p l w k d", l=NL, w=3, k=KB)

        def flat(ap):
            return ap.rearrange("p a b -> p (a b)")

        def att_dst(n, a, k):
            if n < 2:
                return Wqk[:, a, n, k]
            if n < 4:
                return Wfv[:, a, k, (n - 2) * D:(n - 1) * D]
            return Wao[:, a, k]

        cols = [(nwc[:, 0], norm_w), (nwc[:, 1], gnorm_w)]
        for l in range(NL):
            cols.append((bupc[:, l], bup[l]))

        def load_expert(sp, n):
            kind, e = divmod(n, NX)
            w, ws = ((gate_w, sg_w), (up_w, su_w), (down_w, sd_w))[kind]
            c = slice((e - NE) * D, (e - NE + 1) * D)
            src = w[e] if e < NE else ws[:, c] if kind < 2 else ws[c, :]
            sp.dma_start(STAGE[n % NSTAGE].rearrange("p (k d) -> p k d", k=KB),
                         src.rearrange("(k p) d -> p k d", p=P)).then_inc(stage_full[n % NSTAGE], 16)

        with nc.Block() as block:
            @block.sync
            def _(sp):
                sp.dma_start(xi, x).then_inc(s_load[L_X], 16)
                for l in range(NL):
                    for n, w in enumerate((wq, wk, wv, wo)):
                        sp.dma_start(QKVO[l][:, n], w[l].rearrange("(k p) d -> p k d", p=P)).then_inc(s_load[L_QKVO + l], 16)
                for n, w in enumerate((a_q, a_k, a_f, a_v, a_o)):
                    sp.dma_start(ATT[:, n], w.rearrange("(k p) d -> p k d", p=P)).then_inc(s_load[L_ATT], 16)
                for l in range(NL):
                    sp.dma_start(RUP[l].rearrange("p (k f) -> p k f", k=KB),
                                 wup[l].rearrange("(k p) f -> p k f", p=P)).then_inc(s_load[L_UP + l], 16)
                    sp.dma_start(RDN[l].rearrange("p (k d) -> p k d", k=FB),
                                 wdown[l].rearrange("(k p) d -> p k d", p=P)).then_inc(s_load[L_DN + l], 16)
                for n in range(NSTAGE):
                    load_expert(sp, n)

            @block.scalar
            def _(act):
                rows = [(posb[:], pos[0:P, :])]
                for l in range(NL):
                    rows += [(gb[:, l, n], w[l].partition_broadcast(P)) for n, w in enumerate((ga, ba, gm, bm))]
                    rows.append((bdn[:, l], bdown[l].partition_broadcast(P)))
                for dst, src in rows:
                    act.dma_start(dst, src).then_inc(s_load[L_ROWS], 16)
                for dst, src in cols:
                    act.dma_start(dst, src.rearrange("(k p) -> p k", p=P),
                                  allow_slow_non_contiguous=True).then_inc(s_load[L_COLS], 16)
                act.dma_start(rw[:], router_w.rearrange("(k p) e -> p k e", p=P)).then_inc(s_load[L_COLS], 16)
                for l in range(NL):
                    act.wait_ge(s_load[L_UP + l], 16)
                    act.activation(flat(Wup[:, 0, l]), RUP[l], ACT.Copy, scale=WS).then_inc(s_shi, 1)
                    act.wait_ge(s_load[L_DN + l], 16)
                    act.activation(flat(Wdn[:, 0, l]), RDN[l], ACT.Copy, scale=WS).then_inc(s_shi, 1)
                for n in range(3 * NL):
                    act.wait_ge(s_sfull, 2 + n)
                    act.activation(flat(WT[:, n // 3, n % 3]), bank[1 + n][:], ACT.Copy).then_inc(s_rawt, 1)
                act.wait_ge(s_nws, 1)
                for n in range(5):
                    act.wait_ge(s_sfull, 8 + n)
                    for k in range(KB):
                        i = act.activation(att_dst(n, 0, k), bank[(7 + n) % 8][:, k * D:(k + 1) * D], ACT.Identity,
                                           scale=nws[:, n // 4, k:k + 1])
                    i.then_inc(s_shi, 1)
                for n in range(2 * NL):
                    act.wait_ge(s_sfull, 13 + n)
                    act.activation(flat((Wm, Wvo)[n % 2][:, 0, n // 2]), bank[(12 + n) % 8][:], ACT.Copy,
                                   scale=WS).then_inc(s_shi, 1)

            @block.gpsimd
            def _(pool):
                pool.memset(ident[:], 0.0).then_inc(s_const, 1)
                pool.memset(causal[:], 0.0).then_inc(s_const, 1)
                pool.memset(upper[:], 1.0).then_inc(s_const, 1)
                pool.wait_ge(s_const, 3)
                pool.affine_select(out=ident[:], in_=ident[:], compare_op=ALU.not_equal, fill=1.0, base=0,
                                   pattern=[[-1, P]], channel_multiplier=1).then_inc(s_const, 1)
                pool.affine_select(out=causal[:], in_=causal[:], compare_op=ALU.is_ge, fill=NEG, base=0,
                                   pattern=[[-1, P]], channel_multiplier=1).then_inc(s_const, 1)
                pool.affine_select(out=upper[:], in_=upper[:], compare_op=ALU.is_ge, fill=0.0, base=0,
                                   pattern=[[1, P]], channel_multiplier=-1).then_inc(s_const, 1)
                pool.wait_ge(s_load[L_ROWS], 16 * (1 + 5 * NL))

            @block.vector
            def _(dve):
                steps = [0]

                def link(ins):
                    steps[0] += 1
                    ins.then_inc(s_step, 1)
                    dve.wait_ge(s_step, steps[0])

                dve.wait_ge(s_load[L_X], 16)
                link(dve.tensor_copy(xf, xi))
                link(dve.tensor_scalar(xneg, xf, 0.0, float(V), ALU.is_lt, ALU.mult))
                link(dve.tensor_tensor(xf, xf, xneg, ALU.add))
                dve.tensor_scalar(xf, xf, 0.0, float(V - 1), ALU.max, ALU.min).then_inc(s_ids, 1)
                dve.memset(idx[:, SEQS:SEQS + G], 0)
                dve.wait_ge(s_const, 6)
                dve.tensor_scalar(tri[:], upper[:], upper[:, P // 2 - 1:P // 2], None, ALU.subtract)
                dve.wait_ge(s_load[L_COLS], 16 * (len(cols) + 1))
                dve.tensor_scalar(nws[:], nwc[:], WS, None, ALU.mult).then_inc(s_nws, 1)
                dve.wait_ge(s_sfull, 1)
                dve.tensor_copy(idx[:, 0:SEQS], bank[0][:, 0:SEQS]).then_inc(s_idx, 1)
                for n in range(2 * NL):
                    l = n // 2
                    w, raw = (Wdn, RDN[l]) if n % 2 else (Wup, RUP[l])
                    dve.wait_ge(s_shi, n + 1)
                    dve.scalar_tensor_tensor(flat(w[:, 1, l]), raw, WS, flat(w[:, 0, l]), ALU.mult, ALU.subtract).then_inc(s_slo, 1)
                dve.wait_ge(s_nws, 1)
                for n in range(5):
                    dve.wait_ge(s_shi, 2 * NL + n + 1)
                    for k in range(KB):
                        i = dve.scalar_tensor_tensor(att_dst(n, 1, k), bank[(7 + n) % 8][:, k * D:(k + 1) * D],
                                                     nws[:, n // 4, k:k + 1], att_dst(n, 0, k), ALU.mult, ALU.subtract)
                    i.then_inc(s_slo, 1)
                for n in range(2 * NL):
                    w = (Wm, Wvo)[n % 2]
                    dve.wait_ge(s_shi, 2 * NL + 5 + n + 1)
                    dve.scalar_tensor_tensor(flat(w[:, 1, n // 2]), bank[(12 + n) % 8][:], WS, flat(w[:, 0, n // 2]),
                                             ALU.mult, ALU.subtract).then_inc(s_slo, 1)

            @block.tensor
            def _(pe):
                pe.wait_ge(s_const, 6)
                pe.wait_ge(s_ids, 1)
                pe.transpose(bank[0][:, 0:SEQS], xf, ident[0:SEQS, 0:SEQS]).then_inc(s_sfull, 1)

                def turn(src, b):
                    for kk in range(KB):
                        for k in range(KB):
                            i = pe.transpose(bank[b][:, kk * D + k * P:kk * D + (k + 1) * P],
                                             src[:, k, kk * P:(kk + 1) * P], ident[:])
                    i.then_inc(s_sfull, 1)

                for n in range(3 * NL):
                    if n % 3 == 0:
                        pe.wait_ge(s_load[L_QKVO + n // 3], 64)
                    turn(QKVO[n // 3][:, n % 3], 1 + n)
                pe.wait_ge(s_load[L_ATT], 80)
                for n in range(5):
                    if n == 1:
                        pe.wait_ge(s_idx, 1)
                        pe.wait_ge(s_rawt, 3 * NL)
                    turn(ATT[:, n], (7 + n) % 8)
                for n in range(2 * NL):
                    l, w = divmod(n, 2)
                    if n == 3:
                        pe.wait_ge(s_slo, 2 * NL + 1)
                    b = bank[(12 + n) % 8]
                    for k in range(KB):
                        for c in range(KB):
                            lhs = WT[:, l, 2 * w, c, k * P:(k + 1) * P]
                            rhs = QKVO[l][:, 3, c] if w else WT[:, l, 1, c]
                            i = pe.matmul(b[:, k * D:(k + 1) * D], lhs, rhs, start=(c == 0), stop=(c == KB - 1))
                    i.then_inc(s_sfull, 1)

        ROWS = {"a": layer_rows(0), "b": layer_rows(1), "s": S_ROWS, "m": moe_rows(0, NE, NX), "n": moe_rows(NE, NX, NX),
                "w": [("stage", (n,), [("A", 0.5), ("D", 0.6)], []) for n in range(NX)]}
        LAG = {"w": 0} | {p: n for n, p in enumerate("absmn")}
        assert len(WX) == LAG["m"]
        ORDER = {}

        def nothing(g, name, n):
            pass

        def run(eng, letter, do_t, do_s, do_m, do_w=nothing):
            do = {"a": do_t, "b": do_t, "s": do_s, "m": do_m, "n": do_m, "w": do_w}

            def steps(parts, g):
                if parts not in ORDER:
                    some = PRIORITIES[:1] if parts == "absmn" else PRIORITIES
                    ORDER[parts] = min((plan({p: ROWS[p] for p in parts}, y) for y in some), key=lambda c: c[0])[1]
                for part, name, args, at in ORDER[parts]:
                    if at == letter:
                        do[part](g - LAG[part], name, *args)

            for n in range(4):
                steps("absmn"[:n + 1] + "w" * (n < LAG["m"]), n)
            with eng.Fori(4, NG) as g:
                steps("absmn", g)
            for n in range(4):
                steps("absmn"[n + 1:], NG + n)

        def filled(g, name):
            return full[BANK[name]], PER[BANK[name]] * g + ORD[name] + 1

        def vacant(g, name):
            return free[BANK[name]], PER[BANK[name]] * g + ORD[name] + 1

        def taken(g, name):
            return free[BANK[name]], PER[BANK[name]] * g + ORD[name] + 2

        def ps(name):
            return bank[BANK[name]]

        def first(g):
            return isinstance(g, int) and g == 0

        with nc.Block() as block:
            @block.sync
            def _(sp):
                def store(g):
                    sp.wait_ge(acc_done, g + 1)
                    sp.dma_start(out[bass.ds(g * G, G)].rearrange("s t d -> t s d"), ACC).then_inc(out_done, 16)
                    sp.wait_ge(out_done, 16 * g + 16)
                    sp.sem_inc(acc_free, 1)

                for n in range(NSTAGE, len(WX) * NX):
                    sp.wait_ge(stage_low, n - NSTAGE + 1)
                    load_expert(sp, n)
                sp.sem_inc(acc_free, 1)
                with sp.Fori(0, NG) as g:
                    store(g)

            @block.tensor
            def _(pe):
                def products(dst, pairs):
                    for n, (lhs, rhs) in enumerate(pairs):
                        i = pe.matmul(dst, lhs, rhs, start=(n == 0), stop=(n == len(pairs) - 1))
                    return i

                def by_feature(dst, w, xp, m):
                    return products(dst, [(wa[:, k, m * P:(m + 1) * P], xa[:, k])
                                          for k in range(w[0].shape[1]) for wa, xa in passes(w, xp)])

                def by_token(dst, w, xp, j):
                    return products(dst, [(xa[:, k, j * P:(j + 1) * P], wa[:, k])
                                          for k in range(w[0].shape[1]) for wa, xa in passes(w, xp)])

                def both(ap):
                    return ap[:, 0], ap[:, 1]

                def turn(g, src, name):
                    pe.wait_ge(*vacant(g, name))
                    for k in range(KB):
                        for j in range(G):
                            i = pe.transpose(ps(name)[:, k * GT + j * P:k * GT + (j + 1) * P], src[:, j, k * P:(k + 1) * P],
                                             ident[:])
                    i.then_inc(full[BANK[name]], 1)

                HT2, Z2, X2 = [both(h) for h in HTP], both(ZP), both(XP)

                def do_t(g, name, l, q=None):
                    n = f"{name}.{l}"
                    if name == "x":
                        pe.wait_ge((h_ready, out_ready[0])[l], g + 1)
                        turn(g, H[l], n)
                    elif name == "t":
                        pe.wait_ge(ht_ready[l], 2 * g + 1)
                        pe.wait_ge(*vacant(g, n))
                        for m in range(KB):
                            i = by_feature(ps(n)[:, m * GT:(m + 1) * GT], both(Wm[:, :, l]), HT2[l], m)
                        i.then_inc(full[BANK[n]], 1)
                    elif name == "v":
                        pe.wait_ge(*vacant(g, n))
                        for j in range(G):
                            i = by_token(ps(n)[:, j * D:(j + 1) * D], both(Wvo[:, :, l]), HT2[l], j)
                        i.then_inc(full[BANK[n]], 1)
                    elif name == "sc":
                        pe.wait_ge(*taken(g, f"t.{l}"))
                        pe.wait_ge(*vacant(g, n))
                        for j in range(G):
                            js = slice(j * P, (j + 1) * P)
                            i = products(ps(n)[:, js], [(TT[l][:, k, js], HTF[l][:, k, js]) for k in range(KB)])
                        i.then_inc(full[BANK[n]], 1)
                    elif name == "pt":
                        pe.wait_ge(p_ready[l], g + 1)
                        pe.wait_ge(*vacant(g, n))
                        for j in range(G):
                            i = pe.transpose(ps(n)[:, j * P:(j + 1) * P], SM[l][:, j], ident[:])
                        i.then_inc(full[BANK[n]], 1)
                    elif name == "z":
                        pe.wait_ge(*taken(g, f"pt.{l}"))
                        pe.wait_ge(*taken(g, f"v.{l}"))
                        pe.wait_ge(*vacant(g, n))
                        for j in range(G):
                            i = pe.matmul(ps(n)[:, j * D:(j + 1) * D], PT[l][:, j], VO[l][:, j], start=True, stop=True)
                        i.then_inc(full[BANK[n]], 1)
                    elif name == "y":
                        pe.wait_ge(mid_ready[l], g + 1)
                        turn(g, H[l], n)
                    elif name == "up":
                        n = f"up{q}.{l}"
                        if q == 0:
                            pe.wait_ge(ht_ready[l], 2 * g + 2)
                        pe.wait_ge(*vacant(g, n))
                        for m in range(2):
                            i = by_feature(ps(n)[:, m * GT:(m + 1) * GT], both(Wup[:, :, l]), HT2[l], 2 * q + m)
                        i.then_inc(full[BANK[n]], 1)
                    elif name == "dn":
                        pe.wait_ge(a_ready[l], 4 * g + 4)
                        pe.wait_ge(*vacant(g, n))
                        for j in range(G):
                            i = by_token(ps(n)[:, j * D:(j + 1) * D], both(Wdn[:, :, l]), both(AP), j)
                        i.then_inc(full[BANK[n]], 1)

                def do_s(g, name):
                    if name == "gx":
                        pe.wait_ge(xs_ready, 2 * g + 1)
                        turn(g, XS, "gx")
                    elif name == "qk":
                        pe.wait_ge(zt_ready, 2 * g + 1)
                        for c, n in enumerate("qk"):
                            pe.wait_ge(*vacant(g, n))
                            for m in range(KB):
                                i = by_feature(ps(n)[:, m * GT:(m + 1) * GT], both(Wqk[:, :, c]), Z2, m)
                            i.then_inc(full[BANK[n]], 1)
                    elif name == "fv":
                        for j in range(G):
                            pe.wait_ge(*vacant(g, f"fv{j}"))
                            by_token(ps(f"fv{j}")[:], both(Wfv), Z2, j).then_inc(full[BANK[f"fv{j}"]], 1)
                    elif name == "decay":
                        pe.wait_ge(g_ready, g + 1)
                        pe.wait_ge(*vacant(g, "D"))
                        for j in range(G):
                            i = pe.matmul(ps("D")[:, j * D:(j + 1) * D], tri[:], US[:, j], start=True, stop=True)
                        i.then_inc(full[BANK["D"]], 1)
                    elif name in ("scores", "vscores"):
                        if name == "scores":
                            stem, left, right = "A", KT, QT
                            pe.wait_ge(*taken(g, "q"))
                            pe.wait_ge(*taken(g, "k"))
                        else:
                            stem, left, right = "B", SPT, PPT
                            pe.wait_ge(*taken(g, "st"))
                            pe.wait_ge(*taken(g, "gp"))
                        for par in range(2):
                            pe.wait_ge(*vacant(g, f"{stem}{par}"))
                        for j in range(G):
                            js = slice(j * P, (j + 1) * P)
                            for hc in range(2):
                                for par in range(2):
                                    n = f"{stem}{par}"
                                    c = j * 2 + hc
                                    rows = slice(par * DK, (par + 1) * DK)
                                    i = pe.matmul(ps(n)[:, c * P:(c + 1) * P], left[rows, hc, js], right[rows, hc, js],
                                                  start=True, stop=True)
                                    if c == 3:
                                        i.then_inc(full[BANK[n]], 1)
                    elif name == "st":
                        pe.wait_ge(sp_ready, g + 1)
                        turn(g, XS, "st")
                    elif name in ("gz", "o"):
                        if name == "gz":
                            left, right = AT, XS
                            pe.wait_ge(*taken(g, "A0"))
                            pe.wait_ge(*taken(g, "A1"))
                        else:
                            left, right = BT, VB
                            pe.wait_ge(*taken(g, "B0"))
                            pe.wait_ge(*taken(g, "B1"))
                            pe.wait_ge(*taken(g, "fv1"))
                        pe.wait_ge(*vacant(g, name))
                        for j in range(G):
                            for h in range(HEADS):
                                c = j * HEADS + h
                                i = pe.matmul(ps(name)[:, c * DK:(c + 1) * DK], left[:, h % 2, j * 2 + h // 2],
                                              right[:, j, h * DK:(h + 1) * DK], start=True, stop=True)
                        i.then_inc(full[BANK[name]], 1)
                    elif name == "gp":
                        pe.wait_ge(pp_ready, g + 1)
                        turn(g, EB, "gp")
                    elif name == "ot":
                        pe.wait_ge(os_ready, g + 1)
                        turn(g, US, "ot")
                    elif name == "w":
                        pe.wait_ge(zt_ready, 2 * g + 2)
                        pe.wait_ge(*vacant(g, "w"))
                        for j in range(G):
                            i = by_token(ps("w")[:, j * D:(j + 1) * D], both(Wao), Z2, j)
                        i.then_inc(full[BANK["w"]], 1)

                def do_m(g, name, e=None):
                    if name == "mx":
                        if first(g):
                            pe.wait_ge(stage_low, len(WX) * NX)
                        pe.wait_ge(xs_ready, 2 * g + 2)
                        turn(g, XS, "mx")
                    elif name == "router":
                        pe.wait_ge(*taken(g, "mx"))
                        pe.wait_ge(xm_ready, g + 1)
                        pe.wait_ge(*vacant(g, "rl"))
                        for j in range(G):
                            i = products(ps("rl")[:, j * NE:(j + 1) * NE],
                                         [(XF[:, k, j * P:(j + 1) * P], rw[:, k]) for k in range(KB)])
                        i.then_inc(full[BANK["rl"]], 1)
                    elif name in ("g", "u"):
                        n, w = f"{name}{e}", Wg if name == "g" else Wu
                        pe.wait_ge(*vacant(g, n))
                        for m in range(2):
                            i = by_feature(ps(n)[:, m * GT:(m + 1) * GT], both(w[:, :, e]), X2, m)
                        i.then_inc(full[BANK[n]], 1)
                    elif name == "down":
                        n = f"e{e}"
                        pe.wait_ge(mlo_ready, NX * g + e + 1)
                        pe.wait_ge(*vacant(g, n))
                        for j in range(G):
                            i = by_token(ps(n)[:, j * D:(j + 1) * D], both(Wd[:, :, e]), both(MP[e % 2]), j)
                        i.then_inc(full[BANK[n]], 1)

                for b in range(8):
                    pe.sem_inc(free[b], 1)
                run(pe, "P", do_t, do_s, do_m)

            @block.scalar
            def _(act):
                def take(g, name, dst, **kw):
                    act.wait_ge(*filled(g, name))
                    act.activation(dst, ps(name)[:], ACT.Copy, **kw).then_inc(free[BANK[name]], 1)

                def take_pair(g, name, dst, hi):
                    act.wait_ge(*filled(g, name))
                    act.activation(flat(dst), ps(name)[:], ACT.Copy)
                    act.activation(flat(hi), ps(name)[:], ACT.Copy).then_inc(free[BANK[name]], 1)

                def do_t(g, name, l, q=None):
                    n = f"{name}.{l}"
                    if name in ("x", "y"):
                        take_pair(g, n, HTF[l], HTP[l][:, 0])
                    elif name == "t":
                        take(g, n, flat(TT[l]), scale=IWS)
                    elif name == "sexp":
                        act.wait_ge(nb_ready[l], g + 1)
                        for j in range(G):
                            i = act.activation(SM[l][:, j], SM[l][:, j], ACT.Exp, bias=nbias[l][:, j:j + 1],
                                               scale=1.0 / D ** 0.5, accum_out=rsum[l][:, j:j + 1])
                        i.then_inc(p_ready[l], 1)
                    elif name == "up":
                        n = f"up{q}.{l}"
                        if q == 0 and l == 0 and not first(g):
                            act.wait_ge(*filled(g - 1, "dn.1"))
                        act.wait_ge(*filled(g, n))
                        if q >= 2:
                            act.wait_ge(a_ready[l], 4 * g + q - 1)
                        for dst in (RT[:, q % 2], AP[:, 0, 2 * q:2 * q + 2]):
                            for m in range(2):
                                i = act.activation(dst[:, m], ps(n)[:, m * GT:(m + 1) * GT], ACT.Relu, scale=IWS,
                                                   bias=bupc[:, l, 2 * q + m:2 * q + m + 1])
                        i.then_inc(free[BANK[n]], 1)

                def do_s(g, name):
                    if name in ("gx", "ot"):
                        take_pair(g, name, ZF, ZP[:, 0])
                    elif name == "qk":
                        for n, dst in (("q", EB), ("k", PB)):
                            act.wait_ge(*filled(g, n))
                            act.activation(flat(dst), ps(n)[:], ACT.Tanh, scale=0.5 * IWS).then_inc(qe_ready, 1)
                    elif name == "fv":
                        act.wait_ge(*taken(g, "q"))
                        act.wait_ge(*taken(g, "k"))
                        for j in range(G):
                            act.wait_ge(*filled(g, f"fv{j}"))
                            act.activation(PB[:, j], ps(f"fv{j}")[:, 0:D], ACT.Abs, scale=IWS).then_inc(fa_step, 1)
                            act.activation(EB[:, j], ps(f"fv{j}")[:, D:2 * D], ACT.Tanh, scale=0.5 * IWS).then_inc(ve_ready, 1)
                    elif name == "lnf":
                        act.wait_ge(fa_step, (G + 1) * g + G)
                        act.activation(flat(PB), flat(PB), ACT.Exp, scale=-1.0).then_inc(fa_step, 1)
                        act.wait_ge(fa_step, (G + 1) * g + G + 1)
                        act.activation(flat(PB), flat(PB), ACT.Ln, bias=1.0).then_inc(fl_ready, 1)
                    elif name == "gexp":
                        act.wait_ge(g_ready, g + 1)
                        act.activation(flat(XS), flat(US), ACT.Exp, scale=1.0 / GATE_NORM).then_inc(es_ready, 1)
                    elif name == "dexp":
                        act.wait_ge(*taken(g, "D"))
                        act.activation(flat(PB), flat(EB), ACT.Exp, scale=-1.0 / GATE_NORM).then_inc(ei_ready, 1)
                        act.activation(flat(EB), flat(EB), ACT.Exp, scale=1.0 / GATE_NORM).then_inc(e_ready, 1)
                    elif name == "st":
                        take(g, "st", flat(SPT))
                    elif name == "zexp":
                        act.wait_ge(zs_ready, g + 1)
                        act.activation(flat(PB), flat(PB), ACT.Exp).then_inc(ze_ready, 1)
                    elif name == "gp":
                        take(g, "gp", flat(PPT))
                    elif name == "otanh":
                        act.wait_ge(*taken(g, "o"))
                        act.activation(flat(EB), flat(US), ACT.Tanh, scale=0.5).then_inc(oe_ready, 1)
                    elif name == "ssq":
                        act.wait_ge(os_ready, g + 1)
                        for j in range(G):
                            i = act.activation(PB[:, j], US[:, j], ACT.Square, scale=0.5, accum_out=ssq[:, j:j + 1])
                        i.then_inc(sq_ready, 1)

                def high(g, e):
                    act.wait_ge(*taken(g, f"u{e}"))
                    if e >= 2:
                        act.wait_ge(*filled(g, f"e{e - 2}"))
                    act.activation(flat(MP[e % 2][:, 0]), MA[:, e % 2], ACT.Copy).then_inc(mhi_ready, 1)

                def do_m(g, name, e=None):
                    if name == "mx":
                        if first(g):
                            act.wait_ge(stage_low, len(WX) * NX)
                        take_pair(g, "mx", XF, XP[:, 0])
                    elif name == "rexp":
                        act.wait_ge(rx_ready, g + 1)
                        act.activation(ex[:], ex[:], ACT.Exp).then_inc(re_ready, 1)
                    elif name == "g":
                        act.wait_ge(*filled(g, f"g{e}"))
                        act.activation(ME[:, e % 2], ps(f"g{e}")[:], ACT.Tanh, scale=0.5 * IWS).then_inc(me_ready, 1)
                    elif name == "split":
                        high(g, e)

                def do_w(g, name, n):
                    n += NX * g
                    act.wait_ge(stage_full[n % NSTAGE], 16 * (n // NSTAGE) + 16)
                    act.activation(flat(WX[g][:, 0, n % NX]), STAGE[n % NSTAGE], ACT.Copy, scale=WS).then_inc(stage_high, 1)

                run(act, "A", do_t, do_s, do_m, do_w)

            @block.gpsimd
            def _(pool):
                def rows(ap):
                    return ap.to_broadcast([P, G, D])

                def gather():
                    for j in range(G):
                        pool.indirect_dma_start(EMB[:, j], None, emb, bass.IndirectOffsetOnAxis(cur[:, j:j + 1], 0)).then_inc(emb_ready, 16)

                def affine_mul(g, dst, l, n):
                    pool.wait_ge(x_ready[l], 2 * g + n + 1)
                    pool.tensor_tensor(dst, U[l], rows(gb[:, l, 2 * n:2 * n + 1]), ALU.mult).then_inc(pool_step[l], 1)

                def affine_add(g, dst, l, n, done):
                    pool.wait_ge(pool_step[l], 2 * g + n + 1)
                    pool.tensor_tensor(dst, dst, rows(gb[:, l, 2 * n + 1:2 * n + 2]), ALU.add).then_inc(done[l], 1)

                def do_t(g, name, l, q=None):
                    if name == "gather":
                        pool.wait_ge(cur_ready, g + 2)
                        pool.sem_inc(idle, 1)
                        gather()
                    elif name == "mmul":
                        affine_mul(g, H[l], l, 0)
                    elif name == "mid":
                        affine_add(g, H[l], l, 0, mid_ready)
                    elif name == "hr":
                        pool.wait_ge(mid_ready[l], g + 1)
                        pool.tensor_tensor(HR[l], H[l], rows(bdn[:, l:l + 1]), ALU.add).then_inc(hr_ready[l], 1)
                    elif name == "omul":
                        if not first(g):
                            if l == 0:
                                pool.wait_ge(*filled(g - 1, "y.1"))
                            else:
                                pool.wait_ge(*taken(g - 1, "w"))
                        affine_mul(g, (H[1], HS)[l], l, 1)
                    elif name == "out":
                        affine_add(g, (H[1], HS)[l], l, 1, out_ready)

                def do_s(g, name):
                    pass

                def low(g, e):
                    pool.wait_ge(mhi_ready, NX * g + e + 1)
                    pool.tensor_tensor(flat(MP[e % 2][:, 1]), MA[:, e % 2], flat(MP[e % 2][:, 0]), ALU.subtract).then_inc(mlo_ready, 1)

                def do_m(g, name, e=None):
                    if name == "acc":
                        if first(g):
                            pool.wait_ge(stage_low, len(WX) * NX)
                            pool.sem_inc(idle, 1)
                        pool.wait_ge(*taken(g, "w"))
                        pool.sem_inc(idle, 1)
                        pool.wait_ge(acc_free, g + 1)
                        pool.sem_inc(idle, 1)
                        pool.tensor_copy(ACC, HO).then_inc(acc_ready, 1)
                    elif name == "split":
                        low(g, e)

                pool.wait_ge(cur_ready, 1)
                gather()
                run(pool, "G", do_t, do_s, do_m)
                pool.wait_ge(emb_ready, 16 * G * (NG + 1))

            @block.vector
            def _(dve):
                count = dict.fromkeys(LINKS, 0)

                def mark(part, ins):
                    count[part] += 1
                    ins.then_inc(dve_step[part], 1)

                def need(part, g):
                    dve.wait_ge(dve_step[part], LINKS[part] * g + count[part])

                def link(part, g, ins):
                    mark(part, ins)
                    need(part, g)

                def close(part):
                    assert count[part] == LINKS[part], (part, count[part])
                    count[part] = 0

                def guess(part, last):
                    _, _, vare, rstd, _ = NORM[part]
                    mark(part, dve.tensor_scalar(rstd[:].bitcast(I32), vare[:].bitcast(I32), -0.5, GUESS[last],
                                                 ALU.mult, ALU.add))

                def root(part, g, last):
                    _, _, vare, rstd, newt = NORM[part]
                    need(part, g)
                    for c in NEWTON[last]:
                        for j in range(G):
                            i = dve.scalar_tensor_tensor(newt[:, j:j + 1], rstd[:, j:j + 1], vare[:, j:j + 1], rstd[:, j:j + 1],
                                                         ALU.mult, ALU.mult)
                        link(part, g, i)
                        mark(part, dve.scalar_tensor_tensor(rstd[:], newt[:], 3.0 * c * c, rstd[:], ALU.add, ALU.mult))
                        if c != NEWTON[last][-1]:
                            need(part, g)

                def stats(part, g, src, mul=1.0, add=EPS):
                    stat, mv, vare, _, _ = NORM[part]
                    for j in range(G):
                        i = dve.bn_stats(stat[:, j], src[:, j])
                    link(part, g, i)
                    dve.sem_inc(idle, 1)
                    for j in range(G):
                        i = dve.bn_aggr(mv[:, j], stat[:, j])
                    link(part, g, i)
                    link(part, g, dve.tensor_scalar(vare[:], mv[:, :, 1], -mul, -add, ALU.mult, ALU.add))
                    guess(part, 1.0)

                def apply(part, g, src, dst, done):
                    _, mv, _, rstd, _ = NORM[part]
                    need(part, g)
                    for j in range(G):
                        i = dve.tensor_scalar(dst[:, j], src[:, j], mv[:, j, 0:1], rstd[:, j:j + 1], ALU.subtract, ALU.mult)
                    i.then_inc(done, 1)

                def low(g, name, F, Pr, done):
                    dve.wait_ge(*taken(g, name))
                    dve.tensor_tensor(flat(Pr[:, 1]), flat(F), flat(Pr[:, 0]), ALU.subtract).then_inc(done, 1)

                def do_t(g, name, l, q=None):
                    n = f"{name}.{l}"
                    part = "ab"[l]
                    if name == "embed":
                        dve.wait_ge(emb_ready, 16 * G * g + 16 * G)
                        dve.tensor_tensor(H[0], EMB, posb[:, None, :].to_broadcast([P, G, D]), ALU.add).then_inc(h_ready, 1)
                        dve.tensor_copy(cur[:], idx[:, bass.ds(G * g + G, G)]).then_inc(cur_ready, 1)
                    elif name in ("x", "y"):
                        low(g, n, HTF[l], HTP[l], ht_ready[l])
                    elif name == "v":
                        dve.wait_ge(*filled(g, n))
                        dve.tensor_scalar(flat(VO[l]), ps(n)[:], IWS, None, ALU.mult).then_inc(free[BANK[n]], 1)
                    elif name == "sc":
                        dve.wait_ge(*filled(g, n))
                        dve.tensor_tensor(SM[l], ps(n)[:, 0:G * P].rearrange("p (j s) -> p j s", j=G),
                                          causal[:, None, :].to_broadcast([P, G, P]), ALU.add).then_inc(free[BANK[n]], 1)
                        dve.wait_ge(*taken(g, n))
                        link(part, g, dve.tensor_reduce(smax[l][:], SM[l], AX, ALU.max))
                        dve.tensor_scalar(nbias[l][:], smax[l][:], -1.0 / D ** 0.5, None, ALU.mult).then_inc(nb_ready[l], 1)
                    elif name == "pt":
                        dve.wait_ge(p_ready[l], g + 1)
                        dve.reciprocal(rinv[l][:], rsum[l][:])
                        dve.wait_ge(*filled(g, n))
                        dve.tensor_copy(flat(PT[l]), ps(n)[:, 0:G * P]).then_inc(free[BANK[n]], 1)
                    elif name == "z":
                        if not first(g):
                            dve.wait_ge(out_ready[l], g)
                        dve.wait_ge((h_ready, out_ready[0])[l], g + 1)
                        dve.wait_ge(*taken(g, f"pt.{l}"))
                        dve.wait_ge(*filled(g, n))
                        for j in range(G):
                            i = dve.scalar_tensor_tensor(U[l][:, j], ps(n)[:, j * D:(j + 1) * D], rinv[l][:, j:j + 1],
                                                         H[l][:, j], ALU.mult, ALU.add)
                        i.then_inc(free[BANK[n]], 1)
                    elif name == "mstat":
                        dve.wait_ge(*taken(g, f"z.{l}"))
                        stats(part, g, U[l])
                    elif name in ("mroot", "oroot"):
                        root(part, g, 1.0)
                    elif name == "mnorm":
                        apply(part, g, U[l], U[l], x_ready[l])
                    elif name == "up":
                        dve.wait_ge(*taken(g, f"up{q}.{l}"))
                        dve.tensor_tensor(flat(AP[:, 1, 2 * q:2 * q + 2]), flat(RT[:, q % 2]), flat(AP[:, 0, 2 * q:2 * q + 2]),
                                          ALU.subtract).then_inc(a_ready[l], 1)
                    elif name == "dn":
                        dve.wait_ge(hr_ready[l], g + 1)
                        dve.wait_ge(*filled(g, n))
                        dve.scalar_tensor_tensor(flat(U[l]), ps(n)[:], IWS, flat(HR[l]), ALU.mult,
                                                 ALU.add).then_inc(free[BANK[n]], 1)
                    elif name == "ostat":
                        dve.wait_ge(*taken(g, f"dn.{l}"))
                        stats(part, g, U[l])
                    elif name == "onorm":
                        apply(part, g, U[l], U[l], x_ready[l])
                        close(part)


                def do_s(g, name):
                    if name == "nstat":
                        dve.wait_ge(out_ready[1], g + 1)
                        stats("s", g, HS, 1.0 + EPS, EPS * EPS)
                    elif name in ("nroot", "froot"):
                        root("s", g, 1.0)
                    elif name == "norm":
                        if not first(g):
                            dve.wait_ge(*filled(g - 1, "mx"))
                        apply("s", g, HS, XS, xs_ready)
                    elif name in ("gx", "ot"):
                        low(g, name, ZF, ZP, zt_ready)
                    elif name == "qk":
                        for c, (n, tanh, dst) in enumerate((("q", EB, QT), ("k", PB, KT))):
                            dve.wait_ge(qe_ready, 2 * g + c + 1)
                            dve.scalar_tensor_tensor(flat(dst), flat(tanh), 1.0, ps(n)[:], ALU.add,
                                                     ALU.mult).then_inc(free[BANK[n]], 1)
                    elif name == "fv":
                        if not first(g):
                            dve.wait_ge(acc_ready, g)
                        for j in range(G):
                            n = f"fv{j}"
                            dve.wait_ge(ve_ready, G * g + j + 1)
                            i = dve.tensor_scalar(US[:, j], ps(n)[:, 0:D], 0.0, IWS, ALU.min, ALU.mult)
                            if j == G - 1:
                                i.then_inc(mn_ready, 1)
                            dve.scalar_tensor_tensor(VB[:, j], EB[:, j], 1.0, ps(n)[:, D:2 * D], ALU.add,
                                                     ALU.mult).then_inc(free[BANK[n]], 1)
                    elif name == "g":
                        dve.wait_ge(mn_ready, g + 1)
                        dve.wait_ge(fl_ready, g + 1)
                        dve.tensor_tensor(flat(US), flat(US), flat(PB), ALU.subtract).then_inc(g_ready, 1)
                    elif name == "decay":
                        dve.wait_ge(*filled(g, "D"))
                        dve.tensor_scalar(flat(EB), ps("D")[:], EXP_CLAMP * GATE_NORM, -EXP_CLAMP * GATE_NORM,
                                          ALU.min, ALU.max).then_inc(free[BANK["D"]], 1)
                    elif name == "slots":
                        dve.wait_ge(es_ready, g + 1)
                        link("s", g, dve.tensor_scalar(flat(XS), flat(XS), -1.0, 1.0, ALU.mult, ALU.add))
                        dve.wait_ge(ei_ready, g + 1)
                        dve.tensor_tensor(flat(XS), flat(XS), flat(PB), ALU.mult).then_inc(sp_ready, 1)
                    elif name in ("scores", "vscores"):
                        stem, dst, f = ("A", AT, (0.5 * IWS) ** 2) if name == "scores" else ("B", BT, 1.0)
                        for par in range(2):
                            n = f"{stem}{par}"
                            dve.wait_ge(*filled(g, n))
                            dve.scalar_tensor_tensor(dst[:, par], ps(n)[:].rearrange("p (c t) -> p c t", c=4), f,
                                                     upper[:, None, :].to_broadcast([P, 4, P]), ALU.mult,
                                                     ALU.mult).then_inc(free[BANK[n]], 1)
                    elif name == "gz":
                        dve.wait_ge(e_ready, g + 1)
                        dve.wait_ge(*filled(g, "gz"))
                        dve.tensor_tensor(flat(PB), ps("gz")[:], flat(EB), ALU.mult).then_inc(free[BANK["gz"]], 1)
                    elif name == "zmax":
                        z3 = flat(PB).rearrange("p (c m) -> p c m", c=G * HEADS)
                        dve.wait_ge(*taken(g, "gz"))
                        link("s", g, dve.tensor_reduce(zmax[:], z3, AX, ALU.max))
                        dve.tensor_tensor(z3, z3, zmax[:, :, None].to_broadcast([P, G * HEADS, DK]),
                                          ALU.subtract).then_inc(zs_ready, 1)
                    elif name == "pp":
                        dve.wait_ge(ze_ready, g + 1)
                        dve.tensor_tensor(flat(EB), flat(PB), flat(EB), ALU.mult).then_inc(pp_ready, 1)
                    elif name == "zsum":
                        z3 = flat(PB).rearrange("p (c m) -> p c m", c=G * HEADS)
                        link("s", g, dve.tensor_reduce(zsum[:], z3, AX, ALU.add))
                        link("s", g, dve.reciprocal(zsum[:], zsum[:]))
                        link("s", g, dve.tensor_scalar(zsum[:], zsum[:], 0.5 * IWS, None, ALU.mult))
                    elif name == "o":
                        dve.wait_ge(*filled(g, "o"))
                        dve.tensor_tensor(flat(US).rearrange("p (c v) -> p c v", c=G * HEADS),
                                          ps("o")[:].rearrange("p (c v) -> p c v", c=G * HEADS),
                                          zsum[:, :, None].to_broadcast([P, G * HEADS, DK]), ALU.mult).then_inc(free[BANK["o"]], 1)
                    elif name == "osw":
                        dve.wait_ge(oe_ready, g + 1)
                        dve.scalar_tensor_tensor(flat(US), flat(EB), 1.0, flat(US), ALU.add, ALU.mult).then_inc(os_ready, 1)
                    elif name == "root":
                        dve.wait_ge(sq_ready, g + 1)
                        link("s", g, dve.tensor_scalar(NORM["s"][2][:], ssq[:], -1.0 / D, -EPS, ALU.mult, ALU.add))
                        guess("s", 0.5 * IWS)
                        root("s", g, 0.5 * IWS)
                    elif name == "res":
                        need("s", g)
                        dve.wait_ge(*filled(g, "w"))
                        for j in range(G):
                            i = dve.scalar_tensor_tensor(HO[:, j], ps("w")[:, j * D:(j + 1) * D], NORM["s"][3][:, j:j + 1],
                                                         HS[:, j], ALU.mult, ALU.add)
                        i.then_inc(free[BANK["w"]], 1)
                    elif name == "fstat":
                        dve.wait_ge(*taken(g, "w"))
                        stats("s", g, HO)
                    elif name == "fnorm":
                        apply("s", g, HO, XS, xs_ready)
                        close("s")

                def do_m(g, name, e=None):
                    if name == "mx":
                        low(g, "mx", XF, XP, xm_ready)
                    elif name == "router":
                        dve.wait_ge(*filled(g, "rl"))
                        dve.tensor_copy(lg[:], ps("rl")[:, 0:G * NE].rearrange("p (j e) -> p j e", j=G)).then_inc(free[BANK["rl"]], 1)
                        dve.wait_ge(*taken(g, "rl"))
                        dve.sem_inc(idle, 1)
                        for j in range(G):
                            i = dve.max(top[:, j], lg[:, j])
                        link("m", g, i)
                        dve.tensor_tensor(ex[:], lg[:], top[:, :, 0:1].to_broadcast([P, G, NE]), ALU.subtract).then_inc(rx_ready, 1)
                        dve.tensor_tensor(keep[:], lg[:], top[:, :, 1:2].to_broadcast([P, G, NE]), ALU.is_ge)
                    elif name == "gates":
                        dve.wait_ge(re_ready, g + 1)
                        link("m", g, dve.tensor_reduce(esum[:], ex[:], AX, ALU.add))
                        link("m", g, dve.reciprocal(esum[:], esum[:]))
                        link("m", g, dve.tensor_tensor(comb[:], ex[:], keep[:], ALU.mult))
                        link("m", g, dve.scalar_tensor_tensor(comb[:], comb[:], IWS, esum[:, :, None].to_broadcast([P, G, NE]),
                                                              ALU.mult, ALU.mult))
                        close("m")
                    elif name == "glu":
                        dve.wait_ge(me_ready, NX * g + e + 1)
                        if e >= 2:
                            dve.wait_ge(mlo_ready, NX * g + e - 1)
                        dve.scalar_tensor_tensor(MA[:, e % 2], ME[:, e % 2], 1.0, ps(f"g{e}")[:], ALU.add,
                                                 ALU.mult).then_inc(free[BANK[f"g{e}"]], 1)
                    elif name == "u":
                        dve.wait_ge(*filled(g, f"u{e}"))
                        dve.wait_ge(*taken(g, f"g{e}"))
                        dve.scalar_tensor_tensor(MA[:, e % 2], ps(f"u{e}")[:], 0.5 * IWS * IWS, MA[:, e % 2], ALU.mult,
                                                 ALU.mult).then_inc(free[BANK[f"u{e}"]], 1)
                    elif name == "down":
                        if e == 0:
                            dve.wait_ge(acc_ready, g + 1)
                        else:
                            dve.wait_ge(*taken(g, f"e{e - 1}"))
                        n = f"e{e}"
                        dve.wait_ge(*filled(g, n))
                        if e < NE:
                            for j in range(G):
                                i = dve.scalar_tensor_tensor(ACC[:, j], ps(n)[:, j * D:(j + 1) * D], comb[:, j, e:e + 1],
                                                             ACC[:, j], ALU.mult, ALU.add)
                        else:
                            i = dve.scalar_tensor_tensor(flat(ACC), ps(n)[:], IWS, flat(ACC), ALU.mult, ALU.add)
                        i.then_inc(free[BANK[n]], 1)
                        if e == NX - 1:
                            dve.wait_ge(*taken(g, n))
                            dve.sem_inc(acc_done, 1)

                dve.tensor_copy(cur[:], idx[:, 0:G]).then_inc(cur_ready, 1)
                def do_w(g, name, n):
                    n += NX * g
                    dve.wait_ge(stage_high, n + 1)
                    dve.scalar_tensor_tensor(flat(WX[g][:, 1, n % NX]), STAGE[n % NSTAGE], WS, flat(WX[g][:, 0, n % NX]),
                                             ALU.mult, ALU.subtract).then_inc(stage_low, 1)

                run(dve, "D", do_t, do_s, do_m, do_w)


_INS = ['x', 'L0_tok_emb', 'L0_tok_pos', 'L0_tok_wq', 'L0_tok_wk', 'L0_tok_wv', 'L0_tok_wo', 'L0_tok_wup', 'L0_tok_bup',
        'L0_tok_wdown', 'L0_tok_bdown', 'L0_tok_ga', 'L0_tok_ba', 'L0_tok_gm', 'L0_tok_bm', 'L0_attn_norm_weight',
        'L0_attn_w_q', 'L0_attn_w_k', 'L0_attn_w_v', 'L0_attn_w_f', 'L0_attn_gnorm_weight', 'L0_attn_w_o',
        'L0_ffn_router_w', 'L0_ffn_gate_w', 'L0_ffn_up_w', 'L0_ffn_down_w', 'L0_ffn_shared_gate_w',
        'L0_ffn_shared_up_w', 'L0_ffn_shared_down_w']


def kernel(**inputs):
    import numpy as _np
    import concourse.bacc as _bacc
    from concourse import mybir as _mybir
    from concourse.bass_utils import run_bass_kernel_spmd as _run

    nc = _bacc.Bacc("TRN2", target_bir_lowering=False, num_devices=1)
    arrays, args = {}, []
    for name in _INS:
        a = _np.ascontiguousarray(inputs[name])
        arrays[f"in_{name}"] = a
        args.append(nc.dram_tensor(f"in_{name}", a.shape, _mybir.dt.from_np(a.dtype), kind="ExternalInput").ap())
    seqs, steps = inputs["x"].shape
    width = inputs["L0_tok_emb"].shape[1]
    args.append(nc.dram_tensor("out_0", (seqs, steps, width), _mybir.dt.float32, kind="ExternalOutput").ap())
    build(nc, *args)
    r = _run(nc, [arrays], core_ids=[0])
    return r.results[0]["out_0"]
```
